# Optimizing a Trainium2 kernel written in Bass

```python
import numpy as np
import jax
import jax.numpy as jnp

def _softmax(x, axis=-1):
    return jax.nn.softmax(x, axis=axis)
def _gelu(x):
    return jax.nn.gelu(x, approximate=True)
def _silu(x):
    return jax.nn.silu(x)
def _sigmoid(x):
    return jax.nn.sigmoid(x)
def _layernorm(x, axis=-1, eps=1e-5):
    m = jnp.mean(x, axis=axis, keepdims=True)
    v = jnp.var(x, axis=axis, keepdims=True)
    return (x - m) / jnp.sqrt(v + eps)
def _scatter_add(tgt, idx, src, axis=0):
    return tgt.at[idx].add(src)
def _segment_sum(src, seg, n):
    return jax.ops.segment_sum(src, seg, n)

kernel_name = 'mk_metaformer_d2_conv_nhwc128_28faa5'

def setup_inputs(seed: int = 0):
    np.random.seed(seed)
    _w = jnp.asarray
    def _rec_inputs():
        import jax
        import jax.numpy as jnp
        _gk = jax.random.key(seed)
        x = -0.000929 + 1 * jax.random.normal(jax.random.fold_in(_gk, 1), (2, 32, 128, 128), jnp.float32)
        return x
    x = _rec_inputs()
    def _L0_conv_setup():
        import jax, jax.numpy as jnp
        import numpy as np
        EPS = 1e-05
        N_HEADS = 32
        TEMPERATURE = 1.0

        def _inorm(x, g, b):
            m = jnp.mean(x, axis=(-2, -1), keepdims=True)
            v = jnp.var(x, axis=(-2, -1), keepdims=True)
            return (x - m) * jax.lax.rsqrt(v + EPS) * g + b

        def _resample(x, out_hw):
            H, W = x.shape[-2:]
            Ho, Wo = out_hw
            if (H, W) == (Ho, Wo):
                return x
            xf = jnp.fft.rfft2(x, norm='forward')
            kh = min(H, Ho) // 2
            kw = min(W // 2 + 1, Wo // 2 + 1)
            of = jnp.zeros(x.shape[:-2] + (Ho, Wo // 2 + 1), dtype=xf.dtype)
            of = of.at[..., :kh, :kw].set(xf[..., :kh, :kw])
            of = of.at[..., -kh:, :kw].set(xf[..., -kh:, :kw])
            return jnp.fft.irfft2(of, s=(Ho, Wo), norm='forward')

        def _spec_conv(x, w, out_hw):
            m1, m2 = (w.shape[3], w.shape[4])
            Ho, Wo = out_hw
            wc = w[..., 0] + 1j * w[..., 1]
            xf = jnp.fft.rfft2(x, norm='forward')
            top = jnp.einsum('bimn,iomn->bomn', xf[:, :, :m1, :m2], wc[0])
            bot = jnp.einsum('bimn,iomn->bomn', xf[:, :, -m1:, :m2], wc[1])
            of = jnp.zeros((x.shape[0], w.shape[2], Ho, Wo // 2 + 1), dtype=xf.dtype)
            of = of.at[:, :, :m1, :m2].set(top)
            of = of.at[:, :, -m1:, :m2].set(bot)
            return jnp.fft.irfft2(of, s=(Ho, Wo), norm='forward')

        def _fno_layer(x, w, ws, bs, out_hw, norm_gb=None, act=False):
            skip = jnp.einsum('bchw,oc->bohw', x, ws) + bs[None, :, None, None]
            skip = _resample(skip, out_hw)
            fno = _spec_conv(x, w, out_hw)
            if norm_gb is not None:
                fno = _inorm(fno, norm_gb[0], norm_gb[1])
            y = fno + skip
            if act:
                y = jax.nn.gelu(y, approximate=False)
            return y

        def _forward(x, wK, wKs, bKs, wQ, wQs, bQs, wV, wVs, bVs, wP, wPs, bPs, wM0, wM0s, bM0s, wM1, wM1s, bM1s, norm_g, norm_b):
            B, T, H, W = x.shape
            xa = x.reshape(B * T, 1, H, W)
            xa_n = _inorm(xa, norm_g[0], norm_b[0])
            k = _fno_layer(xa_n, wK, wKs, bKs, (H // 2, W // 2))
            q = _fno_layer(xa_n, wQ, wQs, bQs, (H // 2, W // 2))
            v = _fno_layer(xa_n, wV, wVs, bVs, (H, W))

            def to_seq(z):
                h, w = z.shape[-2:]
                z = z.reshape(B, T, N_HEADS, 1, h, w).transpose(0, 2, 1, 3, 4, 5)
                return z.reshape(B, N_HEADS, T, h * w)
            qs, ks, vs = (to_seq(q), to_seq(k), to_seq(v))
            scores = jnp.einsum('bhtd,bhsd->bhts', qs, ks) / (np.sqrt(ks.shape[-1]).astype(np.float32) * TEMPERATURE)
            attn_w = jax.nn.softmax(scores, axis=-1)
            out = jnp.einsum('bhts,bhsd->bhtd', attn_w, vs)
            out = out.reshape(B, N_HEADS, T, 1, H, W).transpose(0, 2, 1, 3, 4, 5)
            out = out.reshape(B * T, N_HEADS, H, W)
            projd = _fno_layer(out, wP, wPs, bPs, (H, W))
            attention = _inorm(projd + xa, norm_g[1], norm_b[1])
            an = _inorm(attention, norm_g[2], norm_b[2])
            m = _fno_layer(an, wM0, wM0s, bM0s, (H, W), (norm_g[3], norm_b[3]), act=True)
            m = _fno_layer(m, wM1, wM1s, bM1s, (H, W), (norm_g[4], norm_b[4]), act=False)
            output = _inorm(m, norm_g[5], norm_b[5]) + attention
            return output.reshape(B, T, H, W)
        key = jax.random.key(seed)
        ks = jax.random.split(key, 16)
        B, T, H, W, heads = (2, 32, 128, 128, 32)

        def rn(k, shape, s=1.0):
            return jax.random.normal(k, shape, jnp.float32) * s
        inp = {'x': rn(ks[0], (B, T, H, W))}
        for i, nm in enumerate(['K', 'Q', 'V']):
            inp['w' + nm] = rn(ks[1 + 3 * i], (2, 1, heads, 16, 16, 2), 1.0 / heads)
            inp['w' + nm + 's'] = rn(ks[2 + 3 * i], (heads, 1), 1.0)
            inp['b' + nm + 's'] = jnp.zeros((heads,), jnp.float32)
        inp['wP'] = rn(ks[10], (2, heads, 1, 32, 32, 2), 1.0 / heads)
        inp['wPs'] = rn(ks[11], (1, heads), 1.0 / heads)
        inp['bPs'] = jnp.zeros((1,), jnp.float32)
        inp['wM0'] = rn(ks[12], (2, 1, 1, 32, 32, 2), 1.0)
        inp['wM0s'] = rn(ks[13], (1, 1), 1.0)
        inp['bM0s'] = jnp.zeros((1,), jnp.float32)
        inp['wM1'] = rn(ks[14], (2, 1, 1, 32, 32, 2), 1.0)
        inp['wM1s'] = rn(ks[15], (1, 1), 1.0)
        inp['bM1s'] = jnp.zeros((1,), jnp.float32)
        inp['norm_g'] = jnp.ones((6,), jnp.float32)
        inp['norm_b'] = jnp.zeros((6,), jnp.float32)
        return inp
    _L0_conv_all = _L0_conv_setup()
    _L0_conv_in = {k: v for k, v in _L0_conv_all.items() if k in ('wK', 'wKs', 'bKs', 'wQ', 'wQs', 'bQs', 'wV', 'wVs', 'bVs', 'wP', 'wPs', 'bPs', 'wM0', 'wM0s', 'bM0s', 'wM1', 'wM1s', 'bM1s', 'norm_g', 'norm_b', )}
    del _L0_conv_all

    def _L0_ffn_setup():
        import jax, jax.numpy as jnp
        import numpy as np
        PADDED_SL = 8192
        TEMPERATURE = 1.0
        SIGMA_POW = 0.25

        def _stu_conv(phi, u, n):
            b, sl, d = u.shape
            sgn = jnp.where(jnp.arange(sl) % 2 == 0, 1.0, -1.0).astype(u.dtype)
            sgn3 = sgn[None, :, None]
            Vf = jnp.fft.rfft(phi, n=n, axis=0)
            Uf_p = jnp.fft.rfft(u, n=n, axis=1)
            Uf_m = jnp.fft.rfft(u * sgn3, n=n, axis=1)
            U_plus = jnp.fft.irfft(Vf[None, :, :, None] * Uf_p[:, :, None, :], n=n, axis=1)[:, :sl]
            U_minus = jnp.fft.irfft(Vf[None, :, :, None] * Uf_m[:, :, None, :], n=n, axis=1)[:, :sl]
            U_minus = U_minus * sgn[None, :, None, None]
            return (U_plus, U_minus)

        def _compute_spectral(u, sigma, phi, Mpp, Mpm):
            U_plus, U_minus = _stu_conv(phi, u, PADDED_SL)
            s = sigma ** SIGMA_POW
            out = jnp.einsum('btkd,k,kde->bte', U_plus, s, Mpp)
            out = out + jnp.einsum('btkd,k,kde->bte', U_minus, s, Mpm)
            return out

        def _compute_ar_u(Mu, u):
            sl = u.shape[1]
            out = jnp.zeros(u.shape[:2] + (Mu.shape[-1],), dtype=u.dtype)
            for i in range(Mu.shape[0]):
                ui = jnp.pad(u, ((0, 0), (i, 0), (0, 0)))[:, :sl]
                out = out + jnp.einsum('btd,de->bte', ui, Mu[i])
            return out

        def _stu(u, sigma, phi, Mu, Mpp, Mpm):
            return _compute_spectral(u, sigma, phi, Mpp, Mpm) + _compute_ar_u(Mu, u)
        key = jax.random.key(seed)
        ks = jax.random.split(key, 8)
        b, sl, d, K, k_u = (2, 4096, 128, 16, 3)
        x = jax.random.normal(ks[0], (b, sl, d), dtype=jnp.float32)
        sigma = jax.random.uniform(ks[1], (K,), dtype=jnp.float32, minval=0.001, maxval=1.0)
        phi = jax.random.normal(ks[2], (sl, K), dtype=jnp.float32) / np.sqrt(sl)
        M_u = jax.random.normal(ks[3], (4, k_u, d, d), dtype=jnp.float32) * 0.02
        M_phi_plus = jax.random.normal(ks[4], (4, K, d, d), dtype=jnp.float32) * 0.02
        M_phi_minus = jax.random.normal(ks[5], (4, K, d, d), dtype=jnp.float32) * 0.02
        log_weights = jnp.ones((4,), dtype=jnp.float32)
        u01 = jax.random.uniform(ks[6], (4,), dtype=jnp.float32, minval=1e-06, maxval=1.0 - 1e-06)
        gumbel = -jnp.log(-jnp.log(u01))
        return {'x': x, 'sigma': sigma, 'phi': phi, 'M_u': M_u, 'M_phi_plus': M_phi_plus, 'M_phi_minus': M_phi_minus, 'log_weights': log_weights, 'gumbel': gumbel}
    _L0_ffn_all = _L0_ffn_setup()
    _L0_ffn_in = {k: v for k, v in _L0_ffn_all.items() if k in ('sigma', 'phi', 'M_u', 'M_phi_plus', 'M_phi_minus', 'log_weights', 'gumbel', )}
    del _L0_ffn_all

    def _L1_conv_setup():
        import jax, jax.numpy as jnp
        import numpy as np
        IN_SIZE = 128
        OUT_SIZE = 128
        FILTER_SIZE = 6
        UP_FACTOR = 2
        DN_FACTOR = 2
        SLOPE = 0.2
        GAIN = float(np.sqrt(2.0))

        def _firwin_kaiser(numtaps, cutoff, width, fs):
            nyq = 0.5 * fs
            atten = 2.285 * (numtaps - 1) * np.pi * (width / nyq) + 7.95
            if atten > 50:
                beta = 0.1102 * (atten - 8.7)
            elif atten > 21:
                beta = 0.5842 * (atten - 21) ** 0.4 + 0.07886 * (atten - 21)
            else:
                beta = 0.0
            c = cutoff / nyq
            alpha = 0.5 * (numtaps - 1)
            m = np.arange(numtaps) - alpha
            h = c * np.sinc(c * m)
            h *= np.kaiser(numtaps, beta)
            h /= h.sum()
            return h.astype(np.float32)

        def _make_filter(size, factor):
            taps = FILTER_SIZE * factor
            f1d = _firwin_kaiser(taps, size / 2.0001, size, size)
            f2d = np.outer(f1d, f1d)[None, None]
            return jnp.asarray(f2d, dtype=jnp.float32)

        def _conv_same(x, f):
            k = f.shape[-1]
            pl = (k - 1) // 2
            pr = k - 1 - pl
            return jax.lax.conv_general_dilated(x, f, (1, 1), [(pl, pr), (pl, pr)])
        key = jax.random.key(seed)
        x = jax.random.normal(key, (16, 32, IN_SIZE, IN_SIZE), dtype=jnp.float32)
        bias = jnp.zeros((1, 32, 1, 1), dtype=jnp.float32)
        up_filter = _make_filter(IN_SIZE, UP_FACTOR)
        dn_filter = _make_filter(OUT_SIZE, DN_FACTOR)
        return {'x': x, 'bias': bias, 'up_filter': up_filter, 'dn_filter': dn_filter}
    _L1_conv_all = _L1_conv_setup()
    _L1_conv_in = {k: v for k, v in _L1_conv_all.items() if k in ('bias', 'up_filter', 'dn_filter', )}
    del _L1_conv_all

    def _L1_ffn_setup():
        import jax, jax.numpy as jnp
        import numpy as np
        B, N, D, C, E, K = (8, 8192, 128, 128, 8, 2)
        key = jax.random.key(seed)
        k0, k1, k2 = jax.random.split(key, 3)
        x = jax.random.normal(k0, (B, N, D), dtype=jnp.float32)
        router_w = jax.random.normal(k1, (D, E), dtype=jnp.float32) * 0.05
        router_b = jnp.zeros((E,), dtype=jnp.float32)
        expert_w = jax.random.normal(k2, (E, D, C), dtype=jnp.float32) * (1.0 / np.sqrt(D))
        expert_b = jnp.zeros((E, C), dtype=jnp.float32)
        return {'x': x, 'router_w': router_w, 'router_b': router_b, 'expert_w': expert_w, 'expert_b': expert_b}
    _L1_ffn_all = _L1_ffn_setup()
    _L1_ffn_in = {k: v for k, v in _L1_ffn_all.items() if k in ('router_w', 'router_b', 'expert_w', 'expert_b', )}
    del _L1_ffn_all

    return {
        "x": x,
        "L0_conv_wK": _L0_conv_in["wK"],
        "L0_conv_wKs": _L0_conv_in["wKs"],
        "L0_conv_bKs": _L0_conv_in["bKs"],
        "L0_conv_wQ": _L0_conv_in["wQ"],
        "L0_conv_wQs": _L0_conv_in["wQs"],
        "L0_conv_bQs": _L0_conv_in["bQs"],
        "L0_conv_wV": _L0_conv_in["wV"],
        "L0_conv_wVs": _L0_conv_in["wVs"],
        "L0_conv_bVs": _L0_conv_in["bVs"],
        "L0_conv_wP": _L0_conv_in["wP"],
        "L0_conv_wPs": _L0_conv_in["wPs"],
        "L0_conv_bPs": _L0_conv_in["bPs"],
        "L0_conv_wM0": _L0_conv_in["wM0"],
        "L0_conv_wM0s": _L0_conv_in["wM0s"],
        "L0_conv_bM0s": _L0_conv_in["bM0s"],
        "L0_conv_wM1": _L0_conv_in["wM1"],
        "L0_conv_wM1s": _L0_conv_in["wM1s"],
        "L0_conv_bM1s": _L0_conv_in["bM1s"],
        "L0_conv_norm_g": _L0_conv_in["norm_g"],
        "L0_conv_norm_b": _L0_conv_in["norm_b"],
        "L0_ffn_sigma": _L0_ffn_in["sigma"],
        "L0_ffn_phi": _L0_ffn_in["phi"],
        "L0_ffn_M_u": _L0_ffn_in["M_u"],
        "L0_ffn_M_phi_plus": _L0_ffn_in["M_phi_plus"],
        "L0_ffn_M_phi_minus": _L0_ffn_in["M_phi_minus"],
        "L0_ffn_log_weights": _L0_ffn_in["log_weights"],
        "L0_ffn_gumbel": _L0_ffn_in["gumbel"],
        "L1_conv_bias": _L1_conv_in["bias"],
        "L1_conv_up_filter": _L1_conv_in["up_filter"],
        "L1_conv_dn_filter": _L1_conv_in["dn_filter"],
        "L1_ffn_router_w": _L1_ffn_in["router_w"],
        "L1_ffn_router_b": _L1_ffn_in["router_b"],
        "L1_ffn_expert_w": _L1_ffn_in["expert_w"],
        "L1_ffn_expert_b": _L1_ffn_in["expert_b"],
    }

def reference(x, L0_conv_wK, L0_conv_wKs, L0_conv_bKs, L0_conv_wQ, L0_conv_wQs, L0_conv_bQs, L0_conv_wV, L0_conv_wVs, L0_conv_bVs, L0_conv_wP, L0_conv_wPs, L0_conv_bPs, L0_conv_wM0, L0_conv_wM0s, L0_conv_bM0s, L0_conv_wM1, L0_conv_wM1s, L0_conv_bM1s, L0_conv_norm_g, L0_conv_norm_b, L0_ffn_sigma, L0_ffn_phi, L0_ffn_M_u, L0_ffn_M_phi_plus, L0_ffn_M_phi_minus, L0_ffn_log_weights, L0_ffn_gumbel, L1_conv_bias, L1_conv_up_filter, L1_conv_dn_filter, L1_ffn_router_w, L1_ffn_router_b, L1_ffn_expert_w, L1_ffn_expert_b):
    import jax
    import jax.numpy as jnp
    def _L0_conv_ref(x, wK, wKs, bKs, wQ, wQs, bQs, wV, wVs, bVs, wP, wPs, bPs, wM0, wM0s, bM0s, wM1, wM1s, bM1s, norm_g, norm_b):
        import jax, jax.numpy as jnp
        import numpy as np
        EPS = 1e-05
        N_HEADS = 32
        TEMPERATURE = 1.0

        def _inorm(x, g, b):
            m = jnp.mean(x, axis=(-2, -1), keepdims=True)
            v = jnp.var(x, axis=(-2, -1), keepdims=True)
            return (x - m) * jax.lax.rsqrt(v + EPS) * g + b

        def _resample(x, out_hw):
            H, W = x.shape[-2:]
            Ho, Wo = out_hw
            if (H, W) == (Ho, Wo):
                return x
            xf = jnp.fft.rfft2(x, norm='forward')
            kh = min(H, Ho) // 2
            kw = min(W // 2 + 1, Wo // 2 + 1)
            of = jnp.zeros(x.shape[:-2] + (Ho, Wo // 2 + 1), dtype=xf.dtype)
            of = of.at[..., :kh, :kw].set(xf[..., :kh, :kw])
            of = of.at[..., -kh:, :kw].set(xf[..., -kh:, :kw])
            return jnp.fft.irfft2(of, s=(Ho, Wo), norm='forward')

        def _spec_conv(x, w, out_hw):
            m1, m2 = (w.shape[3], w.shape[4])
            Ho, Wo = out_hw
            wc = w[..., 0] + 1j * w[..., 1]
            xf = jnp.fft.rfft2(x, norm='forward')
            top = jnp.einsum('bimn,iomn->bomn', xf[:, :, :m1, :m2], wc[0])
            bot = jnp.einsum('bimn,iomn->bomn', xf[:, :, -m1:, :m2], wc[1])
            of = jnp.zeros((x.shape[0], w.shape[2], Ho, Wo // 2 + 1), dtype=xf.dtype)
            of = of.at[:, :, :m1, :m2].set(top)
            of = of.at[:, :, -m1:, :m2].set(bot)
            return jnp.fft.irfft2(of, s=(Ho, Wo), norm='forward')

        def _fno_layer(x, w, ws, bs, out_hw, norm_gb=None, act=False):
            skip = jnp.einsum('bchw,oc->bohw', x, ws) + bs[None, :, None, None]
            skip = _resample(skip, out_hw)
            fno = _spec_conv(x, w, out_hw)
            if norm_gb is not None:
                fno = _inorm(fno, norm_gb[0], norm_gb[1])
            y = fno + skip
            if act:
                y = jax.nn.gelu(y, approximate=False)
            return y

        def _forward(x, wK, wKs, bKs, wQ, wQs, bQs, wV, wVs, bVs, wP, wPs, bPs, wM0, wM0s, bM0s, wM1, wM1s, bM1s, norm_g, norm_b):
            B, T, H, W = x.shape
            xa = x.reshape(B * T, 1, H, W)
            xa_n = _inorm(xa, norm_g[0], norm_b[0])
            k = _fno_layer(xa_n, wK, wKs, bKs, (H // 2, W // 2))
            q = _fno_layer(xa_n, wQ, wQs, bQs, (H // 2, W // 2))
            v = _fno_layer(xa_n, wV, wVs, bVs, (H, W))

            def to_seq(z):
                h, w = z.shape[-2:]
                z = z.reshape(B, T, N_HEADS, 1, h, w).transpose(0, 2, 1, 3, 4, 5)
                return z.reshape(B, N_HEADS, T, h * w)
            qs, ks, vs = (to_seq(q), to_seq(k), to_seq(v))
            scores = jnp.einsum('bhtd,bhsd->bhts', qs, ks) / (np.sqrt(ks.shape[-1]).astype(np.float32) * TEMPERATURE)
            attn_w = jax.nn.softmax(scores, axis=-1)
            out = jnp.einsum('bhts,bhsd->bhtd', attn_w, vs)
            out = out.reshape(B, N_HEADS, T, 1, H, W).transpose(0, 2, 1, 3, 4, 5)
            out = out.reshape(B * T, N_HEADS, H, W)
            projd = _fno_layer(out, wP, wPs, bPs, (H, W))
            attention = _inorm(projd + xa, norm_g[1], norm_b[1])
            an = _inorm(attention, norm_g[2], norm_b[2])
            m = _fno_layer(an, wM0, wM0s, bM0s, (H, W), (norm_g[3], norm_b[3]), act=True)
            m = _fno_layer(m, wM1, wM1s, bM1s, (H, W), (norm_g[4], norm_b[4]), act=False)
            output = _inorm(m, norm_g[5], norm_b[5]) + attention
            return output.reshape(B, T, H, W)
        return _forward(x, wK, wKs, bKs, wQ, wQs, bQs, wV, wVs, bVs, wP, wPs, bPs, wM0, wM0s, bM0s, wM1, wM1s, bM1s, norm_g, norm_b)

    def _L0_ffn_ref(x, sigma, phi, M_u, M_phi_plus, M_phi_minus, log_weights, gumbel):
        import jax, jax.numpy as jnp
        import numpy as np
        PADDED_SL = 8192
        TEMPERATURE = 1.0
        SIGMA_POW = 0.25

        def _stu_conv(phi, u, n):
            b, sl, d = u.shape
            sgn = jnp.where(jnp.arange(sl) % 2 == 0, 1.0, -1.0).astype(u.dtype)
            sgn3 = sgn[None, :, None]
            Vf = jnp.fft.rfft(phi, n=n, axis=0)
            Uf_p = jnp.fft.rfft(u, n=n, axis=1)
            Uf_m = jnp.fft.rfft(u * sgn3, n=n, axis=1)
            U_plus = jnp.fft.irfft(Vf[None, :, :, None] * Uf_p[:, :, None, :], n=n, axis=1)[:, :sl]
            U_minus = jnp.fft.irfft(Vf[None, :, :, None] * Uf_m[:, :, None, :], n=n, axis=1)[:, :sl]
            U_minus = U_minus * sgn[None, :, None, None]
            return (U_plus, U_minus)

        def _compute_spectral(u, sigma, phi, Mpp, Mpm):
            U_plus, U_minus = _stu_conv(phi, u, PADDED_SL)
            s = sigma ** SIGMA_POW
            out = jnp.einsum('btkd,k,kde->bte', U_plus, s, Mpp)
            out = out + jnp.einsum('btkd,k,kde->bte', U_minus, s, Mpm)
            return out

        def _compute_ar_u(Mu, u):
            sl = u.shape[1]
            out = jnp.zeros(u.shape[:2] + (Mu.shape[-1],), dtype=u.dtype)
            for i in range(Mu.shape[0]):
                ui = jnp.pad(u, ((0, 0), (i, 0), (0, 0)))[:, :sl]
                out = out + jnp.einsum('btd,de->bte', ui, Mu[i])
            return out

        def _stu(u, sigma, phi, Mu, Mpp, Mpm):
            return _compute_spectral(u, sigma, phi, Mpp, Mpm) + _compute_ar_u(Mu, u)
        T = x.shape[1]
        outs = []
        for i, frac in enumerate((1, 2, 4, 8)):
            xi = x[:, :T // frac]
            si = _stu(xi, sigma, phi, M_u[i], M_phi_plus[i], M_phi_minus[i])
            si = jnp.pad(si, ((0, 0), (0, T - si.shape[1]), (0, 0)))
            outs.append(si)
        y_soft = jax.nn.softmax((log_weights + gumbel) / TEMPERATURE)
        y_hard = jax.nn.one_hot(jnp.argmax(y_soft), 4, dtype=y_soft.dtype)
        weights = y_hard - jax.lax.stop_gradient(y_soft) + y_soft
        stacked = jnp.stack(outs, axis=-1)
        return jnp.sum(stacked * weights, axis=-1)

    def _L1_conv_ref(x, bias, up_filter, dn_filter):
        import jax, jax.numpy as jnp
        import numpy as np
        IN_SIZE = 128
        OUT_SIZE = 128
        FILTER_SIZE = 6
        UP_FACTOR = 2
        DN_FACTOR = 2
        SLOPE = 0.2
        GAIN = float(np.sqrt(2.0))

        def _firwin_kaiser(numtaps, cutoff, width, fs):
            nyq = 0.5 * fs
            atten = 2.285 * (numtaps - 1) * np.pi * (width / nyq) + 7.95
            if atten > 50:
                beta = 0.1102 * (atten - 8.7)
            elif atten > 21:
                beta = 0.5842 * (atten - 21) ** 0.4 + 0.07886 * (atten - 21)
            else:
                beta = 0.0
            c = cutoff / nyq
            alpha = 0.5 * (numtaps - 1)
            m = np.arange(numtaps) - alpha
            h = c * np.sinc(c * m)
            h *= np.kaiser(numtaps, beta)
            h /= h.sum()
            return h.astype(np.float32)

        def _make_filter(size, factor):
            taps = FILTER_SIZE * factor
            f1d = _firwin_kaiser(taps, size / 2.0001, size, size)
            f2d = np.outer(f1d, f1d)[None, None]
            return jnp.asarray(f2d, dtype=jnp.float32)

        def _conv_same(x, f):
            k = f.shape[-1]
            pl = (k - 1) // 2
            pr = k - 1 - pl
            return jax.lax.conv_general_dilated(x, f, (1, 1), [(pl, pr), (pl, pr)])
        B, C, H, W = x.shape
        x = x + bias
        x = x.reshape(B * C, 1, H, W)
        x = jnp.repeat(jnp.repeat(x, UP_FACTOR, axis=2), UP_FACTOR, axis=3)
        x = _conv_same(x, up_filter)
        x = jax.nn.leaky_relu(x, negative_slope=SLOPE) * GAIN
        x = _conv_same(x, dn_filter)
        x = x[:, :, ::DN_FACTOR, ::DN_FACTOR]
        return x.reshape(B, C, OUT_SIZE, OUT_SIZE)

    def _L1_ffn_ref(x, router_w, router_b, expert_w, expert_b):
        import jax, jax.numpy as jnp
        import numpy as np
        B, N, D, C, E, K = (8, 8192, 128, 128, 8, 2)
        router_probs = jax.nn.softmax(x @ router_w + router_b, axis=-1)
        top_p, top_i = jax.lax.top_k(router_probs, K)
        top_p = top_p / jnp.sum(top_p, axis=-1, keepdims=True)
        expert_out = jnp.einsum('bnd,edc->bnec', x, expert_w) + expert_b
        gathered = jnp.take_along_axis(expert_out, top_i[..., None], axis=2)
        return jnp.einsum('bnk,bnkc->bnc', top_p, gathered)

    def _gn(v, G=32, eps=1e-5):
        B_, H_, W_, C_ = v.shape
        g = v.reshape(B_, H_, W_, G, C_ // G)
        m = jnp.mean(g, axis=(1, 2, 4), keepdims=True)
        s = jnp.var(g, axis=(1, 2, 4), keepdims=True)
        return ((g - m) / jnp.sqrt(s + eps)).reshape(v.shape)

    def _ln_c(v, eps=1e-6):
        m = jnp.mean(v, axis=-1, keepdims=True)
        s = jnp.var(v, axis=-1, keepdims=True)
        return (v - m) / jnp.sqrt(s + eps)

    def _ln_t(v, eps=1e-5):
        m = jnp.mean(v, axis=-1, keepdims=True)
        s = jnp.var(v, axis=-1, keepdims=True)
        return (v - m) / jnp.sqrt(s + eps)

    def _to_tokens(v):
        B_, H_, W_, C_ = v.shape
        return v.reshape(B_, H_ * W_, C_)
    def _from_tokens(t, like):
        return t.reshape(like.shape)

    x = x + _L0_conv_ref(_ln_c(x), L0_conv_wK, L0_conv_wKs, L0_conv_bKs, L0_conv_wQ, L0_conv_wQs, L0_conv_bQs, L0_conv_wV, L0_conv_wVs, L0_conv_bVs, L0_conv_wP, L0_conv_wPs, L0_conv_bPs, L0_conv_wM0, L0_conv_wM0s, L0_conv_bM0s, L0_conv_wM1, L0_conv_wM1s, L0_conv_bM1s, L0_conv_norm_g, L0_conv_norm_b)
    t = _to_tokens(x)
    t = t + _L0_ffn_ref(_ln_t(t), L0_ffn_sigma, L0_ffn_phi, L0_ffn_M_u, L0_ffn_M_phi_plus, L0_ffn_M_phi_minus, L0_ffn_log_weights, L0_ffn_gumbel)
    x = _from_tokens(t, x)
    x = x + _L1_conv_ref(_ln_c(x), L1_conv_bias, L1_conv_up_filter, L1_conv_dn_filter)
    t = _to_tokens(x)
    t = t + _L1_ffn_ref(_ln_t(t), L1_ffn_router_w, L1_ffn_router_b, L1_ffn_expert_w, L1_ffn_expert_b)
    x = _from_tokens(t, x)
    return x


_drawn_inputs = setup_inputs


def setup_inputs(seed=0):
    import zlib

    import numpy as np

    out = dict(_drawn_inputs(seed))
    spreads = {'L0_conv_bKs': (0.0, 2.0),
     'L0_conv_bQs': (0.0, 2.0),
     'L0_conv_bVs': (0.0, 2.0),
     'L0_conv_norm_g': (1.0, 0.2),
     'L0_conv_norm_b': (0.0, 0.1),
     'L0_ffn_log_weights': (1.0, 0.2),
     'L1_conv_bias': (0.0, 0.267),
     'L1_ffn_router_b': (0.0, 0.1),
     'L1_ffn_expert_b': (0.0, 0.398)}
    factors = {'L0_conv_wK': 58.135, 'L0_conv_wQ': 60.375, 'L0_conv_wV': 8.0, 'L0_conv_wPs': 3.11}
    for name, (base, spread) in spreads.items():
        noise = np.random.default_rng([zlib.crc32(name.encode()), seed]).standard_normal(out[name].shape)
        drawn = base * np.exp(spread * noise) if base else spread * noise
        out[name] = jnp.asarray(drawn.astype(out[name].dtype))
    for name, factor in factors.items():
        out[name] = (out[name] * factor).astype(out[name].dtype)
    return out
```

```python
from contextlib import ExitStack

import concourse.bass as bass
import numpy as np
from concourse import mybir

F32 = mybir.dt.float32
ALU = mybir.AluOpType
ACT = mybir.ActivationFunctionType
AX = mybir.AxisListType

B, T, HW = 2, 32, 128
NI = B * T
GROUP = 8
NG = NI // GROUP
HEADS = 32
NM, NN = 64, 32
LM, LN = 32, 16
DS = 64
PIX = HW * HW
FT = 16
HB = 64
NQ = 32
TAPS = 12
EXP = 8


def tables():
    t = {}
    h = np.arange(HW)
    m = np.concatenate([np.arange(NM // 2), np.arange(-NM // 2, 0)])
    n = np.arange(NN)
    ang = 2 * np.pi * np.outer(h, m) / HW
    rows = [np.cos(ang), -np.sin(ang)]
    hd = np.arange(DS)
    rel = hd[None, :, None] / DS - h[:, None, None] / HW
    a1 = np.cos(2 * np.pi * rel * m).sum(-1) / HW
    a2 = np.sin(2 * np.pi * rel * m).sum(-1) / HW
    nn = np.arange(DS // 2 + 1)
    wt = np.where((nn == 0) | (nn == DS // 2), 1.0, 2.0)
    b1 = (wt * np.cos(2 * np.pi * rel * nn)).sum(-1) / HW
    b2 = (wt * np.sin(2 * np.pi * rel * nn)).sum(-1) / HW
    t["dft_rows"] = np.concatenate(rows + [a1, a2], 1)
    an = 2 * np.pi * np.outer(h, n) / HW
    c, s = np.cos(an) / PIX, np.sin(an) / PIX
    t["dft_cols"] = np.concatenate([c, -s, s, c, s, c, -c, s], 1)
    t["down_cols"] = np.concatenate([b1, -b2], 1)
    w2 = np.where(n == 0, 1.0, 2.0)[:, None]
    ca, sa = w2 * np.cos(an.T), w2 * np.sin(an.T)
    t["idft_cols"] = np.concatenate([ca, -sa], 0)
    t["idft_rows"] = np.concatenate([np.cos(ang.T), -np.sin(ang.T)], 0)
    ml = np.concatenate([np.arange(LM // 2), np.arange(-LM // 2, 0)])
    w = np.where(np.arange(LN)[:, None] == 0, 1.0, 2.0) * np.ones((1, LM))
    w[0, ml == -LM // 2] = 2.0
    w *= 64.0
    w = np.tile(w.reshape(LN * 4, LM // 4), (2, 1))
    t["parseval"] = np.repeat(w[:, :, None], HEADS, 2).reshape(128, 256)
    n0 = np.zeros((2, LN, 4, LM // 4, HEADS))
    n0[:, 0] = 1.0
    n0 = n0.reshape(128, 256)
    t["herm_low"] = np.concatenate([1 - 0.5 * n0, 0.5 * n0], 1)
    t["im_sign"] = np.concatenate([np.ones((64, 1)), -np.ones((64, 1))], 0)
    f0 = np.zeros((HEADS, NN, NM))
    f0[:, 0] = 1.0
    f0 = f0.reshape(128, 512)
    t["herm_full"] = np.concatenate([1 - 0.5 * f0, 0.5 * f0], 1)
    t["identity"] = np.eye(128)
    q, j = np.arange(NQ), np.arange(NQ + 1)
    aj = 2 * np.pi * np.outer(j, q) / (2 * NQ)
    re, im, re_b = np.cos(aj), -np.sin(aj), np.cos(aj)
    re_b[:, 0] = (-1.0) ** j
    t["filter_dft"] = np.concatenate([re, im, -im, re_b], 1)
    im_p = im.copy()
    im_p[:, 0] = (-1.0) ** j
    both = np.stack([re, im_p], 1).reshape(NQ + 1, 2 * NQ)
    t["block_dft"] = np.concatenate([np.kron(np.eye(B), both[:NQ]), np.kron(np.eye(B), both[1:])], 1)
    wt = np.where(q == 0, 1.0, 2.0)[:, None] / (2 * NQ)
    inv = np.concatenate([wt * re[:NQ].T, wt * im_p[:NQ].T], 0)
    t["block_idft"] = np.kron(np.eye(B), inv)
    t["masks"] = np.stack([(np.arange(NI) % T < T // f) for f in (1, 2, 4, 8)]).astype(float)
    i = np.arange(TAPS)
    sel = np.zeros((TAPS, 13))
    for q in range(2):
        sel[i, 7 * q + (q + i - 5) // 2 + (3 if q == 0 else 2)] = 1.0
    t["up_sel"] = sel
    pu, pd = np.zeros((TAPS, 2, 256)), np.zeros((TAPS, 2, 256))
    for p in range(2):
        pu[i, p, HW - 1 + (p + i - 5) // 2] = 1.0
        j = i[(i + 1) % 2 == p]
        pd[j, p, HW - 1 - (j - 5 - p) // 2] = 1.0
    t["up_pos"], t["dn_pos"] = pu.reshape(TAPS, 512), pd.reshape(TAPS, 512)
    t["order"] = EXP - np.arange(EXP)
    return {k: np.ascontiguousarray(v, np.float32) for k, v in t.items()}


class Chain:

    def __init__(self, eng, sem):
        self.eng, self.sem, self.n = eng, sem, 0

    def __call__(self, ins):
        self.n += 1
        ins.then_inc(self.sem, 1)
        self.eng.wait_ge(self.sem, self.n)


def sub(ap, offset, dims):
    return bass.AP(ap.tensor, offset, dims)


def row_stats(v, link, st, mean, var, tmp):
    link(v.tensor_tensor(tmp, st[:, :, 1], st[:, :, 4], ALU.subtract))
    link(v.tensor_tensor(mean, st[:, :, 1], st[:, :, 4], ALU.add))
    link(v.tensor_tensor(var, st[:, :, 2], st[:, :, 5], ALU.add))
    link(v.tensor_tensor(tmp, tmp, tmp, ALU.mult))
    link(v.tensor_scalar(var, var, 1.0 / HW, None, ALU.mult))
    link(v.scalar_tensor_tensor(out=var, in0=tmp, scalar=0.25, in1=var, op0=ALU.mult, op1=ALU.add))
    link(v.tensor_scalar(mean, mean, 0.5, None, ALU.mult))


def newton_rsqrt(v, link, var, root, out, tmp, root_ready, n):
    v.wait_ge(root_ready, n)
    link(v.reciprocal(out, root))
    link(v.tensor_tensor(tmp, out, out, ALU.mult))
    link(v.tensor_tensor(tmp, tmp, var, ALU.mult))
    link(v.tensor_scalar(tmp, tmp, -0.5, 1.5, ALU.mult, ALU.add))
    link(v.tensor_tensor(out, out, tmp, ALU.mult))


class Core:

    def __init__(self, nc, ctx, a):
        self.nc, self.ctx, self.a = nc, ctx, a
        self.x = self.sb("acts", [HW, NI, HW])
        self.ones = self.sb("ones", [128, 128])
        self.ident = self.sb("ident", [128, 128])
        self.norm_g = self.sb("norm_g", [128, 6])
        self.norm_b = self.sb("norm_b", [128, 6])

    def image_buffer(self, ctx):
        self.xa = self.sb("xa", [HW, NI, HW], ctx=ctx)

    def sb(self, name, shape, dt=F32, ctx=None):
        return (ctx or self.ctx).enter_context(self.nc.sbuf_tensor(name, shape, dt))

    def ps(self, name, shape, ctx):
        return ctx.enter_context(self.nc.psum_tensor(name, shape, F32))

    def sem(self, name):
        return self.ctx.enter_context(self.nc.semaphore(name))


def stage_spectrum(k, att):
    nc, a = k.nc, k.a
    with ExitStack() as ctx:
        sb = lambda name, shape: k.sb(name, shape, ctx=ctx)
        x, xa = k.x, k.xa
        st = sb("s1_st", [128, NI, 6])
        mean, var, rstd, root, tmp, scale = (sb(f"s1_{n}", [128, NI]) for n in ("mean", "var", "rstd", "root", "tmp", "scale"))
        rows = sb("s1_rows", [128, 256])
        cols = sb("s1_cols", [128, 128])
        down = sb("s1_down", [128, 128])
        xn = sb("s1_xn", [128, GROUP, HW])
        yt = sb("s1_yt", [128, GROUP, 256])
        xfs = sb("s1_xf", [64, NI, NM])
        xls = sb("s1_xl", [64, LM, NI])
        xds = sb("s1_xd", [64, NI, DS])
        ps_a = k.ps("s1_psa", [128, GROUP, 256], ctx)
        ps_x = k.ps("s1_psx", [64, 512], ctx)
        ps_d = k.ps("s1_psd", [64, 512], ctx)
        ps_s = k.ps("s1_pss", [128, 512], ctx)
        loaded = k.sem("s1_loaded")
        chain = k.sem("s1_chain")
        ones_set = k.sem("s1_ones_set")
        var_ready, root_ready = k.sem("s1_var_ready"), k.sem("s1_root_ready")
        rowvar_ready, imgvar_ready = k.sem("s1_rowvar_ready"), k.sem("s1_imgvar_ready")
        xn_ready, xn_stored = k.sem("s1_xn_ready"), k.sem("s1_xn_stored")
        rows_done, yt_ready = k.sem("s1_rows_done"), k.sem("s1_yt_ready")
        spec_done, down_done = k.sem("s1_spec_done"), k.sem("s1_down_done")
        spec_copied, down_copied = k.sem("s1_spec_copied"), k.sem("s1_down_copied")
        gram_done, stored = k.sem("s1_gram_done"), k.sem("s1_stored")

        block = ctx.enter_context(nc.Block())

        @block.sync
        def _(sp):
            for q in range(4):
                sp.dma_start(x[:, 16 * q:16 * q + 16, :],
                             a["x"][16 * q:16 * q + 16].rearrange("i h w -> h i w")).then_inc(loaded, 16)
            sp.dma_start(rows[:, :], a["dft_rows"]).then_inc(loaded, 16)
            sp.dma_start(cols[:, :], a["dft_cols"][:, 0:128]).then_inc(loaded, 16)
            sp.dma_start(down[:, :], a["down_cols"]).then_inc(loaded, 16)
            sp.dma_start(k.ident[:, :], a["identity"]).then_inc(loaded, 16)
            sp.dma_start(k.norm_g[:, :], sub(a["norm_g"], 0, [[0, 128], [1, 6]])).then_inc(loaded, 16)
            sp.dma_start(k.norm_b[:, :], sub(a["norm_b"], 0, [[0, 128], [1, 6]])).then_inc(loaded, 16)
            with sp.Fori(0, NG) as g:
                sp.wait_ge(xn_ready, g + 1)
                sp.dma_start(a["xn_d"][bass.ds(g * GROUP, GROUP)].rearrange("i h w -> h i w"),
                             xn[:, :, :]).then_inc(xn_stored, 16)
            sp.wait_ge(xn_stored, 16 * NG)
            sp.wait_ge(spec_copied, NG)
            sp.dma_start(sub(a["xf_d"], 0, [[NM, 64], [64 * NM, NI], [1, NM]]), xfs[:, :, :]).then_inc(stored, 16)
            for c in range(2):
                sp.dma_start(a["xl_d"][c * LN:(c + 1) * LN], xls[c * NN:c * NN + LN, :, :]).then_inc(stored, 16)
            sp.wait_ge(stored, 48)

        @block.vector
        def _(v):
            link = Chain(v, chain)
            v.memset(k.ones[:, :], 1.0 / HW).then_inc(ones_set, 1)
            v.wait_ge(loaded, 160)
            with v.Fori(0, NI) as i:
                v.bn_stats(st[:, bass.ds(i, 1), :], x[:, bass.ds(i, 1), :])
            link(v.memset(tmp[:, :], 0.0))
            row_stats(v, link, st, mean[:, :], var[:, :], tmp[:, :])
            link(v.tensor_scalar(rstd[:, :], var[:, :], 1e-6, None, ALU.add))
            v.tensor_copy(scale[:, :], rstd[:, :]).then_inc(var_ready, 1)
            v.wait_ge(var_ready, 1)
            newton_rsqrt(v, link, scale[:, :], root[:, :], rstd[:, :], tmp[:, :], root_ready, 1)
            link(v.tensor_tensor(tmp[:, :], rstd[:, :], rstd[:, :], ALU.mult))
            v.tensor_tensor(var[:, :], var[:, :], tmp[:, :], ALU.mult).then_inc(rowvar_ready, 1)
            with v.Fori(0, NI) as i:
                v.tensor_scalar(xa[:, bass.ds(i, 1), :], x[:, bass.ds(i, 1), :], mean[:, bass.ds(i, 1)],
                                rstd[:, bass.ds(i, 1)], ALU.subtract, ALU.mult)
            v.wait_ge(imgvar_ready, 1)
            link(v.tensor_scalar(tmp[:, :], ps_s[:, 0:NI], 1e-5, None, ALU.add))
            v.tensor_copy(var[:, :], tmp[:, :]).then_inc(var_ready, 1)
            v.wait_ge(var_ready, 2)
            newton_rsqrt(v, link, var[:, :], root[:, :], scale[:, :], tmp[:, :], root_ready, 2)
            link(v.tensor_scalar(scale[:, :], scale[:, :], k.norm_g[:, 0:1], None, ALU.mult))
            with v.Fori(0, NG) as g:
                v.wait_ge(rows_done, g)
                v.wait_ge(xn_stored, g * 16)
                for i in range(GROUP):
                    ins = v.tensor_scalar(xn[:, i, :], xa[:, bass.ds(g * GROUP + i, 1), :],
                                          scale[:, bass.ds(g * GROUP + i, 1)], k.norm_b[:, 0:1], ALU.mult, ALU.add)
                ins.then_inc(xn_ready, 1)
                v.wait_ge(spec_done, g + 1)
                src = ps_x[:, :].rearrange("p (i m) -> p i m", m=NM)
                v.tensor_copy(xfs[:, bass.ds(g * GROUP, GROUP), :], src)
                dst = xls[:, :, bass.ds(g * GROUP, GROUP)].rearrange("p m i -> p i m")
                v.tensor_copy(dst[:, :, 0:16], src[:, :, 0:16])
                v.tensor_copy(dst[:, :, 16:32], src[:, :, 48:64]).then_inc(spec_copied, 1)
            v.wait_ge(gram_done, 1)
            for b in range(B):
                ins = v.tensor_copy(att.gram[T * b:T * b + T, :], ps_s[T * b:T * b + T, T * b:T * b + T])
            ins.then_inc(chain, 1)

        @block.scalar
        def _(s):
            s.wait_ge(var_ready, 1)
            s.activation(root[:, :], scale[:, :], ACT.Sqrt).then_inc(root_ready, 1)
            s.wait_ge(var_ready, 2)
            s.activation(root[:, :], var[:, :], ACT.Sqrt).then_inc(root_ready, 1)
            with s.Fori(0, NG) as g:
                s.wait_ge(rows_done, g + 1)
                s.wait_ge(down_done, g)
                for q in range(4):
                    ins = s.activation(yt[:, 2 * q:2 * q + 2, :], ps_a[:, 2 * q:2 * q + 2, :], ACT.Copy)
                ins.then_inc(yt_ready, 1)
                s.wait_ge(down_done, g + 1)
                s.activation(xds[:, bass.ds(g * GROUP, GROUP), :],
                             ps_d[:, :].rearrange("p (i m) -> p i m", m=DS), ACT.Copy).then_inc(down_copied, 1)

        @block.tensor
        def _(pe):
            pe.wait_ge(ones_set, 1)
            pe.wait_ge(rowvar_ready, 1)
            pe.matmul(ps_s[:, 0:NI], k.ones[:, :], var[:, :], start=True, stop=True).then_inc(imgvar_ready, 1)
            with pe.Fori(0, NG) as g:
                pe.wait_ge(xn_ready, g + 1)
                pe.wait_ge(yt_ready, g)
                for i in range(GROUP):
                    mm = pe.matmul(ps_a[:, i, :], xn[:, i, :], rows[:, :], start=True, stop=True)
                mm.then_inc(rows_done, 1)
                pe.wait_ge(yt_ready, g + 1)
                pe.wait_ge(spec_copied, g)
                pe.matmul(ps_x[:, :], cols[:, 0:64], yt[:, :, 0:64], start=True, stop=False)
                pe.matmul(ps_x[:, :], cols[:, 64:128], yt[:, :, 64:128], start=False, stop=True).then_inc(spec_done, 1)
                pe.wait_ge(down_copied, g)
                pe.matmul(ps_d[:, :], down[:, 0:64], yt[:, :, 128:192], start=True, stop=False)
                pe.matmul(ps_d[:, :], down[:, 64:128], yt[:, :, 192:256], start=False, stop=True).then_inc(down_done, 1)
            pe.wait_ge(down_copied, NG)
            pe.wait_ge(var_ready, 2)
            for r in range(DS):
                mm = pe.matmul(ps_s[0:64, 0:NI], xds[:, :, r], xds[:, :, r], start=(r == 0), stop=(r == DS - 1))
            mm.then_inc(gram_done, 1)


class Attention:

    def __init__(self, k, ctx):
        self.gram = k.sb("gram", [64, T], ctx=ctx)
        self.mix_t = k.sb("mix_t", [128, 128], ctx=ctx)
        self.prob_t = k.sb("prob_t", [128, HEADS // 4, B, T], ctx=ctx)
        self.dc = k.sb("dc", [1, 1], ctx=ctx)


def stage_attention(k, att):
    nc, a = k.nc, k.a
    with ExitStack() as ctx:
        sb = lambda name, shape: k.sb(name, shape, ctx=ctx)
        xl = sb("s2_xl", [128, 8, NI])
        xt = sb("s2_xt", [128, 8, NI])
        xw = sb("s2_xw", [128, 8, NI])
        herm = sb("s2_herm", [128, 2, 256])
        pars = sb("s2_pars", [128, 256])
        sign = sb("s2_sign", [128, 1])
        wk, wq = sb("s2_wk", [128, 4, 256]), sb("s2_wq", [128, 4, 256])
        skip = sb("s2_skip", [128, 4, HEADS])
        vec = sb("s2_vec", [128, 2, HEADS])
        cr, ci, t1, t2 = (sb(f"s2_{n}", [128, 256]) for n in ("cr", "ci", "t1", "t2"))
        kp = sb("s2_kp", [128, 8, HEADS, NI])
        kq = sb("s2_kq", [128, 4, HEADS, NI])
        sc = sb("s2_sc", [64, HEADS, T])
        sx = sb("s2_sx", [64, HEADS, T])
        mx, sm, rs = (sb(f"s2_{n}", [64, HEADS]) for n in ("mx", "sm", "rs"))
        qk = sb("s2_qk", [128, HEADS])
        mix = sb("s2_mix", [64, T])
        mixt = sb("s2_mixt", [64, T])
        pt = sb("s2_pt", [64, HEADS, T])
        dcv = sb("s2_dcv", [1, 3, HEADS])
        bp = sb("s2_bp", [1, 1])
        dct = sb("s2_dct", [1, HEADS])
        ps = k.ps("s2_ps", [64, HEADS, T], ctx)
        loaded, chain, fixed = k.sem("s2_loaded"), k.sem("s2_chain"), k.sem("s2_fixed")
        k_ready, scores_done = k.sem("s2_k_ready"), k.sem("s2_scores_done")
        shifted, exped, turned, moved = k.sem("s2_shifted"), k.sem("s2_exped"), k.sem("s2_turned"), k.sem("s2_moved")

        block = ctx.enter_context(nc.Block())

        @block.sync
        def _(sp):
            n = LN * 4 * 512
            src = sub(a["xl_d"], 0, [[512, 128], [NI, 8], [1, NI]])
            sp.dma_start(xl[:, :, :], src).then_inc(loaded, 16)
            sp.dma_start(xt[:, :, :], src).then_inc(loaded, 16)
            sp.dma_start(xw[0:64, :, :], sub(a["xl_d"], n, [[512, 64], [NI, 8], [1, NI]])).then_inc(loaded, 16)
            sp.dma_start(xw[64:128, :, :], sub(a["xl_d"], 0, [[512, 64], [NI, 8], [1, NI]])).then_inc(loaded, 16)
            sp.dma_start(herm[:, :, :], a["herm_low"].rearrange("p (u f) -> p u f", u=2)).then_inc(loaded, 16)
            sp.dma_start(pars[:, :], a["parseval"]).then_inc(loaded, 16)
            sp.dma_start(sign[:, :], a["im_sign"]).then_inc(loaded, 16)
            sp.dma_start(wk[:, :, :], a["wK"]).then_inc(loaded, 16)
            sp.dma_start(wq[:, :, :], a["wQ"]).then_inc(loaded, 16)
            for j, name in enumerate(("wQs", "wKs", "bQs", "bKs")):
                sp.dma_start(skip[:, j, :], sub(a[name], 0, [[0, 128], [1, HEADS]])).then_inc(loaded, 16)
            for j, name in enumerate(("wVs", "wPs")):
                sp.dma_start(vec[:, j, :], sub(a[name], 0, [[0, 128], [1, HEADS]])).then_inc(loaded, 16)
            sp.dma_start(dcv[:, 0, :], sub(a["bVs"], 0, [[0, 1], [1, HEADS]])).then_inc(loaded, 16)
            sp.dma_start(dcv[:, 1, :], sub(a["wPs"], 0, [[0, 1], [1, HEADS]])).then_inc(loaded, 16)
            sp.dma_start(dcv[:, 2, :], sub(a["wP00"], 0, [[0, 1], [1, HEADS]])).then_inc(loaded, 16)
            sp.dma_start(bp[:, :], sub(a["bPs"], 0, [[0, 1], [1, 1]])).then_inc(loaded, 16)
            sp.wait_ge(turned, 1)
            for b in range(B):
                for o in range(4):
                    sp.dma_start(att.prob_t[32 * o:32 * o + 32, :, b, :],
                                 pt[32 * b:32 * b + 32, o::4, :]).then_inc(moved, 16)
            sp.wait_ge(moved, 128)

        @block.vector
        def _(v):
            link = Chain(v, chain)
            tt = lambda o, x, y, op: link(v.tensor_tensor(o, x, y, op))
            v.wait_ge(loaded, 19 * 16)

            def head(j):
                return skip[:, j:j + 1, :].broadcast_to([128, 8, HEADS])

            r3 = lambda t: t.rearrange("p (m o) -> p m o", o=HEADS)
            for w in (wk, wq):
                tt(w[:, 0, :], w[:, 0, :], herm[:, 0, :], ALU.mult)
                tt(w[:, 1, :], w[:, 1, :], herm[:, 0, :], ALU.mult)
                tt(w[:, 2, :], w[:, 2, :], herm[:, 1, :], ALU.mult)
                tt(w[:, 3, :], w[:, 3, :], herm[:, 1, :], ALU.mult)
                tt(w[:, 0, :], w[:, 0, :], w[:, 2, :], ALU.add)
                tt(w[:, 1, :], w[:, 1, :], w[:, 3, :], ALU.subtract)
            kr, ki, qr, qi = wk[:, 0, :], wk[:, 1, :], wq[:, 0, :], wq[:, 1, :]
            tt(r3(cr[:, :]), r3(kr), head(0), ALU.mult)
            tt(r3(t1[:, :]), r3(qr), head(1), ALU.mult)
            tt(cr[:, :], cr[:, :], t1[:, :], ALU.add)
            tt(t1[:, :], qr, kr, ALU.mult)
            tt(cr[:, :], cr[:, :], t1[:, :], ALU.add)
            tt(t1[:, :], qi, ki, ALU.mult)
            tt(cr[:, :], cr[:, :], t1[:, :], ALU.add)
            tt(cr[:, :], cr[:, :], pars[:, :], ALU.mult)
            tt(r3(ci[:, :]), r3(qi), head(1), ALU.mult)
            tt(r3(t1[:, :]), r3(ki), head(0), ALU.mult)
            tt(ci[:, :], ci[:, :], t1[:, :], ALU.subtract)
            tt(t1[:, :], qi, kr, ALU.mult)
            tt(ci[:, :], ci[:, :], t1[:, :], ALU.add)
            tt(t1[:, :], qr, ki, ALU.mult)
            tt(ci[:, :], ci[:, :], t1[:, :], ALU.subtract)
            tt(ci[:, :], ci[:, :], pars[:, :], ALU.mult)
            link(v.tensor_scalar(ci[:, :], ci[:, :], sign[:, 0:1], None, ALU.mult))
            for half in range(2):
                m0 = 4 * half
                bx = lambda t: t[:, m0:m0 + 4, :].unsqueeze(2).broadcast_to([128, 4, HEADS, NI])
                bc = lambda t: r3(t[:, :])[:, m0:m0 + 4, :].unsqueeze(3).broadcast_to([128, 4, HEADS, NI])
                for m in range(4):
                    v.tensor_tensor(kp[:, m0 + m, :, :], bx(xl)[:, m], bc(cr)[:, m], ALU.mult)
                    v.tensor_tensor(kq[:, m, :, :], bx(xw)[:, m], bc(ci)[:, m], ALU.mult).then_inc(chain, 1)
                    link.n += 1
                v.wait_ge(chain, link.n)
                tt(kp[:, m0:m0 + 4, :, :], kp[:, m0:m0 + 4, :, :], kq[:, :, :, :], ALU.add)
            z = slice(0, 1)
            col = lambda t, p: r3(t)[p:p + 1, 0, :]
            tt(t1[z, 0:HEADS], col(qr, 0), skip[z, 0, :], ALU.add)
            tt(t1[z, 0:HEADS], t1[z, 0:HEADS], skip[z, 3, :], ALU.mult)
            link(v.tensor_scalar(t1[z, 0:HEADS], t1[z, 0:HEADS], 64.0, None, ALU.mult))
            tt(kp[z, 0, :, :], kp[z, 0, :, :], t1[z, 0:HEADS].unsqueeze(2).broadcast_to([1, HEADS, NI]), ALU.add)
            y = slice(64, 65)
            tt(t1[y, 0:HEADS], col(kr, 64), skip[y, 1, :], ALU.add)
            tt(kp[y, 0, :, :], xw[y, 0, :].unsqueeze(1).broadcast_to([1, HEADS, NI]),
               t1[y, 0:HEADS].unsqueeze(2).broadcast_to([1, HEADS, NI]), ALU.mult)
            tt(kp[y, 0, :, :], kp[y, 0, :, :], skip[y, 3, :].unsqueeze(2).broadcast_to([1, HEADS, NI]), ALU.add)
            link(v.tensor_scalar(t1[y, 0:HEADS], skip[y, 2, :], 64.0, None, ALU.mult))
            tt(kp[y, 0, :, :], kp[y, 0, :, :], t1[y, 0:HEADS].unsqueeze(2).broadcast_to([1, HEADS, NI]), ALU.mult)
            v.memset(xt[y, 0, :], 1.0).then_inc(k_ready, 1)
            tt(qk[:, :], skip[:, 0, :], skip[:, 1, :], ALU.mult)
            link(v.tensor_scalar(qk[:, :], qk[:, :], 1.0 / 64, None, ALU.mult))
            tt(sx[:, :, :], att.gram[:, :].unsqueeze(1).broadcast_to([64, HEADS, T]),
               qk[0:64, :].unsqueeze(2).broadcast_to([64, HEADS, T]), ALU.mult)
            v.wait_ge(scores_done, 1)
            for o in range(0, HEADS, 16):
                tt(sc[:, o:o + 16, :], ps[:, o:o + 16, :], sx[:, o:o + 16, :], ALU.add)
            link(v.tensor_reduce(mx[:, :], sc[:, :, :], AX.X, ALU.max))
            v.tensor_tensor(sc[:, :, :], sc[:, :, :], mx[:, :].unsqueeze(2).broadcast_to([64, HEADS, T]),
                            ALU.subtract).then_inc(shifted, 1)
            v.wait_ge(exped, 1)
            link(v.tensor_reduce(sm[:, :], sx[:, :, :], AX.X, ALU.add))
            link(v.reciprocal(rs[:, :], sm[:, :]))
            tt(sx[:, :, :], sx[:, :, :], rs[:, :].unsqueeze(2).broadcast_to([64, HEADS, T]), ALU.mult)
            v.transpose(pt[:, :, :].rearrange("p o t -> p (o t)"),
                        sx[:, :, :].rearrange("p o t -> p (o t)")).then_inc(turned, 1)
            tt(qk[:, :], vec[:, 0, :], vec[:, 1, :], ALU.mult)
            tt(sc[:, :, :], sx[:, :, :], qk[0:64, :].unsqueeze(2).broadcast_to([64, HEADS, T]), ALU.mult)
            link(v.tensor_reduce(mix[:, :], sc[:, :, :].rearrange("p o s -> p s o"), AX.X, ALU.add))
            link(v.transpose(mixt[:, :], mix[:, :]))
            link(v.memset(att.mix_t[:, :], 0.0))
            for half in range(2):
                for b in range(B):
                    p = 64 * half + 32 * b
                    link(v.tensor_copy(att.mix_t[p:p + 32, p:p + 32], mixt[32 * b:32 * b + 32, :]))
            tt(dct[:, :], dcv[:, 1, :], dcv[:, 2, :], ALU.add)
            tt(dct[:, :], dct[:, :], dcv[:, 0, :], ALU.mult)
            link(v.tensor_reduce(att.dc[:, :], dct[:, :], AX.X, ALU.add))
            tt(att.dc[:, :], att.dc[:, :], bp[:, :], ALU.add)

        @block.scalar
        def _(s):
            s.wait_ge(shifted, 1)
            s.activation(sx[:, :, :], sc[:, :, :], ACT.Exp).then_inc(exped, 1)

        @block.tensor
        def _(pe):
            pe.wait_ge(k_ready, 1)
            pe.wait_ge(loaded, 19 * 16)
            for b in range(B):
                for o in range(0, HEADS, 16):
                    for m in range(8):
                        mm = pe.matmul(ps[T * b:T * b + T, o:o + 16, :], xt[:, m, T * b:T * b + T],
                                       kp[:, m, o:o + 16, T * b:T * b + T], start=(m == 0), stop=(m == 7))
            mm.then_inc(scores_done, 1)


def stage_value_tables(k):
    nc, a = k.nc, k.a
    with ExitStack() as ctx:
        sb = lambda name, shape: k.sb(name, shape, ctx=ctx)
        wv, wp = sb("s3_wv", [128, 4, 512]), sb("s3_wp", [128, 2, 512])
        herm = sb("s3_herm", [128, 2, 512])
        fac = sb("s3_fac", [128, 2])
        d, t = sb("s3_d", [128, 2, 512]), sb("s3_t", [128, 3, 512])
        loaded, chain, stored = k.sem("s3_loaded"), k.sem("s3_chain"), k.sem("s3_stored")
        block = ctx.enter_context(nc.Block())

        @block.sync
        def _(sp):
            sp.dma_start(wv[:, :, :], a["wV"]).then_inc(loaded, 16)
            sp.dma_start(wp[:, :, :], a["wP"]).then_inc(loaded, 16)
            sp.dma_start(herm[:, :, :], a["herm_full"].rearrange("p (u f) -> p u f", u=2)).then_inc(loaded, 16)
            for j, name in enumerate(("wVs", "wPs")):
                sp.dma_start(fac[:, j:j + 1], sub(a[name], 0, [[1, HEADS], [0, 4], [1, 1]])).then_inc(loaded, 16)
            sp.wait_ge(chain, 15)
            for c in range(2):
                sp.dma_start(sub(a["d_d"], 2048 * c, [[4096, HEADS], [512, 4], [1, 512]]), d[:, c, :]).then_inc(stored, 16)
            sp.wait_ge(stored, 32)

        @block.vector
        def _(v):
            link = Chain(v, chain)
            tt = lambda o, x, y, op: link(v.tensor_tensor(o, x, y, op))
            v.wait_ge(loaded, 80)
            for j in range(4):
                tt(wv[:, j, :], wv[:, j, :], herm[:, j // 2, :], ALU.mult)
            tt(wv[:, 0, :], wv[:, 0, :], wv[:, 2, :], ALU.add)
            tt(wv[:, 1, :], wv[:, 1, :], wv[:, 3, :], ALU.subtract)
            vr, vi, pr, pi = wv[:, 0, :], wv[:, 1, :], wp[:, 0, :], wp[:, 1, :]
            link(v.tensor_scalar(t[:, 0, :], vr, fac[:, 0:1], None, ALU.add))
            tt(d[:, 0, :], pr, t[:, 0, :], ALU.mult)
            tt(t[:, 1, :], pi, vi, ALU.mult)
            tt(d[:, 0, :], d[:, 0, :], t[:, 1, :], ALU.subtract)
            link(v.scalar_tensor_tensor(out=d[:, 0, :], in0=vr, scalar=fac[:, 1:2], in1=d[:, 0, :],
                                        op0=ALU.mult, op1=ALU.add))
            tt(d[:, 1, :], pr, vi, ALU.mult)
            tt(t[:, 2, :], pi, t[:, 0, :], ALU.mult)
            tt(d[:, 1, :], d[:, 1, :], t[:, 2, :], ALU.add)
            link(v.scalar_tensor_tensor(out=d[:, 1, :], in0=vi, scalar=fac[:, 1:2], in1=d[:, 1, :],
                                        op0=ALU.mult, op1=ALU.add))


def stage_mix(k, att):
    nc, a = k.nc, k.a
    with ExitStack() as ctx:
        sb = lambda name, shape: k.sb(name, shape, ctx=ctx)
        HALF = NN * NM // 2
        x4 = sb("s4_x4", [128, B, 2, HALF])
        dd = sb("s4_dd", [128, 2, 2, HALF])
        y = sb("s4_y", [128, 2, 2, HALF])
        tv, tp = sb("s4_tv", [128, HALF]), sb("s4_tp", [128, HALF])
        z = sb("s4_z", [64, 4 * 512])
        xin, xout = sb("s4_xin", [128, 4, 512]), sb("s4_xout", [128, 4, 512])
        psz = k.ps("s4_psz", [64, 4 * 512], ctx)
        pss = k.ps("s4_pss", [128, 4, 512], ctx)
        x4_loaded, d_loaded = k.sem("s4_x4_loaded"), [k.sem("s4_d0_loaded"), k.sem("s4_d1_loaded")]
        re_ready, im_ready = k.sem("s4_re_ready"), k.sem("s4_im_ready")
        chain_v, chain_p = k.sem("s4_chain_v"), k.sem("s4_chain_p")
        mixed, z_copied, z_stored = k.sem("s4_mixed"), k.sem("s4_z_copied"), k.sem("s4_z_stored")
        xin_loaded, skip_done = k.sem("s4_xin_loaded"), k.sem("s4_skip_done")
        skip_copied, skip_stored = k.sem("s4_skip_copied"), k.sem("s4_skip_stored")
        block = ctx.enter_context(nc.Block())
        STEPS = HEADS // 4 * B

        @block.sync
        def _(sp):
            with sp.Fori(0, 2) as nh:
                sp.wait_ge(mixed, nh * STEPS)
                for b in range(B):
                    for o in range(4):
                        sp.dma_start(x4[32 * o:32 * o + 32, b, :, :],
                                     sub(a["xf_d"], nh * HALF + b * T * 4096,
                                         [[4096, T], [2048, 2], [1, HALF]])).then_inc(x4_loaded, 16)
                for oc in range(HEADS // 4):
                    if oc >= 2:
                        sp.wait_ge(re_ready, nh * STEPS + 2 * (oc - 1))
                        sp.wait_ge(im_ready, nh * STEPS + 2 * (oc - 1))
                    for o in range(4):
                        sp.dma_start(dd[32 * o:32 * o + 32, oc % 2, :, :],
                                     sub(a["d_d"], nh * HALF + (4 * oc + o) * 4096,
                                         [[0, 32], [2048, 2], [1, HALF]])).then_inc(d_loaded[oc % 2], 16)
                sp.wait_ge(z_copied, nh + 1)
                sp.dma_start(sub(a["z_d"], nh * HALF, [[4096, NI], [2048, 2], [1, HALF]]),
                             z[:, :].rearrange("p (c f) -> p c f", c=2)).then_inc(z_stored, 16)
            sp.wait_ge(z_stored, 32)

        @block.gpsimd
        def _(p):
            with p.Fori(0, 2) as nh:
                p.wait_ge(x4_loaded, 128 * nh + 128)
                for j in range(STEPS):
                    oc, b = j // 2, j % 2
                    p.wait_ge(d_loaded[oc % 2], 256 * nh + 64 * (oc // 2) + 64)
                    if j >= 2:
                        p.wait_ge(mixed, nh * STEPS + (j - 1))
                    dr, di, xr, xi = dd[:, oc % 2, 0, :], dd[:, oc % 2, 1, :], x4[:, b, 0, :], x4[:, b, 1, :]
                    p.tensor_tensor(tp[:, :], di, xr, ALU.mult).then_inc(chain_p, 1)
                    p.tensor_tensor(y[:, j % 2, 1, :], dr, xi, ALU.mult).then_inc(chain_p, 1)
                    p.wait_ge(chain_p, nh * 2 * STEPS + (2 * j + 2))
                    p.tensor_tensor(y[:, j % 2, 1, :], y[:, j % 2, 1, :], tp[:, :], ALU.add).then_inc(im_ready, 1)
                    p.wait_ge(im_ready, nh * STEPS + (j + 1))

        @block.vector
        def _(v):
            with v.Fori(0, 2) as nh:
                v.wait_ge(x4_loaded, 128 * nh + 128)
                for j in range(STEPS):
                    oc, b = j // 2, j % 2
                    v.wait_ge(d_loaded[oc % 2], 256 * nh + 64 * (oc // 2) + 64)
                    if j >= 2:
                        v.wait_ge(mixed, nh * STEPS + (j - 1))
                    dr, di, xr, xi = dd[:, oc % 2, 0, :], dd[:, oc % 2, 1, :], x4[:, b, 0, :], x4[:, b, 1, :]
                    v.tensor_tensor(tv[:, :], di, xi, ALU.mult).then_inc(chain_v, 1)
                    v.tensor_tensor(y[:, j % 2, 0, :], dr, xr, ALU.mult).then_inc(chain_v, 1)
                    v.wait_ge(chain_v, nh * 2 * STEPS + (2 * j + 2))
                    v.tensor_tensor(y[:, j % 2, 0, :], y[:, j % 2, 0, :], tv[:, :], ALU.subtract).then_inc(re_ready, 1)
                    v.wait_ge(re_ready, nh * STEPS + (j + 1))

        @block.scalar
        def _(s):
            with s.Fori(0, 4) as i:
                for half in range(2):
                    s.dma_start(xin[64 * half:64 * half + 64, :, :],
                                sub(a["xn_d"], half * (PIX // 2) + i * 2048,
                                    [[PIX, NI], [512, 4], [1, 512]])).then_inc(xin_loaded, 16)
                s.wait_ge(skip_done, i + 1)
                for j in range(4):
                    ins = s.activation(xout[:, j, :], pss[:, j, :], ACT.Copy)
                ins.then_inc(skip_copied, 1)
                s.wait_ge(skip_copied, i + 1)
                for half in range(2):
                    s.dma_start(sub(a["sk_d"], half * (PIX // 2) + i * 2048, [[PIX, NI], [512, 4], [1, 512]]),
                                xout[64 * half:64 * half + 64, :, :]).then_inc(skip_stored, 16)
                s.wait_ge(skip_stored, 32 * i + 32)
            with s.Fori(0, 2) as nh:
                s.wait_ge(mixed, nh * STEPS + STEPS)
                for j in range(4):
                    ins = s.activation(z[:, 512 * j:512 * j + 512], psz[:, 512 * j:512 * j + 512], ACT.Copy)
                ins.then_inc(z_copied, 1)
                s.wait_ge(z_stored, 16 * nh + 16)

        @block.tensor
        def _(pe):
            with pe.Fori(0, 4) as i:
                pe.wait_ge(xin_loaded, 32 * i + 32)
                pe.wait_ge(skip_copied, i)
                for j in range(4):
                    mm = pe.matmul(pss[:, j, :], att.mix_t[:, :], xin[:, j, :], start=True, stop=True)
                mm.then_inc(skip_done, 1)
            with pe.Fori(0, 2) as nh:
                pe.wait_ge(z_copied, nh)
                for j in range(STEPS):
                    oc, b = j // 2, j % 2
                    pe.wait_ge(re_ready, nh * STEPS + (j + 1))
                    pe.wait_ge(im_ready, nh * STEPS + (j + 1))
                    for q in range(4):
                        mm = pe.matmul(psz[T * b:T * b + T, 512 * q:512 * q + 512], att.prob_t[:, oc, b, :],
                                       y[:, j % 2, q // 2, 512 * (q % 2):512 * (q % 2) + 512],
                                       start=(oc == 0), stop=(oc == HEADS // 4 - 1))
                    mm.then_inc(mixed, 1)


def pe_inverse(pe, z, icols, irows, ps_b, bs, ps_o, z_ready, n_z, cols_done, bs_ready, n_b, out_done):
    pe.wait_ge(z_ready, n_z)
    for i in range(GROUP):
        mm = pe.matmul(ps_b[:, i, :], z[:, i, :, :], icols[:, :], start=True, stop=True)
    mm.then_inc(cols_done, 1)
    pe.wait_ge(bs_ready, n_b)
    for i in range(0, GROUP, 4):
        mm = pe.matmul(ps_o[:, i:i + 4, :], irows[:, :], bs[:, i:i + 4, :], start=True, stop=True)
    mm.then_inc(out_done, 1)


def stage_project(k, att):
    nc, a = k.nc, k.a
    with ExitStack() as ctx:
        sb = lambda name, shape: k.sb(name, shape, ctx=ctx)
        zs, zw = sb("s5_zs", [64, NI, NM]), sb("s5_zw", [64, NI, NM])
        sign = sb("s5_sign", [64, 1])
        sk = sb("s5_sk", [128, GROUP, HW])
        z = sb("s5_z", [64, GROUP, 2, NM])
        icols, irows = sb("s5_icols", [64, 128]), sb("s5_irows", [128, 128])
        dc = sb("s5_dc", [64, 1])
        bs = sb("s5_bs", [128, GROUP, HW])
        ps_b, ps_o = k.ps("s5_psb", [128, GROUP, HW], ctx), k.ps("s5_pso", [128, GROUP, HW], ctx)
        loaded, sk_loaded, dc_added = k.sem("s5_loaded"), k.sem("s5_sk_loaded"), k.sem("s5_dc_added")
        z_ready, cols_done, bs_ready = k.sem("s5_z_ready"), k.sem("s5_cols_done"), k.sem("s5_bs_ready")
        out_done, out_added, sk_added = k.sem("s5_out_done"), k.sem("s5_out_added"), k.sem("s5_sk_added")
        block = ctx.enter_context(nc.Block())

        @block.sync
        def _(sp):
            sp.dma_start(zs[:, :, :], sub(a["z_d"], 0, [[NM, 64], [4096, NI], [1, NM]])).then_inc(loaded, 16)
            for c in range(2):
                sp.dma_start(zw[32 * c:32 * c + 32, :, :],
                             sub(a["z_d"], 2048 * (1 - c), [[NM, 32], [4096, NI], [1, NM]])).then_inc(loaded, 16)
            sp.dma_start(sign[:, :], a["im_sign"][32:96]).then_inc(loaded, 16)
            sp.dma_start(icols[:, :], a["idft_cols"]).then_inc(loaded, 16)
            sp.dma_start(irows[:, :], a["idft_rows"]).then_inc(loaded, 16)
            with sp.Fori(0, NG) as g:
                sp.wait_ge(sk_added, g)
                sp.dma_start(sk[:, :, :], a["sk_d"][bass.ds(g * GROUP, GROUP)].rearrange("i h w -> h i w"))\
                  .then_inc(sk_loaded, 16)
            sp.wait_ge(sk_loaded, 16 * NG)

        @block.vector
        def _(v):
            v.wait_ge(loaded, 96)
            v.tensor_scalar(zs[0:1, :, 0], zs[0:1, :, 0], att.dc[0:1, 0:1], None, ALU.add).then_inc(dc_added, 1)
            v.tensor_copy(dc[32:33, :], att.dc[0:1, 0:1]).then_inc(dc_added, 1)
            v.wait_ge(dc_added, 2)
            v.tensor_scalar(zw[32:33, :, 0], zw[32:33, :, 0], dc[32:33, 0:1], None, ALU.add).then_inc(dc_added, 1)
            v.wait_ge(dc_added, 3)
            with v.Fori(0, NG) as g:
                v.wait_ge(cols_done, g)
                v.tensor_copy(z[:, :, 0, :], zs[:, bass.ds(g * GROUP, GROUP), :])
                v.tensor_scalar(z[:, :, 1, :], zw[:, bass.ds(g * GROUP, GROUP), :], sign[:, 0:1], None, ALU.mult)\
                 .then_inc(z_ready, 1)
                v.wait_ge(sk_loaded, 16 * g + 16)
                xg = k.xa[:, bass.ds(g * GROUP, GROUP), :]
                v.tensor_tensor(xg, xg, sk[:, :, :], ALU.add).then_inc(sk_added, 1)
                v.wait_ge(sk_added, g + 1)
                v.wait_ge(out_done, g + 1)
                for i in range(0, GROUP, 4):
                    xg = k.xa[:, bass.ds(g * GROUP + i, 4), :]
                    ins = v.tensor_tensor(xg, ps_o[:, i:i + 4, :], xg, ALU.add)
                ins.then_inc(out_added, 1)

        @block.scalar
        def _(s):
            with s.Fori(0, NG) as g:
                s.wait_ge(cols_done, g + 1)
                s.wait_ge(out_done, g)
                for i in range(0, GROUP, 4):
                    ins = s.activation(bs[:, i:i + 4, :], ps_b[:, i:i + 4, :], ACT.Copy)
                ins.then_inc(bs_ready, 1)

        @block.tensor
        def _(pe):
            pe.wait_ge(loaded, 96)
            with pe.Fori(0, NG) as g:
                pe.wait_ge(out_added, g)
                pe_inverse(pe, z, icols, irows, ps_b, bs, ps_o, z_ready, g + 1, cols_done, bs_ready, g + 1, out_done)


def v_row_moments(v, link, src, st, mom, tmp, ready):
    with v.Fori(0, NI) as i:
        v.bn_stats(st[:, bass.ds(i, 1), :], src[:, bass.ds(i, 1), :])
    link(v.memset(tmp, 0.0))
    row_stats(v, link, st, mom[:, 0, :], mom[:, 1, :], tmp)
    link(v.tensor_tensor(tmp, mom[:, 0, :], mom[:, 0, :], ALU.mult))
    v.tensor_tensor(mom[:, 1, :], mom[:, 1, :], tmp, ALU.add).then_inc(ready, 1)


def v_image_norm(v, link, ps, mom_done, n, mean, var, scale, bias, tmp, veps, root, gain, shift, var_ready, root_ready, nr):
    v.wait_ge(mom_done, n)
    link(v.tensor_copy(mean, ps[:, 0:NI]))
    link(v.tensor_tensor(tmp, mean, mean, ALU.mult))
    link(v.tensor_tensor(var, ps[:, NI:2 * NI], tmp, ALU.subtract))
    link(v.tensor_scalar(veps, var, 0.0, 1e-5, ALU.max, ALU.add))
    v.tensor_scalar(veps, veps, 1.0, None, ALU.mult).then_inc(var_ready, 1)
    v.wait_ge(var_ready, nr)
    newton_rsqrt(v, link, veps, root, scale, tmp, root_ready, nr)
    link(v.tensor_scalar(scale, scale, gain, None, ALU.mult))
    link(v.tensor_tensor(tmp, mean, scale, ALU.mult))
    link(v.tensor_scalar(bias, tmp, -1.0, shift, ALU.mult, ALU.add))


def stage_mixer(k):
    nc, a = k.nc, k.a
    with ExitStack() as ctx:
        sb = lambda name, shape: k.sb(name, shape, ctx=ctx)
        f, m = sb("s6_f", [HW, NI, HW]), sb("s6_m", [HW, NI, HW])
        st = sb("s6_st", [128, NI, 6])
        mom = sb("s6_mom", [128, 2, NI])
        names = ("mean", "var", "scale", "bias", "tmp", "veps", "root", "as", "ab", "fs", "fb")
        mean, var, scale, bias, tmp, veps, root, a_s, a_b, f_s, f_b = (sb(f"s6_{n}", [128, NI]) for n in names)
        rows, cols = sb("s6_rows", [128, 128]), sb("s6_cols", [128, 256])
        icols, irows = sb("s6_icols", [64, 128]), sb("s6_irows", [128, 128])
        w = sb("s6_w", [64, 2, 2, NM])
        sk = sb("s6_sk", [128, 2, 2])
        xg = sb("s6_xg", [128, GROUP, HW])
        yt = sb("s6_yt", [128, GROUP, 128])
        z, zt = sb("s6_z", [64, GROUP, 2, NM]), sb("s6_zt", [64, GROUP, 2, NM])
        bs = sb("s6_bs", [128, GROUP, HW])
        ps_a, ps_b, ps_o = (k.ps(f"s6_{n}", [128, GROUP, HW], ctx) for n in ("psa", "psb", "pso"))
        ps_x, ps_w = k.ps("s6_psx", [128, 512], ctx), k.ps("s6_psw", [64, 512], ctx)
        loaded, chain = k.sem("s6_loaded"), k.sem("s6_chain")
        mom_ready, mom_done = k.sem("s6_mom_ready"), k.sem("s6_mom_done")
        var_ready, root_ready = k.sem("s6_var_ready"), k.sem("s6_root_ready")
        xg_ready, rows_done, yt_ready = k.sem("s6_xg_ready"), k.sem("s6_rows_done"), k.sem("s6_yt_ready")
        spec_done, mul_done, z_ready = k.sem("s6_spec_done"), k.sem("s6_mul_done"), k.sem("s6_z_ready")
        cols_done, bs_ready, out_done = k.sem("s6_cols_done"), k.sem("s6_bs_ready"), k.sem("s6_out_done")
        f_ready, pre_ready, gelu_done = k.sem("s6_f_ready"), k.sem("s6_pre_ready"), k.sem("s6_gelu_done")
        part_ready = k.sem("s6_part_ready")
        block = ctx.enter_context(nc.Block())

        @block.sync
        def _(sp):
            sp.dma_start(rows[:, :], a["dft_rows"][:, 0:128]).then_inc(loaded, 16)
            sp.dma_start(cols[:, :], a["dft_cols"]).then_inc(loaded, 16)
            sp.dma_start(icols[:, :], a["idft_cols"]).then_inc(loaded, 16)
            sp.dma_start(irows[:, :], a["idft_rows"]).then_inc(loaded, 16)
            for j in range(2):
                sp.dma_start(w[:, j, :, :], a[f"wM{j}"]).then_inc(loaded, 16)
                sp.dma_start(sk[:, j, 0:1], sub(a[f"wM{j}s"], 0, [[0, 128], [1, 1]])).then_inc(loaded, 16)
                sp.dma_start(sk[:, j, 1:2], sub(a[f"bM{j}s"], 0, [[0, 128], [1, 1]])).then_inc(loaded, 16)
            sp.wait_ge(loaded, 160)

        @block.vector
        def _(v):
            link = Chain(v, chain)
            tt = lambda o, x, y, op: link(v.tensor_tensor(o, x, y, op))
            v.wait_ge(loaded, 160)
            v_row_moments(v, link, k.xa, st, mom, tmp[:, :], mom_ready)
            v_image_norm(v, link, ps_x, mom_done, 1, mean[:, :], var[:, :], scale[:, :], bias[:, :], tmp[:, :],
                         veps[:, :], root[:, :], k.norm_g[:, 1:2], k.norm_b[:, 1:2], var_ready, root_ready, 1)
            with v.Fori(0, NI) as i:
                one = bass.ds(i, 1)
                v.tensor_scalar(k.xa[:, one, :], k.xa[:, one, :], scale[:, one], bias[:, one], ALU.mult, ALU.add)
            tt(tmp[:, :], scale[:, :], scale[:, :], ALU.mult)
            tt(veps[:, :], var[:, :], tmp[:, :], ALU.mult)
            link(v.tensor_scalar(veps[:, :], veps[:, :], 1e-5, None, ALU.add))
            v.tensor_scalar(veps[:, :], veps[:, :], 1.0, None, ALU.mult).then_inc(var_ready, 1)
            v.wait_ge(var_ready, 2)
            newton_rsqrt(v, link, veps[:, :], root[:, :], a_s[:, :], tmp[:, :], root_ready, 2)
            link(v.tensor_scalar(a_s[:, :], a_s[:, :], k.norm_g[:, 2:3], None, ALU.mult))
            link(v.tensor_scalar(tmp[:, :], a_s[:, :], k.norm_b[:, 1:2], None, ALU.mult))
            link(v.tensor_scalar(a_b[:, :], tmp[:, :], -1.0, k.norm_b[:, 2:3], ALU.mult, ALU.add))
            for layer in range(2):
                n0 = layer * NG
                wr = w[:, layer, 0:1, :].broadcast_to([64, GROUP, NM])
                wi = w[:, layer, 1:2, :].broadcast_to([64, GROUP, NM])
                if layer == 1:
                    v.wait_ge(gelu_done, NI)
                with v.Fori(0, NG) as g:
                    v.wait_ge(rows_done, g + n0)
                    if layer == 0:
                        for i in range(GROUP):
                            one = bass.ds(g * GROUP + i, 1)
                            ins = v.tensor_scalar(xg[:, i, :], k.xa[:, one, :], a_s[:, one], a_b[:, one], ALU.mult, ALU.add)
                    else:
                        ins = v.tensor_copy(xg[:, :, :], m[:, bass.ds(g * GROUP, GROUP), :])
                    ins.then_inc(xg_ready, 1)
                    v.wait_ge(spec_done, g + (n0 + 1))
                    v.wait_ge(cols_done, g + n0)
                    x3 = lambda t: t.rearrange("p (i m) -> p i m", m=NM)
                    v.tensor_tensor(z[:, :, 0, :], x3(ps_x[0:64, :]), wr, ALU.mult).then_inc(mul_done, 1)
                    v.tensor_tensor(zt[:, :, 0, :], x3(ps_w[:, :]), wi, ALU.mult).then_inc(mul_done, 1)
                    v.tensor_tensor(z[:, :, 1, :], x3(ps_x[0:64, :]), wi, ALU.mult).then_inc(mul_done, 1)
                    v.tensor_tensor(zt[:, :, 1, :], x3(ps_w[:, :]), wr, ALU.mult).then_inc(mul_done, 1)
                    v.wait_ge(mul_done, g * 4 + (4 * n0 + 4))
                    v.tensor_tensor(z[:, :, 0, :], z[:, :, 0, :], zt[:, :, 0, :], ALU.add)
                    v.tensor_tensor(z[:, :, 1, :], z[:, :, 1, :], zt[:, :, 1, :], ALU.subtract).then_inc(z_ready, 1)
                v.wait_ge(f_ready, NG * (layer + 1))
                v_row_moments(v, link, f, st, mom, tmp[:, :], mom_ready)
                v_image_norm(v, link, ps_x, mom_done, 2 + layer, mean[:, :], var[:, :], f_s[:, :], f_b[:, :],
                             tmp[:, :], veps[:, :], root[:, :], k.norm_g[:, 3 + layer:4 + layer],
                             k.norm_b[:, 3 + layer:4 + layer], var_ready, root_ready, 3 + layer)
                if layer == 0:
                    link(v.tensor_scalar(scale[:, :], a_s[:, :], sk[:, 0, 0:1], None, ALU.mult))
                    link(v.tensor_scalar(tmp[:, :], a_b[:, :], sk[:, 0, 0:1], sk[:, 0, 1:2], ALU.mult, ALU.add))
                    tt(bias[:, :], f_b[:, :], tmp[:, :], ALU.add)
                    src = k.xa
                else:
                    link(v.memset(tmp[:, :], 0.0))
                    link(v.tensor_scalar(scale[:, :], tmp[:, :], sk[:, 1, 0:1], None, ALU.add))
                    link(v.tensor_scalar(bias[:, :], f_b[:, :], sk[:, 1, 1:2], None, ALU.add))
                    src = m
                with v.Fori(0, NI) as i:
                    one = bass.ds(i, 1)
                    v.tensor_scalar(f[:, one, :], f[:, one, :], f_s[:, one], bias[:, one], ALU.mult, ALU.add)\
                     .then_inc(part_ready, 1)
                v.wait_ge(part_ready, NI * (layer + 1))
                with v.Fori(0, NI) as i:
                    one = bass.ds(i, 1)
                    v.scalar_tensor_tensor(out=f[:, one, :], in0=src[:, one, :], scalar=scale[:, one], in1=f[:, one, :],
                                           op0=ALU.mult, op1=ALU.add).then_inc(pre_ready, 1)
            v.wait_ge(pre_ready, 2 * NI)
            v_row_moments(v, link, f, st, mom, tmp[:, :], mom_ready)
            v_image_norm(v, link, ps_x, mom_done, 4, mean[:, :], var[:, :], scale[:, :], bias[:, :], tmp[:, :],
                         veps[:, :], root[:, :], k.norm_g[:, 5:6], k.norm_b[:, 5:6], var_ready, root_ready, 5)
            with v.Fori(0, NI) as i:
                one = bass.ds(i, 1)
                v.tensor_scalar(f[:, one, :], f[:, one, :], scale[:, one], bias[:, one], ALU.mult, ALU.add)
            tt(k.x[:, :, :], k.x[:, :, :], k.xa[:, :, :], ALU.add)
            tt(k.x[:, :, :], k.x[:, :, :], f[:, :, :], ALU.add)

        @block.scalar
        def _(s):
            def root_step(n):
                s.wait_ge(var_ready, n)
                s.activation(root[:, :], veps[:, :], ACT.Sqrt).then_inc(root_ready, 1)

            root_step(1)
            root_step(2)
            for layer in range(2):
                n0 = layer * NG
                with s.Fori(0, NG) as g:
                    s.wait_ge(rows_done, g + (n0 + 1))
                    s.wait_ge(spec_done, g + n0)
                    for i in range(0, GROUP, 4):
                        ins = s.activation(yt[:, i:i + 4, :], ps_a[:, i:i + 4, :], ACT.Copy)
                    ins.then_inc(yt_ready, 1)
                    s.wait_ge(cols_done, g + (n0 + 1))
                    s.wait_ge(out_done, g + n0)
                    for i in range(0, GROUP, 4):
                        ins = s.activation(bs[:, i:i + 4, :], ps_b[:, i:i + 4, :], ACT.Copy)
                    ins.then_inc(bs_ready, 1)
                    s.wait_ge(out_done, g + (n0 + 1))
                    for i in range(0, GROUP, 4):
                        ins = s.activation(f[:, bass.ds(g * GROUP + i, 4), :], ps_o[:, i:i + 4, :], ACT.Copy)
                    ins.then_inc(f_ready, 1)
                root_step(3 + layer)
                if layer == 0:
                    with s.Fori(0, NI) as i:
                        s.wait_ge(pre_ready, i + 1)
                        s.activation(m[:, bass.ds(i, 1), :], f[:, bass.ds(i, 1), :], ACT.Gelu).then_inc(gelu_done, 1)
            root_step(5)

        @block.tensor
        def _(pe):
            def moments(n):
                pe.wait_ge(mom_ready, n)
                pe.matmul(ps_x[:, 0:128], k.ones[:, :], mom[:, :, :], start=True, stop=True).then_inc(mom_done, 1)

            moments(1)
            pe.wait_ge(loaded, 160)
            for layer in range(2):
                n0 = layer * NG
                with pe.Fori(0, NG) as g:
                    pe.wait_ge(xg_ready, g + (n0 + 1))
                    for i in range(GROUP):
                        mm = pe.matmul(ps_a[:, i, :], xg[:, i, :], rows[:, :], start=True, stop=True)
                    mm.then_inc(rows_done, 1)
                    pe.wait_ge(yt_ready, g + (n0 + 1))
                    pe.matmul(ps_x[0:64, :], cols[:, 0:64], yt[:, :, 0:64], start=True, stop=False)
                    pe.matmul(ps_x[0:64, :], cols[:, 64:128], yt[:, :, 64:128], start=False, stop=True)
                    pe.matmul(ps_w[:, :], cols[:, 128:192], yt[:, :, 0:64], start=True, stop=False)
                    pe.matmul(ps_w[:, :], cols[:, 192:256], yt[:, :, 64:128], start=False, stop=True).then_inc(spec_done, 1)
                    pe.wait_ge(f_ready, g + n0)
                    pe_inverse(pe, z, icols, irows, ps_b, bs, ps_o, z_ready, g + (n0 + 1), cols_done,
                               bs_ready, g + (n0 + 1), out_done)
                moments(2 + layer)
            moments(4)


NK = FT + 2
NF = 2 * NK


def stage_stu_setup(k, stu):
    nc, a = k.nc, k.a
    with ExitStack() as ctx:
        sb = lambda name, shape: k.sb(name, shape, ctx=ctx)
        st = sb("s7_st", [128, NI, 6])
        mean, var, rstd, root, tmp, veps = (sb(f"s7_{n}", [128, NI]) for n in ("mean", "var", "rstd", "root", "tmp", "veps"))
        ug = sb("s7_u", [128, GROUP, HW])
        mload = sb("s7_mload", [128, 2, FT * 128])
        mp, mm_ = sb("s7_mp", [128, FT * 128]), sb("s7_mm", [128, FT * 128])
        mu, mut = sb("s7_mu", [128, 4, 3, 128]), sb("s7_mut", [128, 3, 128])
        lw, oh, ys = sb("s7_lw", [128, 2, 4]), sb("s7_oh", [128, 4]), sb("s7_ys", [128, 4])
        z4, t4, u4 = sb("s7_z4", [128, 4]), sb("s7_t4", [128, 4]), sb("s7_u4", [128, 4])
        one = sb("s7_one", [128, 2])
        masks = sb("s7_masks", [128, 4, NI])
        sig, sq, sr, s_t = (sb(f"s7_{n}", [128, FT]) for n in ("sig", "sq", "sr", "st4"))
        phi = sb("s7_phi", [33, NF, 128])
        fb = sb("s7_fb", [33, 128])
        gt = sb("s7_gt", [64, NF, 128, 2])
        ps = k.ps("s7_ps", [128, 2, 512], ctx)
        loaded, m_loaded = k.sem("s7_loaded"), [k.sem("s7_m0_loaded"), k.sem("s7_m1_loaded")]
        chain, var_ready, root_ready = k.sem("s7_chain"), k.sem("s7_var_ready"), k.sem("s7_root_ready")
        u_ready, u_stored, m_used = k.sem("s7_u_ready"), k.sem("s7_u_stored"), k.sem("s7_m_used")
        exp_in, exp_done = k.sem("s7_exp_in"), k.sem("s7_exp_done")
        g_done, g_copied, g_stored = k.sem("s7_g_done"), k.sem("s7_g_copied"), k.sem("s7_g_stored")
        block = ctx.enter_context(nc.Block())

        @block.sync
        def _(sp):
            sp.dma_start(phi[:, :, :], a["phi"]).then_inc(loaded, 16)
            sp.dma_start(fb[:, :], a["filter_dft"]).then_inc(loaded, 16)
            sp.dma_start(lw[:, 0, :], sub(a["log_weights"], 0, [[0, 128], [1, 4]])).then_inc(loaded, 16)
            sp.dma_start(lw[:, 1, :], sub(a["gumbel"], 0, [[0, 128], [1, 4]])).then_inc(loaded, 16)
            sp.dma_start(sig[:, :], sub(a["sigma"], 0, [[0, 128], [1, FT]])).then_inc(loaded, 16)
            sp.dma_start(masks[:, :, :], sub(a["masks"], 0, [[0, 128], [NI, 4], [1, NI]])).then_inc(loaded, 16)
            sp.dma_start(mu[:, :, :, :].rearrange("d i t e -> d (i t) e"),
                         a["M_u"].rearrange("i t d e -> d (i t) e")).then_inc(loaded, 16)
            for j in range(8):
                src = a["M_phi_plus"] if j % 2 == 0 else a["M_phi_minus"]
                if j >= 2:
                    sp.wait_ge(m_used, j - 1)
                sp.dma_start(mload[:, j % 2, :].rearrange("d (k e) -> d k e", e=128),
                             src[j // 2].rearrange("k d e -> d k e")).then_inc(m_loaded[j % 2], 16)
            with sp.Fori(0, NG) as g:
                sp.wait_ge(u_ready, g + 1)
                sp.dma_start(a["u_d"][bass.ds(g * GROUP, GROUP)].rearrange("i h w -> h i w"), ug[:, :, :])\
                  .then_inc(u_stored, 16)
            sp.wait_ge(u_stored, 16 * NG)
            sp.wait_ge(g_copied, 9)
            for c in range(2):
                sp.dma_start(sub(a["tc_d"], c * NF * 256, [[2 * NF * 256, NQ], [1, NF * 256]]),
                             gt[32 * c:32 * c + 32, :, :, :].rearrange("p f x c -> p (f x c)")).then_inc(g_stored, 16)
            sp.wait_ge(g_stored, 32)

        @block.vector
        def _(v):
            link = Chain(v, chain)
            tt = lambda o, x, y, op: link(v.tensor_tensor(o, x, y, op))
            ts = lambda o, x, s1, s2, op0, op1=None: link(v.tensor_scalar(o, x, s1, s2, op0, op1) if op1 is not None
                                                          else v.tensor_scalar(o, x, s1, s2, op0))
            v.wait_ge(loaded, 112)
            tt(z4[:, :], lw[:, 0, :], lw[:, 1, :], ALU.add)
            link(v.tensor_reduce(one[:, 0:1], z4[:, :], AX.X, ALU.max))
            v.tensor_scalar(z4[:, :], z4[:, :], one[:, 0:1], None, ALU.subtract).then_inc(exp_in, 1)
            v.wait_ge(exp_done, 1)
            link(v.tensor_reduce(one[:, 0:1], t4[:, :], AX.X, ALU.add))
            link(v.reciprocal(one[:, 1:2], one[:, 0:1]))
            ts(ys[:, :], t4[:, :], one[:, 1:2], None, ALU.mult)
            link(v.tensor_reduce(one[:, 0:1], ys[:, :], AX.X, ALU.max))
            ts(u4[:, :], ys[:, :], one[:, 0:1], None, ALU.is_equal)
            link(v.memset(one[:, 1:2], 1.0))
            for i in range(4):
                tt(oh[:, i:i + 1], u4[:, i:i + 1], one[:, 1:2], ALU.mult)
                tt(one[:, 1:2], one[:, 1:2], oh[:, i:i + 1], ALU.subtract)
            tt(t4[:, :], oh[:, :], ys[:, :], ALU.subtract)
            tt(t4[:, :], t4[:, :], ys[:, :], ALU.add)
            for i in range(4):
                if i == 0:
                    ts(stu.mask[:, :], masks[:, i, :], oh[:, i:i + 1], None, ALU.mult)
                else:
                    link(v.scalar_tensor_tensor(out=stu.mask[:, :], in0=masks[:, i, :], scalar=oh[:, i:i + 1],
                                                in1=stu.mask[:, :], op0=ALU.mult, op1=ALU.add))
            ts(sq[:, :], sig[:, :], 1.0, None, ALU.mult)
            for n in range(2):
                v.tensor_scalar(s_t[:, :], sq[:, :], 1.0, None, ALU.mult).then_inc(var_ready, 1)
                v.wait_ge(root_ready, n + 1)
                ts(s_t[:, :], sr[:, :], 1e-30, None, ALU.max)
                link(v.reciprocal(s_t[:, :], s_t[:, :]))
                tt(s_t[:, :], s_t[:, :], sq[:, :], ALU.mult)
                tt(s_t[:, :], s_t[:, :], sr[:, :], ALU.add)
                ts(sq[:, :], s_t[:, :], 0.5, None, ALU.mult)
            for j in range(8):
                acc = mp if j % 2 == 0 else mm_
                v.wait_ge(m_loaded[j % 2], 16 * (j // 2) + 16)
                if j < 2:
                    v.tensor_scalar(acc[:, :], mload[:, j % 2, :], t4[:, 0:1], None, ALU.mult).then_inc(m_used, 1)
                else:
                    v.scalar_tensor_tensor(out=acc[:, :], in0=mload[:, j % 2, :], scalar=t4[:, j // 2:j // 2 + 1],
                                           in1=acc[:, :], op0=ALU.mult, op1=ALU.add).then_inc(m_used, 1)
                v.wait_ge(m_used, j + 1)
            for s_, (dst, op) in enumerate(((stu.me, ALU.add), (stu.mo, ALU.subtract))):
                tt(mload[:, 0, :], mp[:, :], mm_[:, :], op)
                tt(dst[:, 0:FT, :], mload[:, 0, :].rearrange("d (k e) -> d k e", e=128),
                   sq[:, :].unsqueeze(2).broadcast_to([128, FT, 128]), ALU.mult)
            for i in range(4):
                if i == 0:
                    ts(mut[:, :, :], mu[:, i, :, :], t4[:, 0:1], None, ALU.mult)
                else:
                    link(v.scalar_tensor_tensor(out=mut[:, :, :], in0=mu[:, i, :, :], scalar=t4[:, i:i + 1],
                                                in1=mut[:, :, :], op0=ALU.mult, op1=ALU.add))
            link(v.tensor_copy(stu.me[:, FT, :], mut[:, 0, :]))
            link(v.tensor_copy(stu.me[:, FT + 1, :], mut[:, 2, :]))
            link(v.tensor_copy(stu.mo[:, FT, :], mut[:, 1, :]))
            with v.Fori(0, NI) as i:
                v.bn_stats(st[:, bass.ds(i, 1), :], k.x[:, bass.ds(i, 1), :])
            link(v.memset(tmp[:, :], 0.0))
            row_stats(v, link, st, mean[:, :], var[:, :], tmp[:, :])
            ts(tmp[:, :], var[:, :], 1e-5, None, ALU.add)
            v.tensor_copy(veps[:, :], tmp[:, :]).then_inc(var_ready, 1)
            v.wait_ge(var_ready, 3)
            newton_rsqrt(v, link, veps[:, :], root[:, :], rstd[:, :], tmp[:, :], root_ready, 3)
            with v.Fori(0, NG) as g:
                v.wait_ge(u_stored, 16 * g)
                for i in range(GROUP):
                    o = bass.ds(g * GROUP + i, 1)
                    ins = v.tensor_scalar(ug[:, i, :], k.x[:, o, :], mean[:, o], rstd[:, o], ALU.subtract, ALU.mult)
                ins.then_inc(u_ready, 1)

        @block.scalar
        def _(s):
            s.wait_ge(exp_in, 1)
            s.activation(t4[:, :], z4[:, :], ACT.Exp).then_inc(exp_done, 1)
            for n in range(2):
                s.wait_ge(var_ready, n + 1)
                s.activation(sr[:, :], s_t[:, :], ACT.Sqrt).then_inc(root_ready, 1)
            for n in range(9):
                s.wait_ge(g_done, n + 1)
                for r in range(4):
                    dst = gt[32 * (r // 2):32 * (r // 2) + 32, 4 * n:4 * n + 4, :, r % 2]
                    ins = s.activation(dst, ps[32 * r:32 * r + 32, n % 2, :].rearrange("p (f x) -> p f x", x=128), ACT.Copy)
                ins.then_inc(g_copied, 1)
            s.wait_ge(var_ready, 3)
            s.activation(root[:, :], veps[:, :], ACT.Sqrt).then_inc(root_ready, 1)

        @block.tensor
        def _(pe):
            pe.wait_ge(loaded, 112)
            for n in range(9):
                if n >= 2:
                    pe.wait_ge(g_copied, n - 1)
                pe.matmul(ps[:, n % 2, :], fb[:, :], phi[:, 4 * n:4 * n + 4, :], start=True, stop=True).then_inc(g_done, 1)


def stage_stu_blocks(k, stu):
    nc, a = k.nc, k.a
    with ExitStack() as ctx:
        ug = k.sb("s8_u", [64, 2, GROUP, HW], ctx=ctx)
        fwd = k.sb("s8_fwd", [64, 2, 128], ctx=ctx)
        ps = k.ps("s8_ps", [128, 2, GROUP, 128], ctx)
        psl = k.ps("s8_psl", [128, 128], ctx)
        loaded, u_loaded = k.sem("s8_loaded"), [k.sem("s8_u0_loaded"), k.sem("s8_u1_loaded")]
        done, copied, last = k.sem("s8_done"), k.sem("s8_copied"), k.sem("s8_last")
        block = ctx.enter_context(nc.Block())

        @block.sync
        def _(sp):
            sp.dma_start(fwd[:, :, :], a["block_dft"].rearrange("p (u f) -> p u f", u=2)).then_inc(loaded, 16)
            with sp.Fori(0, 8) as i:
                for u in range(2):
                    sp.wait_ge(done, 2 * i)
                    sp.dma_start(ug[:, u, :, :],
                                 sub(a["u_d"], (2 * i + u) * GROUP * HW, [[PIX, NI], [HW, GROUP], [1, HW]]))\
                      .then_inc(u_loaded[u], 16)
            sp.wait_ge(done, 16)

        @block.tensor
        def _(pe):
            pe.wait_ge(loaded, 16)
            with pe.Fori(0, 8) as i:
                for u in range(2):
                    pe.wait_ge(u_loaded[u], 16 * i + 16)
                    pe.wait_ge(copied, 2 * i)
                    for j in range(GROUP):
                        mm = pe.matmul(ps[:, u, j, :], ug[:, u, j, :], fwd[:, 0, :], start=True, stop=True)
                    mm.then_inc(done, 1)
            pe.matmul(psl[:, :], ug[:, 1, GROUP - 1, :], fwd[:, 1, :], start=True, stop=True).then_inc(last, 1)

        @block.scalar
        def _(s):
            with s.Fori(0, 8) as i:
                for u in range(2):
                    s.wait_ge(done, 2 * i + (u + 1))
                    for j in range(0, GROUP, 4):
                        ins = s.activation(stu.xt[:, bass.ds((2 * i + u) * GROUP + j, 4), :], ps[:, u, j:j + 4, :], ACT.Copy)
                    ins.then_inc(copied, 1)
            s.wait_ge(last, 1)
            s.activation(stu.xl[:, :], psl[:, :], ACT.Copy)


def stage_stu_filter(k, stu):
    nc, a = k.nc, k.a
    CH = [4, 4, 4, 4, 2]
    UN = 8 * len(CH)
    with ExitStack() as ctx:
        sb = lambda name, shape: k.sb(name, shape, ctx=ctx)
        tc = sb("s9_tc", [128, 2, NF, 128])
        xs = sb("s9_xs", [128, 2, 3, B, 128])
        w = sb("s9_w", [128, 2, 4, 2, 2, B, 128])
        y = sb("s9_y", [128, 2, 512])
        psw = k.ps("s9_psw", [128, 4, 512], ctx)
        psy = k.ps("s9_psy", [128, 2, 512], ctx)
        tc_loaded, y_stored = [k.sem(f"s9_tc{u}_loaded") for u in range(2)], [k.sem(f"s9_y{u}_stored") for u in range(2)]
        xs_ready, w_done = k.sem("s9_xs_ready"), k.sem("s9_w_done")
        copied = [k.sem("s9_copied_v"), k.sem("s9_copied_s")]
        proj_done, filt_done, q_done, y_copied = k.sem("s9_proj_done"), k.sem("s9_filt_done"), k.sem("s9_q_done"), k.sem("s9_y_copied")
        block = ctx.enter_context(nc.Block())
        NC = len(CH)

        def source(p, s):
            return s if p == 0 else 2 - 2 * s

        @block.sync
        def _(sp):
            def load(u, q):
                for c in range(2):
                    sp.dma_start(tc[64 * c:64 * c + 64, u, :, :],
                                 sub(a["tc_d"], (2 * q + c) * (NF * 256), [[2, 64], [256, NF], [1, 128]]))\
                      .then_inc(tc_loaded[u], 16)

            def store(u, q):
                for c in range(2):
                    sp.dma_start(sub(a["yh_d"], (2 * q + c) * (64 * 512), [[512, 64], [1, 512]]), y[c::2, u, :])\
                      .then_inc(y_stored[u], 16)

            load(0, 0)
            load(1, 1)
            with sp.Fori(0, NQ // 2 - 1) as i:
                for u in range(2):
                    sp.wait_ge(q_done, 2 * i + (u + 1))
                    load(u, 2 * i + (u + 2))
                    sp.wait_ge(y_copied, 2 * i + (u + 1))
                    store(u, 2 * i + u)
            for u in range(2):
                sp.wait_ge(y_copied, NQ - 1 + u)
                store(u, NQ - 2 + u)
                sp.wait_ge(y_stored[u], 16 * NQ)

        @block.gpsimd
        def _(p):
            xt = stu.xt[:, :, :].rearrange("d (t s) (b c q) -> d s b q c t", s=2, b=B, c=2)

            def stage(u, q):
                one = bass.ds(q, 1)
                for s in range(2):
                    for b in range(B):
                        dst = xs[:, u, s, b, :].rearrange("d (c t) -> d c t", c=2)
                        p.tensor_copy(dst, xt[:, s, b, one, :, :].rearrange("d q c t -> d (q c) t"))
                for b in range(B):
                    dst = xs[:, u, 2, b, :].rearrange("d (c t) -> d c t", c=2)
                    p.tensor_copy(dst[:, :, 1:64], xt[:, 1, b, one, :, 0:63].rearrange("d q c t -> d (q c) t"))
                xl = stu.xl[:, :].rearrange("d (b c q) -> d b c q", b=B, c=2)
                p.tensor_copy(xs[:, u, 2, :, :].rearrange("d b (c t) -> d b c t", c=2)[:, :, :, 0:1],
                              xl[:, :, :, one]).then_inc(xs_ready, 1)

            stage(0, 0)
            stage(1, 1)
            with p.Fori(0, NQ // 2 - 1) as i:
                for u in range(2):
                    p.wait_ge(proj_done, 2 * i + (u + 1))
                    stage(u, 2 * i + (u + 2))

        @block.tensor
        def _(pe):
            with pe.Fori(0, NQ // 2) as i:
                for u in range(2):
                    pe.wait_ge(xs_ready, 2 * i + (u + 1))
                    for c in range(NC + 1):
                        if c < NC:
                            for j in range(8):
                                pr, s, b = j // 4, j // 2 % 2, j % 2
                                n = 8 * c + j
                                if n >= 4:
                                    pe.wait_ge(copied[n % 2], (2 * i + u) * (UN // 2) + (n // 2 - 1))
                                m = stu.me if pr == 0 else stu.mo
                                kk = CH[c] - (c == NC - 1) * pr
                                mm = pe.matmul(psw[:, n % 4, 0:128 * kk], xs[:, u, source(pr, s), b, :],
                                               m[:, 4 * c:4 * c + kk, :], start=True, stop=True)
                                mm.then_inc(w_done, 1)
                                if n == UN - 1:
                                    pe.wait_ge(w_done, (2 * i + u) * UN + UN)
                                    pe.sem_inc(proj_done, 1)
                        if c == 1:
                            pe.wait_ge(tc_loaded[u], 32 * i + 32)
                            pe.wait_ge(y_copied, 2 * i + u)
                        if c > 0:
                            g = c - 1
                            for e in range(2):
                                pe.wait_ge(copied[e], (2 * i + u) * (UN // 2) + 4 * c)
                            for kk in range(CH[g]):
                                for pr in range(2):
                                    f = 2 * (4 * g + kk) + pr
                                    if f == NF - 1:
                                        continue
                                    mm = pe.matmul(psy[:, u, :], tc[:, u, f, :], w[:, (u * NC + g) % 2, kk, pr, :, :, :],
                                                   start=(f == 0), stop=(f == NF - 2))
                            mm.then_inc(filt_done, 1)
                    pe.wait_ge(filt_done, (2 * i + u) * NC + NC)
                    pe.sem_inc(q_done, 1)

        def copy_out(eng, put, mine, i):
            for u in range(2):
                for c in range(NC):
                    g = u * NC + c
                    eng.wait_ge(filt_done, i * (2 * NC) + max(g - 1, 0))
                    for j in range(mine, 8, 2):
                        pr, s, b = j // 4, j // 2 % 2, j % 2
                        n = 8 * c + j
                        kk = CH[c] - (c == NC - 1) * pr
                        eng.wait_ge(w_done, (2 * i + u) * UN + (n + 1))
                        put(w[:, g % 2, 0:kk, pr, s, b, :],
                            psw[:, n % 4, 0:128 * kk].rearrange("p (k e) -> p k e", e=128)).then_inc(copied[mine], 1)
                if mine == 1:
                    eng.wait_ge(q_done, 2 * i + (u + 1))
                    eng.wait_ge(y_stored[u], 32 * i)
                    eng.activation(y[:, u, :], psy[:, u, :], ACT.Copy).then_inc(y_copied, 1)

        @block.vector
        def _(v):
            with v.Fori(0, NQ // 2) as i:
                copy_out(v, v.tensor_copy, 0, i)

        @block.scalar
        def _(s):
            with s.Fori(0, NQ // 2) as i:
                copy_out(s, lambda o, x: s.activation(o, x, ACT.Copy), 1, i)


def stage_stu_output(k, stu):
    nc, a = k.nc, k.a
    with ExitStack() as ctx:
        sb = lambda name, shape: k.sb(name, shape, ctx=ctx)
        zq = sb("s10_zq", [128, 2, 16, HW])
        yn = sb("s10_yn", [64, 2, 16, HW])
        inv = sb("s10_inv", [128, 64])
        yg = sb("s10_yg", [128, 2, GROUP, HW])
        ps = k.ps("s10_ps", [64, 2, 16, HW], ctx)
        loaded, z_loaded = k.sem("s10_loaded"), [k.sem(f"s10_z{u}_loaded") for u in range(2)]
        done, copied, stored = k.sem("s10_done"), k.sem("s10_copied"), k.sem("s10_stored")
        y_loaded, added = [k.sem(f"s10_y{u}_loaded") for u in range(2)], k.sem("s10_added")
        block = ctx.enter_context(nc.Block())

        @block.sync
        def _(sp):
            sp.dma_start(inv[:, :], a["block_idft"]).then_inc(loaded, 16)
            with sp.Fori(0, 4) as i:
                for u in range(2):
                    sp.wait_ge(done, 2 * i)
                    for b in range(B):
                        for c in range(2):
                            sp.dma_start(zq[64 * b + 32 * c:64 * b + 32 * c + 32, u, :, :],
                                         sub(a["yh_d"], c * 32768 + b * 128 + (2 * i + u) * (8 * 512),
                                             [[65536, NQ], [256, 16], [1, 128]])).then_inc(z_loaded[u], 16)
            sp.wait_ge(stored, 16 * 8)
            with sp.Fori(0, 4) as i:
                for u in range(2):
                    sp.wait_ge(added, 2 * i)
                    sp.dma_start(yg[:, u, :, :],
                                 a["y_d"][bass.ds((2 * i + u) * GROUP, GROUP)].rearrange("i h w -> h i w"))\
                      .then_inc(y_loaded[u], 16)
            sp.wait_ge(added, 8)

        @block.tensor
        def _(pe):
            pe.wait_ge(loaded, 16)
            with pe.Fori(0, 4) as i:
                for u in range(2):
                    pe.wait_ge(z_loaded[u], 64 * i + 64)
                    pe.wait_ge(copied, 2 * i)
                    for j in range(0, 16, 4):
                        mm = pe.matmul(ps[:, u, j:j + 4, :], inv[:, :], zq[:, u, j:j + 4, :], start=True, stop=True)
                    mm.then_inc(done, 1)

        @block.scalar
        def _(s):
            with s.Fori(0, 4) as i:
                for u in range(2):
                    s.wait_ge(done, 2 * i + (u + 1))
                    s.wait_ge(stored, 32 * i)
                    for j in range(8):
                        ins = s.activation(yn[:, u, 14 - 2 * j:16 - 2 * j, :], ps[:, u, 2 * j:2 * j + 2, :], ACT.Copy)
                    ins.then_inc(copied, 1)
                    s.wait_ge(copied, 2 * i + (u + 1))
                    s.dma_start(sub(a["y_d"], (112 - 16 * (2 * i + u)) * HW, [[PIX, NI], [HW, 16], [1, HW]]), yn[:, u, :, :])\
                     .then_inc(stored, 16)

        @block.vector
        def _(v):
            with v.Fori(0, 4) as i:
                for u in range(2):
                    v.wait_ge(y_loaded[u], 16 * i + 16)
                    for j in range(GROUP):
                        o = bass.ds((2 * i + u) * GROUP + j, 1)
                        ins = v.scalar_tensor_tensor(out=k.x[:, o, :], in0=yg[:, u, j, :], scalar=stu.mask[:, o],
                                                     in1=k.x[:, o, :], op0=ALU.mult, op1=ALU.add)
                    ins.then_inc(added, 1)


class Stu:

    def __init__(self, k, ctx):
        self.mask = k.sb("stu_mask", [128, NI], ctx=ctx)
        self.me = k.sb("stu_me", [128, NK, 128], ctx=ctx)
        self.mo = k.sb("stu_mo", [128, NK - 1, 128], ctx=ctx)

    def spectrum(self, k, ctx):
        self.xt = k.sb("stu_xt", [128, HW, 128], ctx=ctx)
        self.xl = k.sb("stu_xl", [128, 128], ctx=ctx)


def v_row_norm(v, link, x, st, mean, var, rstd, root, tmp, eps, var_ready, root_ready):
    with v.Fori(0, NI) as i:
        v.bn_stats(st[:, bass.ds(i, 1), :], x[:, bass.ds(i, 1), :])
    link(v.memset(tmp, 0.0))
    row_stats(v, link, st, mean, var, tmp)
    link(v.tensor_scalar(tmp, var, eps, None, ALU.add))
    v.tensor_copy(var, tmp).then_inc(var_ready, 1)
    v.wait_ge(var_ready, 1)
    newton_rsqrt(v, link, var, root, rstd, tmp, root_ready, 1)


WU = 13
PADW = HW + 6
GAIN = float(np.sqrt(2.0))


def stage_resample_conv(k):
    nc, a = k.nc, k.a
    with ExitStack() as ctx:
        sb = lambda name, shape: k.sb(name, shape, ctx=ctx)
        st = sb("s11_st", [128, NI, 6])
        mean, var, rstd, root, tmp, bias = (sb(f"s11_{n}", [128, NI]) for n in ("mean", "var", "rstd", "root", "tmp", "bias"))
        v_in = sb("s11_v", [128, NI, PADW])
        mid = sb("s11_mid", [128, 2, 2, 2, 4, PADW])
        up_f, dn_f = sb("s11_upf", [TAPS, TAPS]), sb("s11_dnf", [TAPS, TAPS])
        sel = sb("s11_sel", [TAPS, WU])
        pu, pd = sb("s11_pu", [TAPS, 512]), sb("s11_pd", [TAPS, 512])
        upc = sb("s11_upc", [TAPS, WU])
        gu, gd = sb("s11_gu", [WU, 512]), sb("s11_gd", [TAPS, 512])
        bu, bd = sb("s11_bu", [128, 2 * WU, 128]), sb("s11_bd", [128, 2 * TAPS, 128])
        ps_m = k.ps("s11_psm", [128, 4, 512], ctx)
        ps_z = k.ps("s11_psz", [128, 2, 512], ctx)
        loaded, taps_done, taps_copied = k.sem("s11_loaded"), k.sem("s11_taps_done"), k.sem("s11_taps_copied")
        bands_stored, bands_loaded = k.sem("s11_bands_stored"), k.sem("s11_bands_loaded")
        chain, var_ready, root_ready = k.sem("s11_chain"), k.sem("s11_var_ready"), k.sem("s11_root_ready")
        v_ready, padded = k.sem("s11_v_ready"), k.sem("s11_padded")
        mid_ready = k.sem("s11_mid_ready")
        mid_done, mid_copied = k.sem("s11_mid_done"), k.sem("s11_mid_copied")
        z_done, z_added = k.sem("s11_z_done"), k.sem("s11_z_added")
        block = ctx.enter_context(nc.Block())

        @block.sync
        def _(sp):
            for t, n in ((up_f, "up_t"), (dn_f, "dn"), (sel, "up_sel"), (pu, "up_pos"), (pd, "dn_pos")):
                sp.dma_start(t[:, :], a[n]).then_inc(loaded, 16)
            sp.dma_start(bias[:, :], sub(a["bias"], 0, [[0, 128], [1, NI]])).then_inc(loaded, 16)
            sp.wait_ge(taps_copied, 3)
            sp.dma_start(a["gu_d"], gu[:, :]).then_inc(bands_stored, 16)
            sp.dma_start(a["gd_d"], gd[:, :]).then_inc(bands_stored, 16)
            sp.wait_ge(bands_stored, 32)
            sp.dma_start(bu[:, :, :], sub(a["gu_d"], 0, [[1, 128], [256, 2 * WU], [1, 128]])).then_inc(bands_loaded, 16)
            sp.dma_start(bd[:, :, :], sub(a["gd_d"], 0, [[1, 128], [256, 2 * TAPS], [1, 128]])).then_inc(bands_loaded, 16)
            sp.wait_ge(bands_loaded, 32)

        @block.gpsimd
        def _(p):
            p.memset(v_in[:, :, :], 0.0).then_inc(padded, 1)
            p.memset(mid[:, :, :, :, :, :], 0.0).then_inc(padded, 1)

        @block.vector
        def _(v):
            link = Chain(v, chain)
            v_row_norm(v, link, k.x, st, mean[:, :], var[:, :], rstd[:, :], root[:, :], tmp[:, :], 1e-6, var_ready, root_ready)
            v.wait_ge(loaded, 96)
            link(v.tensor_tensor(tmp[:, :], mean[:, :], rstd[:, :], ALU.mult))
            link(v.tensor_tensor(bias[:, :], bias[:, :], tmp[:, :], ALU.subtract))
            v.wait_ge(padded, 1)
            with v.Fori(0, NI) as i:
                o = bass.ds(i, 1)
                v.tensor_scalar(v_in[:, o, 3:3 + HW], k.x[:, o, :], rstd[:, o], bias[:, o], ALU.mult, ALU.add)\
                 .then_inc(v_ready, 1)
            with v.Fori(0, 8) as i:
                for u in range(2):
                    for pq in range(4):
                        v.wait_ge(mid_copied, 8 * i + (4 * u + pq + 1))
                        y = mid[:, u, pq // 2, pq % 2, :, 3:3 + HW]
                        v.scalar_tensor_tensor(out=y, in0=y, scalar=0.2, in1=y, op0=ALU.mult, op1=ALU.max)\
                         .then_inc(mid_ready, 1)
                for u in range(2):
                    v.wait_ge(z_done, 2 * i + (u + 1))
                    xg = k.x[:, bass.ds((2 * i + u) * 4, 4), :]
                    v.tensor_tensor(xg, ps_z[:, u, :].rearrange("p (i w) -> p i w", w=HW), xg, ALU.add).then_inc(z_added, 1)

        @block.scalar
        def _(s):
            s.wait_ge(taps_done, 1)
            s.activation(upc[:, :], ps_m[0:TAPS, 0, 0:WU], ACT.Copy).then_inc(taps_copied, 1)
            s.wait_ge(taps_done, 3)
            s.activation(gu[:, :], ps_m[0:WU, 1, :], ACT.Copy).then_inc(taps_copied, 1)
            s.activation(gd[:, :], ps_m[0:TAPS, 2, :], ACT.Copy).then_inc(taps_copied, 1)
            s.wait_ge(var_ready, 1)
            s.activation(root[:, :], var[:, :], ACT.Sqrt).then_inc(root_ready, 1)
            s.wait_ge(padded, 2)
            with s.Fori(0, 8) as i:
                s.wait_ge(z_done, 2 * i)
                for u in range(2):
                    for pq in range(4):
                        s.wait_ge(mid_done, 8 * i + (4 * u + pq + 1))
                        s.activation(mid[:, u, pq // 2, pq % 2, :, 3:3 + HW],
                                     ps_m[:, pq, :].rearrange("p (i w) -> p i w", w=HW), ACT.Copy,
                                     scale=GAIN).then_inc(mid_copied, 1)

        @block.tensor
        def _(pe):
            pe.wait_ge(loaded, 96)
            pe.matmul(ps_m[0:TAPS, 0, 0:WU], up_f[:, :], sel[:, :], start=True, stop=True).then_inc(taps_done, 1)
            pe.matmul(ps_m[0:TAPS, 2, :], dn_f[:, :], pd[:, :], start=True, stop=True).then_inc(taps_done, 1)
            pe.wait_ge(taps_copied, 1)
            pe.matmul(ps_m[0:WU, 1, :], upc[:, :], pu[:, :], start=True, stop=True).then_inc(taps_done, 1)
            pe.wait_ge(taps_copied, 3)
            pe.wait_ge(bands_loaded, 32)
            with pe.Fori(0, 8) as i:
                for u in range(2):
                    pe.wait_ge(v_ready, 8 * i + (4 * u + 4))
                    four = bass.ds((2 * i + u) * 4, 4)
                    for pq in range(4):
                        p, q = pq // 2, pq % 2
                        pe.wait_ge(mid_copied, 8 * i + (4 * u - 4 + pq + 1) if u else 8 * i)
                        shifts = list(range(-3, 4)) if q == 0 else list(range(-2, 4))
                        for n, dc in enumerate(shifts):
                            mm = pe.matmul(ps_m[:, pq, :], bu[:, 2 * (7 * q + n) + p, :],
                                           v_in[:, four, 3 + dc:3 + dc + HW], start=(n == 0), stop=(n == len(shifts) - 1))
                        mm.then_inc(mid_done, 1)
                for u in range(2):
                    pe.wait_ge(mid_ready, 8 * i + (4 * u + 4))
                    pe.wait_ge(z_added, 2 * i)
                    for n in range(2 * TAPS):
                        j, p = n // 2, n % 2
                        q = 0 if j % 2 else 1
                        dc = (j - 5 - q) // 2
                        mm = pe.matmul(ps_z[:, u, :], bd[:, n, :], mid[:, u, p, q, :, 3 + dc:3 + dc + HW],
                                       start=(n == 0), stop=(n == 2 * TAPS - 1))
                    mm.then_inc(z_done, 1)


def stage_experts(k):
    nc, a = k.nc, k.a
    with ExitStack() as ctx:
        sb = lambda name, shape: k.sb(name, shape, ctx=ctx)
        G = GROUP
        st = sb("s12_st", [128, NI, 6])
        mean, var, rstd, root, tmp = (sb(f"s12_{n}", [128, NI]) for n in ("mean", "var", "rstd", "root", "tmp"))
        tn, tt_ = sb("s12_tn", [128, G, HW]), sb("s12_tt", [128, G, HW])
        we = sb("s12_we", [128, EXP * 128])
        wr = sb("s12_wr", [128, EXP])
        rb, order = sb("s12_rb", [128, EXP]), sb("s12_order", [128, EXP])
        eb = sb("s12_eb", [G * EXP, G * 128])
        lg, ex, eq, oh = (sb(f"s12_{n}", [128, G, EXP]) for n in ("lg", "ex", "eq", "oh"))
        gates_sb = sb("s12_gates_sb", [128, 2 * G, EXP])
        g1 = gates_sb[:, 0:G, :]
        m0, m1, m2, r0 = (sb(f"s12_{n}", [128, G]) for n in ("m0", "m1", "m2", "r0"))
        gt = sb("s12_gt", [G * EXP, 128])
        ps_t = k.ps("s12_pst", [128, G, 128], ctx)
        ps_l = k.ps("s12_psl", [128, 512], ctx)
        ps_e = k.ps("s12_pse", [128, 2, EXP, 128], ctx)
        loaded, chain, loop = k.sem("s12_loaded"), k.sem("s12_chain"), k.sem("s12_loop")
        var_ready, root_ready = k.sem("s12_var_ready"), k.sem("s12_root_ready")
        tn_ready, turned, tt_ready, logits = k.sem("s12_tn_ready"), k.sem("s12_turned"), k.sem("s12_tt_ready"), k.sem("s12_logits")
        exp_in, exp_done, gates, gt_done = k.sem("s12_exp_in"), k.sem("s12_exp_done"), k.sem("s12_gates"), k.sem("s12_gt_done")
        gt_copied, base, exp_ready = k.sem("s12_gt_copied"), k.sem("s12_base"), k.sem("s12_exp_ready")
        used, based, out_stored = k.sem("s12_used"), k.sem("s12_based"), k.sem("s12_out_stored")
        block = ctx.enter_context(nc.Block())
        STEPS = 21

        @block.sync
        def _(sp):
            sp.dma_start(we[:, :].rearrange("d (e c) -> d e c", c=128), a["expert_w"].rearrange("e d c -> d e c")).then_inc(loaded, 16)
            sp.dma_start(wr[:, :], a["router_w"]).then_inc(loaded, 16)
            sp.dma_start(rb[:, :], sub(a["router_b"], 0, [[0, 128], [1, EXP]])).then_inc(loaded, 16)
            sp.dma_start(order[:, :], sub(a["order"], 0, [[0, 128], [1, EXP]])).then_inc(loaded, 16)
            sp.dma_start(eb[:, :], a["expert_b"]).then_inc(loaded, 16)
            with sp.Fori(0, NG) as g:
                sp.wait_ge(used, G * EXP * g + G * EXP)
                sp.dma_start(a["out"][bass.ds(g * G, G)].rearrange("i h w -> h i w"), k.x[:, bass.ds(g * G, G), :])\
                  .then_inc(out_stored, 16)
            sp.wait_ge(out_stored, 16 * NG)

        @block.vector
        def _(v):
            link = Chain(v, chain)
            v_row_norm(v, link, k.x, st, mean[:, :], var[:, :], rstd[:, :], root[:, :], tmp[:, :], 1e-5, var_ready, root_ready)
            v.wait_ge(loaded, 80)
            link(v.memset(gates_sb[:, :, :], 0.0))
            with v.Fori(0, NG) as g:
                step = [0]

                def link_g(ins):
                    step[0] += 1
                    ins.then_inc(loop, 1)
                    v.wait_ge(loop, g * STEPS + step[0])

                tt = lambda o, x, y, op: link_g(v.tensor_tensor(o, x, y, op))
                wide = lambda t: t.unsqueeze(2).broadcast_to([128, G, EXP])
                v.wait_ge(turned, g)
                for i in range(G):
                    o = bass.ds(g * G + i, 1)
                    ins = v.tensor_scalar(tn[:, i, :], k.x[:, o, :], mean[:, o], rstd[:, o], ALU.subtract, ALU.mult)
                ins.then_inc(tn_ready, 1)
                v.wait_ge(logits, g + 1)
                tt(lg[:, :, :], ps_l[:, 0:G * EXP].rearrange("p (i e) -> p i e", e=EXP),
                   rb[:, :].unsqueeze(1).broadcast_to([128, G, EXP]), ALU.add)
                link_g(v.tensor_reduce(m0[:, :], lg[:, :, :], AX.X, ALU.max))
                v.tensor_tensor(lg[:, :, :], lg[:, :, :], wide(m0[:, :]), ALU.subtract).then_inc(exp_in, 1)
                v.wait_ge(exp_done, g + 1)
                link_g(v.tensor_reduce(m0[:, :], ex[:, :, :], AX.X, ALU.add))
                link_g(v.reciprocal(r0[:, :], m0[:, :]))
                tt(ex[:, :, :], ex[:, :, :], wide(r0[:, :]), ALU.mult)
                for n, m in enumerate((m1, m2)):
                    link_g(v.tensor_reduce(m[:, :], ex[:, :, :], AX.X, ALU.max))
                    tt(eq[:, :, :], ex[:, :, :], wide(m[:, :]), ALU.is_equal)
                    tt(eq[:, :, :], eq[:, :, :], order[:, :].unsqueeze(1).broadcast_to([128, G, EXP]), ALU.mult)
                    link_g(v.tensor_reduce(r0[:, :], eq[:, :, :], AX.X, ALU.max))
                    tt(oh[:, :, :], eq[:, :, :], wide(r0[:, :]), ALU.is_equal)
                    if n == 0:
                        tt(g1[:, :, :], oh[:, :, :], wide(m[:, :]), ALU.mult)
                        link_g(v.scalar_tensor_tensor(out=ex[:, :, :], in0=oh[:, :, :], scalar=-2.0, in1=ex[:, :, :],
                                                      op0=ALU.mult, op1=ALU.add))
                    else:
                        tt(oh[:, :, :], oh[:, :, :], wide(m[:, :]), ALU.mult)
                tt(m1[:, :], m1[:, :], m2[:, :], ALU.add)
                link_g(v.reciprocal(r0[:, :], m1[:, :]))
                v.tensor_tensor(g1[:, :, :], g1[:, :, :], oh[:, :, :], ALU.add).then_inc(loop, 1)
                v.wait_ge(loop, g * STEPS + STEPS)
                v.tensor_tensor(g1[:, :, :], g1[:, :, :], wide(r0[:, :]), ALU.mult).then_inc(gates, 1)
                assert step[0] == STEPS - 1, step[0]
                v.wait_ge(base, g + 1)
                for i in range(0, G, 4):
                    xg = k.x[:, bass.ds(g * G + i, 4), :]
                    v.tensor_tensor(xg, ps_t[:, i:i + 4, :], xg, ALU.add).then_inc(based, 1)
                v.wait_ge(based, 2 * g + 2)
                v.wait_ge(gates, g + 1)
                for i in range(0, G, 2):
                    for u in range(2):
                        v.wait_ge(exp_ready, g * G + (i + u + 1))
                    for e in range(EXP):
                        for u in range(2):
                            n = EXP * i + 2 * e + u + 1
                            if e:
                                v.wait_ge(used, g * (G * EXP) + (n - 2))
                            xi = k.x[:, bass.ds(g * G + i + u, 1), :]
                            v.scalar_tensor_tensor(out=xi, in0=ps_e[:, u, e, :], scalar=g1[:, i + u, e:e + 1], in1=xi,
                                                   op0=ALU.mult, op1=ALU.add).then_inc(used, 1)

        @block.scalar
        def _(s):
            s.wait_ge(var_ready, 1)
            s.activation(root[:, :], var[:, :], ACT.Sqrt).then_inc(root_ready, 1)
            with s.Fori(0, NG) as g:
                s.wait_ge(turned, g + 1)
                s.wait_ge(exp_ready, g * G)
                for i in range(0, G, 4):
                    ins = s.activation(tt_[:, i:i + 4, :], ps_t[:, i:i + 4, :], ACT.Copy)
                ins.then_inc(tt_ready, 1)
                s.wait_ge(exp_in, g + 1)
                s.activation(ex[:, :, :], lg[:, :, :], ACT.Exp).then_inc(exp_done, 1)
                s.wait_ge(gt_done, g + 1)
                s.activation(gt[:, :], ps_l[0:G * EXP, 128:256], ACT.Copy).then_inc(gt_copied, 1)

        @block.tensor
        def _(pe):
            pe.wait_ge(loaded, 80)
            with pe.Fori(0, NG) as g:
                pe.wait_ge(tn_ready, g + 1)
                pe.wait_ge(based, 2 * g)
                for i in range(G):
                    mm = pe.transpose(ps_t[:, i, :], tn[:, i, :], k.ident[:, :])
                mm.then_inc(turned, 1)
                pe.wait_ge(tt_ready, g + 1)
                pe.wait_ge(gt_copied, g)
                for i in range(G):
                    mm = pe.matmul(ps_l[:, EXP * i:EXP * i + EXP], tt_[:, i, :], wr[:, :], start=True, stop=True)
                mm.then_inc(logits, 1)
                pe.wait_ge(gates, g + 1)
                pe.transpose(ps_l[:, 128:256], gates_sb[:, :, :].rearrange("p i e -> p (i e)"), k.ident[:, :]).then_inc(gt_done, 1)
                pe.wait_ge(gt_copied, g + 1)
                for i in range(0, G, 4):
                    mm = pe.matmul(ps_t[:, i:i + 4, :], gt[:, :], eb[:, 128 * i:128 * i + 512], start=True, stop=True)
                mm.then_inc(base, 1)
                for i in range(0, G):
                    pe.wait_ge(used, g * (G * EXP) + EXP * (i - i % 2))
                    for h in range(2):
                        mm = pe.matmul(ps_e[:, i % 2, 4 * h:4 * h + 4, :], tt_[:, i, :], we[:, 512 * h:512 * h + 512],
                                       start=True, stop=True)
                    mm.then_inc(exp_ready, 1)


def low_modes(w):
    w = np.concatenate([w[0, 0], w[1, 0]], 1)
    rev = np.zeros_like(w)
    rev[:, 1:LM // 2, 0] = w[:, :LM // 2:-1, 0]
    rev[:, LM // 2 + 1:, 0] = w[:, LM // 2 - 1:0:-1, 0]
    rev[:, 0, 0] = w[:, 0, 0]
    parts = [x[..., c].transpose(2, 1, 0).reshape(64, 256) for x in (w, rev) for c in range(2)]
    one = np.stack(parts, 1)
    return np.concatenate([one, one], 0)


def full_modes(w):
    full = np.zeros((HEADS, NM, NN, 2), w.dtype)
    full[:, :LM // 2, :LN] = w[0, 0]
    full[:, NM - LM // 2:, :LN] = w[1, 0]
    rev = np.zeros_like(full)
    idx = (-np.arange(NM)) % NM
    keep = np.arange(NM) != NM // 2
    rev[:, keep, 0] = full[:, idx[keep], 0]
    parts = [x[..., c].transpose(0, 2, 1).reshape(128, 512) for x in (full, rev) for c in range(2)]
    return np.stack(parts, 1)


def layout(inputs):
    r = {}
    g = {n: np.asarray(v) for n, v in inputs.items()}
    r["x"] = g["x"].reshape(NI, HW, HW)
    c = "L0_conv_"
    r["norm_g"], r["norm_b"] = g[c + "norm_g"], g[c + "norm_b"]
    for n in "KQ":
        r["w" + n] = low_modes(g[c + "w" + n])
    for n in "KQV":
        r[f"w{n}s"] = g[f"{c}w{n}s"].reshape(HEADS)
        r[f"b{n}s"] = g[f"{c}b{n}s"]
    r["wV"] = full_modes(g[c + "wV"])
    wp = np.concatenate([g[c + "wP"][0, :, 0], g[c + "wP"][1, :, 0]], 1)
    r["wP"] = np.stack([wp[..., j].transpose(0, 2, 1).reshape(128, 512) for j in range(2)], 1)
    r["wP00"] = wp[:, 0, 0, 0]
    r["wPs"] = g[c + "wPs"].reshape(HEADS)
    r["bPs"] = g[c + "bPs"]
    for n in ("M0", "M1"):
        w = np.concatenate([g[f"{c}w{n}"][0, 0, 0], g[f"{c}w{n}"][1, 0, 0]], 0).transpose(1, 0, 2)
        r["w" + n] = np.stack([np.concatenate([w[..., j]] * 2, 0) for j in range(2)], 1)
        r[f"w{n}s"] = g[f"{c}w{n}s"].reshape(1)
        r[f"b{n}s"] = g[f"{c}b{n}s"]
    f = "L0_ffn_"
    for n in ("sigma", "log_weights", "gumbel", "M_u", "M_phi_plus", "M_phi_minus"):
        r[n] = g[f + n]
    at = HB * np.arange(NQ + 1)[:, None] + (HB - 1) - np.arange(128)[None]
    inside = (at >= 0) & (at < PIX // 8)
    phi = np.zeros((NQ + 1, NF, 128), np.float32)
    for p in range(2):
        phi[:, p:2 * FT:2] = np.where(inside[..., None], g[f + "phi"][p::2][np.where(inside, at, 0)], 0).transpose(0, 2, 1)
    phi[:, 2 * FT] = phi[:, 2 * FT + 1] = at == 0
    phi[:, 2 * FT + 2] = at == 1
    r["phi"] = phi
    r["bias"] = np.tile(g["L1_conv_bias"].reshape(T), B)
    r["up_t"], r["dn"] = g["L1_conv_up_filter"][0, 0].T, g["L1_conv_dn_filter"][0, 0]
    for n in ("router_w", "router_b", "expert_w"):
        r[n] = g["L1_ffn_" + n]
    eb = np.zeros((GROUP, EXP, GROUP, 128), np.float32)
    eb[np.arange(GROUP), :, np.arange(GROUP)] = g["L1_ffn_expert_b"]
    r["expert_b"] = eb.reshape(GROUP * EXP, GROUP * 128)
    r.update(tables())
    return {n: np.ascontiguousarray(v) for n, v in r.items()}


SCRATCH = {
    "u_d": (NI, HW, HW), "tc_d": (NQ, 2, NF, 128, 2), "yh_d": (NQ, 2, 64, 512), "y_d": (NI, HW, HW),
    "gu_d": (13, 512), "gd_d": (TAPS, 512),
    "xn_d": (NI, HW, HW), "xf_d": (NI, 2, NN, NM), "xl_d": (2 * LN, LM, NI),
    "d_d": (HEADS, 2, NN, NM), "z_d": (NI, 2, NN, NM), "sk_d": (NI, HW, HW),
}


def program(nc, a):
    with ExitStack() as ctx:
        k = Core(nc, ctx, a)
        with ExitStack() as conv:
            k.image_buffer(conv)
            with ExitStack() as attn:
                att = Attention(k, attn)
                stage_spectrum(k, att)
                stage_attention(k, att)
                stage_value_tables(k)
                stage_mix(k, att)
                stage_project(k, att)
            stage_mixer(k)
        with ExitStack() as ffn:
            stu = Stu(k, ffn)
            stage_stu_setup(k, stu)
            with ExitStack() as spec:
                stu.spectrum(k, spec)
                stage_stu_blocks(k, stu)
                stage_stu_filter(k, stu)
            stage_stu_output(k, stu)
        stage_resample_conv(k)
        stage_experts(k)


def kernel(**inputs):
    import concourse.bacc as bacc
    from concourse.bass_utils import run_bass_kernel_spmd

    nc = bacc.Bacc("TRN2", target_bir_lowering=False, num_devices=1)
    arrays, a = {}, {}
    for name, v in layout(inputs).items():
        arrays[f"in_{name}"] = v
        a[name] = nc.dram_tensor(f"in_{name}", v.shape, mybir.dt.from_np(v.dtype), kind="ExternalInput").ap()
    for name, shape in SCRATCH.items():
        a[name] = nc.dram_tensor(name, shape, F32, kind="Internal").ap()
    a["out"] = nc.dram_tensor("out_x", (NI, HW, HW), F32, kind="ExternalOutput").ap()
    program(nc, a)
    r = run_bass_kernel_spmd(nc, [arrays], core_ids=[0])
    return r.results[0]["out_x"].reshape(B, T, HW, HW)
```

```python
from contextlib import ExitStack

import concourse.bass as bass
import numpy as np
from concourse import mybir

F32 = mybir.dt.float32
F32R = mybir.dt.float32r
ALU = mybir.AluOpType
ACT = mybir.ActivationFunctionType
AX = mybir.AxisListType

B, T, HW = 2, 32, 128
NI = B * T
GROUP = 8
NG = NI // GROUP
HEADS = 32
NM, NN = 64, 32
LM, LN = 32, 16
DS = 64
PIX = HW * HW
FT = 16
HB = 64
NQ = 32
TAPS = 12
EXP = 8


def tables():
    t = {}
    h = np.arange(HW)
    m = np.concatenate([np.arange(NM // 2), np.arange(-NM // 2, 0)])
    n = np.arange(NN)
    ang = 2 * np.pi * np.outer(h, m) / HW
    rows = [np.cos(ang), -np.sin(ang)]
    hd = np.arange(DS)
    rel = hd[None, :, None] / DS - h[:, None, None] / HW
    a1 = np.cos(2 * np.pi * rel * m).sum(-1) / HW
    a2 = np.sin(2 * np.pi * rel * m).sum(-1) / HW
    nn = np.arange(DS // 2 + 1)
    wt = np.where((nn == 0) | (nn == DS // 2), 1.0, 2.0)
    b1 = (wt * np.cos(2 * np.pi * rel * nn)).sum(-1) / HW
    b2 = (wt * np.sin(2 * np.pi * rel * nn)).sum(-1) / HW
    t["dft_rows"] = np.concatenate(rows + [a1, a2], 1)
    an = 2 * np.pi * np.outer(h, n) / HW
    c, s = np.cos(an) / PIX, np.sin(an) / PIX
    t["dft_cols"] = np.concatenate([c, -s, s, c, s, c, -c, s], 1)
    t["down_cols"] = np.concatenate([b1, -b2], 1)
    w2 = np.where(n == 0, 1.0, 2.0)[:, None]
    ca, sa = w2 * np.cos(an.T), w2 * np.sin(an.T)
    t["idft_cols"] = np.concatenate([ca, -sa], 0)
    t["idft_rows"] = np.concatenate([np.cos(ang.T), -np.sin(ang.T)], 0)
    ml = np.concatenate([np.arange(LM // 2), np.arange(-LM // 2, 0)])
    w = np.where(np.arange(LN)[:, None] == 0, 1.0, 2.0) * np.ones((1, LM))
    w[0, ml == -LM // 2] = 2.0
    w *= 64.0
    w = np.tile(w.reshape(LN * 4, LM // 4), (2, 1))
    t["parseval"] = np.repeat(w[:, :, None], HEADS, 2).reshape(128, 256)
    n0 = np.zeros((2, LN, 4, LM // 4, HEADS))
    n0[:, 0] = 1.0
    n0 = n0.reshape(128, 256)
    t["herm_low"] = np.concatenate([1 - 0.5 * n0, 0.5 * n0], 1)
    t["im_sign"] = np.concatenate([np.ones((64, 1)), -np.ones((64, 1))], 0)
    f0 = np.zeros((HEADS, NN, NM))
    f0[:, 0] = 1.0
    f0 = f0.reshape(128, 512)
    t["herm_full"] = np.concatenate([1 - 0.5 * f0, 0.5 * f0], 1)
    t["identity"] = np.eye(128)
    q, j = np.arange(NQ), np.arange(NQ + 1)
    aj = 2 * np.pi * np.outer(j, q) / (2 * NQ)
    re, im, re_b = np.cos(aj), -np.sin(aj), np.cos(aj)
    re_b[:, 0] = (-1.0) ** j
    t["filter_dft"] = np.concatenate([re, im, -im, re_b], 1)
    im_p = im.copy()
    im_p[:, 0] = (-1.0) ** j
    both = np.stack([re, im_p], 1).reshape(NQ + 1, 2 * NQ)
    t["block_dft"] = np.concatenate([np.kron(np.eye(B), both[:NQ]), np.kron(np.eye(B), both[1:])], 1)
    wt = np.where(q == 0, 1.0, 2.0)[:, None] / (2 * NQ)
    inv = np.concatenate([wt * re[:NQ].T, wt * im_p[:NQ].T], 0)
    t["block_idft"] = np.kron(np.eye(B), inv)
    t["masks"] = np.stack([(np.arange(NI) % T < T // f) for f in (1, 2, 4, 8)]).astype(float)
    i = np.arange(TAPS)
    sel = np.zeros((TAPS, 13))
    for q in range(2):
        sel[i, 7 * q + (q + i - 5) // 2 + (3 if q == 0 else 2)] = 1.0
    t["up_sel"] = sel
    pu, pd = np.zeros((TAPS, 2, 256)), np.zeros((TAPS, 2, 256))
    for p in range(2):
        pu[i, p, HW - 1 + (p + i - 5) // 2] = 1.0
        j = i[(i + 1) % 2 == p]
        pd[j, p, HW - 1 - (j - 5 - p) // 2] = 1.0
    t["up_pos"], t["dn_pos"] = pu.reshape(TAPS, 512), pd.reshape(TAPS, 512)
    t["order"] = EXP - np.arange(EXP)
    return {k: np.ascontiguousarray(v, np.float32) for k, v in t.items()}


class Chain:

    def __init__(self, eng, sem):
        self.eng, self.sem, self.n = eng, sem, 0

    def __call__(self, ins):
        self.n += 1
        ins.then_inc(self.sem, 1)
        self.eng.wait_ge(self.sem, self.n)


def sub(ap, offset, dims):
    return bass.AP(ap.tensor, offset, dims)


def row_stats(v, link, st, mean, var, tmp):
    link(v.tensor_tensor(tmp, st[:, :, 1], st[:, :, 4], ALU.subtract))
    link(v.tensor_tensor(mean, st[:, :, 1], st[:, :, 4], ALU.add))
    link(v.tensor_tensor(var, st[:, :, 2], st[:, :, 5], ALU.add))
    link(v.tensor_tensor(tmp, tmp, tmp, ALU.mult))
    link(v.tensor_scalar(var, var, 1.0 / HW, None, ALU.mult))
    link(v.scalar_tensor_tensor(out=var, in0=tmp, scalar=0.25, in1=var, op0=ALU.mult, op1=ALU.add))
    link(v.tensor_scalar(mean, mean, 0.5, None, ALU.mult))


def newton_rsqrt(v, link, var, root, out, tmp, root_ready, n):
    v.wait_ge(root_ready, n)
    link(v.reciprocal(out, root))
    link(v.tensor_tensor(tmp, out, out, ALU.mult))
    link(v.tensor_tensor(tmp, tmp, var, ALU.mult))
    link(v.tensor_scalar(tmp, tmp, -0.5, 1.5, ALU.mult, ALU.add))
    link(v.tensor_tensor(out, out, tmp, ALU.mult))


class Core:

    def __init__(self, nc, ctx, a):
        self.nc, self.ctx, self.a = nc, ctx, a
        self.sems = []
        self.x = self.sb("acts", [HW, NI, HW])
        self.ones = self.sb("ones", [128, 128])
        self.ident = self.sb("ident", [128, 128])
        self.norm_g = self.sb("norm_g", [128, 6])
        self.norm_b = self.sb("norm_b", [128, 6])

    def image_buffer(self, ctx):
        self.xa = self.sb("xa", [HW, NI, HW], ctx=ctx)

    def sb(self, name, shape, dt=F32, ctx=None):
        return (ctx or self.ctx).enter_context(self.nc.sbuf_tensor(name, shape, dt))

    def ps(self, name, shape, ctx):
        return ctx.enter_context(self.nc.psum_tensor(name, shape, F32))

    def sem(self, name):
        self.sems.append(self.nc.alloc_semaphore(name))
        return self.sems[-1]

    def recycle_sems(self):
        self.nc.clear_and_free_semaphores(self.sems)
        self.nc.all_engine_barrier()
        self.sems = []


def stage_spectrum(k, att):
    nc, a = k.nc, k.a
    with ExitStack() as ctx:
        sb = lambda name, shape: k.sb(name, shape, ctx=ctx)
        x, xa = k.x, k.xa
        st = sb("s1_st", [128, NI, 6])
        mean, var, rstd, root, tmp, scale = (sb(f"s1_{n}", [128, NI]) for n in ("mean", "var", "rstd", "root", "tmp", "scale"))
        rows = sb("s1_rows", [128, 256])
        cols = sb("s1_cols", [128, 128])
        down = sb("s1_down", [128, 128])
        xn = sb("s1_xn", [128, GROUP, HW])
        yt = sb("s1_yt", [128, GROUP, 256])
        xfs = sb("s1_xf", [64, NI, NM])
        xls = sb("s1_xl", [64, LM, NI])
        xds = sb("s1_xd", [64, NI, DS])
        ps_a = k.ps("s1_psa", [128, GROUP, 256], ctx)
        ps_x = k.ps("s1_psx", [64, 512], ctx)
        ps_d = k.ps("s1_psd", [64, 512], ctx)
        ps_s = k.ps("s1_pss", [128, 512], ctx)
        loaded = k.sem("s1_loaded")
        chain = k.sem("s1_chain")
        ones_set = k.sem("s1_ones_set")
        var_ready, root_ready = k.sem("s1_var_ready"), k.sem("s1_root_ready")
        rowvar_ready, imgvar_ready = k.sem("s1_rowvar_ready"), k.sem("s1_imgvar_ready")
        xn_ready, xn_stored = k.sem("s1_xn_ready"), k.sem("s1_xn_stored")
        rows_done, yt_ready = k.sem("s1_rows_done"), k.sem("s1_yt_ready")
        spec_done, down_done = k.sem("s1_spec_done"), k.sem("s1_down_done")
        spec_copied, down_copied = k.sem("s1_spec_copied"), k.sem("s1_down_copied")
        gram_done, stored = k.sem("s1_gram_done"), k.sem("s1_stored")

        block = ctx.enter_context(nc.Block())

        @block.sync
        def _(sp):
            for q in range(4):
                sp.dma_start(x[:, 16 * q:16 * q + 16, :],
                             a["x"][16 * q:16 * q + 16].rearrange("i h w -> h i w")).then_inc(loaded, 16)
            sp.dma_start(rows[:, :], a["dft_rows"]).then_inc(loaded, 16)
            sp.dma_start(cols[:, :], a["dft_cols"][:, 0:128]).then_inc(loaded, 16)
            sp.dma_start(down[:, :], a["down_cols"]).then_inc(loaded, 16)
            sp.dma_start(k.ident[:, :], a["identity"]).then_inc(loaded, 16)
            sp.dma_start(k.norm_g[:, :], sub(a["norm_g"], 0, [[0, 128], [1, 6]])).then_inc(loaded, 16)
            sp.dma_start(k.norm_b[:, :], sub(a["norm_b"], 0, [[0, 128], [1, 6]])).then_inc(loaded, 16)
            with sp.Fori(0, NG) as g:
                sp.wait_ge(xn_ready, g + 1)
                sp.dma_start(a["xn_d"][bass.ds(g * GROUP, GROUP)].rearrange("i h w -> h i w"),
                             xn[:, :, :]).then_inc(xn_stored, 16)
            sp.wait_ge(xn_stored, 16 * NG)
            sp.wait_ge(spec_copied, NG)
            sp.dma_start(sub(a["xf_d"], 0, [[NM, 64], [64 * NM, NI], [1, NM]]), xfs[:, :, :]).then_inc(stored, 16)
            for c in range(2):
                sp.dma_start(a["xl_d"][c * LN:(c + 1) * LN], xls[c * NN:c * NN + LN, :, :]).then_inc(stored, 16)
            sp.wait_ge(stored, 48)

        @block.vector
        def _(v):
            link = Chain(v, chain)
            v.memset(k.ones[:, :], 1.0 / HW).then_inc(ones_set, 1)
            v.wait_ge(loaded, 160)
            with v.Fori(0, NI) as i:
                v.bn_stats(st[:, bass.ds(i, 1), :], x[:, bass.ds(i, 1), :])
            link(v.memset(tmp[:, :], 0.0))
            row_stats(v, link, st, mean[:, :], var[:, :], tmp[:, :])
            link(v.tensor_scalar(rstd[:, :], var[:, :], 1e-6, None, ALU.add))
            v.tensor_copy(scale[:, :], rstd[:, :]).then_inc(var_ready, 1)
            v.wait_ge(var_ready, 1)
            newton_rsqrt(v, link, scale[:, :], root[:, :], rstd[:, :], tmp[:, :], root_ready, 1)
            link(v.tensor_tensor(tmp[:, :], rstd[:, :], rstd[:, :], ALU.mult))
            v.tensor_tensor(var[:, :], var[:, :], tmp[:, :], ALU.mult).then_inc(rowvar_ready, 1)
            with v.Fori(0, NI) as i:
                v.tensor_scalar(xa[:, bass.ds(i, 1), :], x[:, bass.ds(i, 1), :], mean[:, bass.ds(i, 1)],
                                rstd[:, bass.ds(i, 1)], ALU.subtract, ALU.mult)
            v.wait_ge(imgvar_ready, 1)
            link(v.tensor_scalar(tmp[:, :], ps_s[:, 0:NI], 1e-5, None, ALU.add))
            v.tensor_copy(var[:, :], tmp[:, :]).then_inc(var_ready, 1)
            v.wait_ge(var_ready, 2)
            newton_rsqrt(v, link, var[:, :], root[:, :], scale[:, :], tmp[:, :], root_ready, 2)
            link(v.tensor_scalar(scale[:, :], scale[:, :], k.norm_g[:, 0:1], None, ALU.mult))
            with v.Fori(0, NG) as g:
                v.wait_ge(rows_done, g)
                v.wait_ge(xn_stored, g * 16)
                for i in range(GROUP):
                    ins = v.tensor_scalar(xn[:, i, :], xa[:, bass.ds(g * GROUP + i, 1), :],
                                          scale[:, bass.ds(g * GROUP + i, 1)], k.norm_b[:, 0:1], ALU.mult, ALU.add)
                ins.then_inc(xn_ready, 1)
                v.wait_ge(spec_done, g + 1)
                src = ps_x[:, :].rearrange("p (i m) -> p i m", m=NM)
                v.tensor_copy(xfs[:, bass.ds(g * GROUP, GROUP), :], src)
                dst = xls[:, :, bass.ds(g * GROUP, GROUP)].rearrange("p m i -> p i m")
                v.tensor_copy(dst[:, :, 0:16], src[:, :, 0:16])
                v.tensor_copy(dst[:, :, 16:32], src[:, :, 48:64]).then_inc(spec_copied, 1)
            v.wait_ge(gram_done, 1)
            for b in range(B):
                ins = v.tensor_copy(att.gram[T * b:T * b + T, :], ps_s[T * b:T * b + T, T * b:T * b + T])
            ins.then_inc(chain, 1)

        @block.scalar
        def _(s):
            s.wait_ge(var_ready, 1)
            s.activation(root[:, :], scale[:, :], ACT.Sqrt).then_inc(root_ready, 1)
            s.wait_ge(var_ready, 2)
            s.activation(root[:, :], var[:, :], ACT.Sqrt).then_inc(root_ready, 1)
            with s.Fori(0, NG) as g:
                s.wait_ge(rows_done, g + 1)
                s.wait_ge(down_done, g)
                for q in range(4):
                    ins = s.activation(yt[:, 2 * q:2 * q + 2, :], ps_a[:, 2 * q:2 * q + 2, :], ACT.Copy)
                ins.then_inc(yt_ready, 1)
                s.wait_ge(down_done, g + 1)
                s.activation(xds[:, bass.ds(g * GROUP, GROUP), :],
                             ps_d[:, :].rearrange("p (i m) -> p i m", m=DS), ACT.Copy).then_inc(down_copied, 1)

        @block.tensor
        def _(pe):
            pe.wait_ge(ones_set, 1)
            pe.wait_ge(rowvar_ready, 1)
            pe.matmul(ps_s[:, 0:NI], k.ones[:, :], var[:, :], start=True, stop=True).then_inc(imgvar_ready, 1)
            with pe.Fori(0, NG) as g:
                pe.wait_ge(xn_ready, g + 1)
                pe.wait_ge(yt_ready, g)
                for i in range(GROUP):
                    mm = pe.matmul(ps_a[:, i, :], xn[:, i, :], rows[:, :], start=True, stop=True)
                mm.then_inc(rows_done, 1)
                pe.wait_ge(yt_ready, g + 1)
                pe.wait_ge(spec_copied, g)
                pe.matmul(ps_x[:, :], cols[:, 0:64], yt[:, :, 0:64], start=True, stop=False)
                pe.matmul(ps_x[:, :], cols[:, 64:128], yt[:, :, 64:128], start=False, stop=True).then_inc(spec_done, 1)
                pe.wait_ge(down_copied, g)
                pe.matmul(ps_d[:, :], down[:, 0:64], yt[:, :, 128:192], start=True, stop=False)
                pe.matmul(ps_d[:, :], down[:, 64:128], yt[:, :, 192:256], start=False, stop=True).then_inc(down_done, 1)
            pe.wait_ge(down_copied, NG)
            pe.wait_ge(var_ready, 2)
            for r in range(DS):
                mm = pe.matmul(ps_s[0:64, 0:NI], xds[:, :, r], xds[:, :, r], start=(r == 0), stop=(r == DS - 1))
            mm.then_inc(gram_done, 1)


class Attention:

    def __init__(self, k, ctx):
        self.gram = k.sb("gram", [64, T], ctx=ctx)
        self.mix_t = k.sb("mix_t", [128, 128], ctx=ctx)
        self.prob_t = k.sb("prob_t", [128, HEADS // 4, B, T], ctx=ctx)
        self.dc = k.sb("dc", [1, 1], ctx=ctx)


def stage_attention(k, att):
    nc, a = k.nc, k.a
    with ExitStack() as ctx:
        sb = lambda name, shape: k.sb(name, shape, ctx=ctx)
        xl = sb("s2_xl", [128, 8, NI])
        xt = sb("s2_xt", [128, 8, NI])
        xw = sb("s2_xw", [128, 8, NI])
        herm = sb("s2_herm", [128, 2, 256])
        pars = sb("s2_pars", [128, 256])
        sign = sb("s2_sign", [128, 1])
        wk, wq = sb("s2_wk", [128, 4, 256]), sb("s2_wq", [128, 4, 256])
        skip = sb("s2_skip", [128, 4, HEADS])
        vec = sb("s2_vec", [128, 2, HEADS])
        cr, ci, t1, t2 = (sb(f"s2_{n}", [128, 256]) for n in ("cr", "ci", "t1", "t2"))
        kp = sb("s2_kp", [128, 8, HEADS, NI])
        kq = sb("s2_kq", [128, 4, HEADS, NI])
        sc = sb("s2_sc", [64, HEADS, T])
        sx = sb("s2_sx", [64, HEADS, T])
        mx, sm, rs = (sb(f"s2_{n}", [64, HEADS]) for n in ("mx", "sm", "rs"))
        qk = sb("s2_qk", [128, HEADS])
        mix = sb("s2_mix", [64, T])
        mixt = sb("s2_mixt", [64, T])
        pt = sb("s2_pt", [64, HEADS, T])
        dcv = sb("s2_dcv", [1, 3, HEADS])
        bp = sb("s2_bp", [1, 1])
        dct = sb("s2_dct", [1, HEADS])
        ps = k.ps("s2_ps", [64, HEADS, T], ctx)
        loaded, chain, fixed = k.sem("s2_loaded"), k.sem("s2_chain"), k.sem("s2_fixed")
        k_ready, scores_done = k.sem("s2_k_ready"), k.sem("s2_scores_done")
        shifted, exped, turned, moved = k.sem("s2_shifted"), k.sem("s2_exped"), k.sem("s2_turned"), k.sem("s2_moved")

        block = ctx.enter_context(nc.Block())

        @block.sync
        def _(sp):
            n = LN * 4 * 512
            src = sub(a["xl_d"], 0, [[512, 128], [NI, 8], [1, NI]])
            sp.dma_start(xl[:, :, :], src).then_inc(loaded, 16)
            sp.dma_start(xt[:, :, :], src).then_inc(loaded, 16)
            sp.dma_start(xw[0:64, :, :], sub(a["xl_d"], n, [[512, 64], [NI, 8], [1, NI]])).then_inc(loaded, 16)
            sp.dma_start(xw[64:128, :, :], sub(a["xl_d"], 0, [[512, 64], [NI, 8], [1, NI]])).then_inc(loaded, 16)
            sp.dma_start(herm[:, :, :], a["herm_low"].rearrange("p (u f) -> p u f", u=2)).then_inc(loaded, 16)
            sp.dma_start(pars[:, :], a["parseval"]).then_inc(loaded, 16)
            sp.dma_start(sign[:, :], a["im_sign"]).then_inc(loaded, 16)
            sp.dma_start(wk[:, :, :], a["wK"]).then_inc(loaded, 16)
            sp.dma_start(wq[:, :, :], a["wQ"]).then_inc(loaded, 16)
            for j, name in enumerate(("wQs", "wKs", "bQs", "bKs")):
                sp.dma_start(skip[:, j, :], sub(a[name], 0, [[0, 128], [1, HEADS]])).then_inc(loaded, 16)
            for j, name in enumerate(("wVs", "wPs")):
                sp.dma_start(vec[:, j, :], sub(a[name], 0, [[0, 128], [1, HEADS]])).then_inc(loaded, 16)
            sp.dma_start(dcv[:, 0, :], sub(a["bVs"], 0, [[0, 1], [1, HEADS]])).then_inc(loaded, 16)
            sp.dma_start(dcv[:, 1, :], sub(a["wPs"], 0, [[0, 1], [1, HEADS]])).then_inc(loaded, 16)
            sp.dma_start(dcv[:, 2, :], sub(a["wP00"], 0, [[0, 1], [1, HEADS]])).then_inc(loaded, 16)
            sp.dma_start(bp[:, :], sub(a["bPs"], 0, [[0, 1], [1, 1]])).then_inc(loaded, 16)
            sp.wait_ge(turned, 1)
            for b in range(B):
                for o in range(4):
                    sp.dma_start(att.prob_t[32 * o:32 * o + 32, :, b, :],
                                 pt[32 * b:32 * b + 32, o::4, :]).then_inc(moved, 16)
            sp.wait_ge(moved, 128)

        @block.vector
        def _(v):
            link = Chain(v, chain)
            tt = lambda o, x, y, op: link(v.tensor_tensor(o, x, y, op))
            v.wait_ge(loaded, 19 * 16)

            def head(j):
                return skip[:, j:j + 1, :].broadcast_to([128, 8, HEADS])

            r3 = lambda t: t.rearrange("p (m o) -> p m o", o=HEADS)
            for w in (wk, wq):
                tt(w[:, 0, :], w[:, 0, :], herm[:, 0, :], ALU.mult)
                tt(w[:, 1, :], w[:, 1, :], herm[:, 0, :], ALU.mult)
                tt(w[:, 2, :], w[:, 2, :], herm[:, 1, :], ALU.mult)
                tt(w[:, 3, :], w[:, 3, :], herm[:, 1, :], ALU.mult)
                tt(w[:, 0, :], w[:, 0, :], w[:, 2, :], ALU.add)
                tt(w[:, 1, :], w[:, 1, :], w[:, 3, :], ALU.subtract)
            kr, ki, qr, qi = wk[:, 0, :], wk[:, 1, :], wq[:, 0, :], wq[:, 1, :]
            tt(r3(cr[:, :]), r3(kr), head(0), ALU.mult)
            tt(r3(t1[:, :]), r3(qr), head(1), ALU.mult)
            tt(cr[:, :], cr[:, :], t1[:, :], ALU.add)
            tt(t1[:, :], qr, kr, ALU.mult)
            tt(cr[:, :], cr[:, :], t1[:, :], ALU.add)
            tt(t1[:, :], qi, ki, ALU.mult)
            tt(cr[:, :], cr[:, :], t1[:, :], ALU.add)
            tt(cr[:, :], cr[:, :], pars[:, :], ALU.mult)
            tt(r3(ci[:, :]), r3(qi), head(1), ALU.mult)
            tt(r3(t1[:, :]), r3(ki), head(0), ALU.mult)
            tt(ci[:, :], ci[:, :], t1[:, :], ALU.subtract)
            tt(t1[:, :], qi, kr, ALU.mult)
            tt(ci[:, :], ci[:, :], t1[:, :], ALU.add)
            tt(t1[:, :], qr, ki, ALU.mult)
            tt(ci[:, :], ci[:, :], t1[:, :], ALU.subtract)
            tt(ci[:, :], ci[:, :], pars[:, :], ALU.mult)
            link(v.tensor_scalar(ci[:, :], ci[:, :], sign[:, 0:1], None, ALU.mult))
            for half in range(2):
                m0 = 4 * half
                bx = lambda t: t[:, m0:m0 + 4, :].unsqueeze(2).broadcast_to([128, 4, HEADS, NI])
                bc = lambda t: r3(t[:, :])[:, m0:m0 + 4, :].unsqueeze(3).broadcast_to([128, 4, HEADS, NI])
                for m in range(4):
                    v.tensor_tensor(kp[:, m0 + m, :, :], bx(xl)[:, m], bc(cr)[:, m], ALU.mult)
                    v.tensor_tensor(kq[:, m, :, :], bx(xw)[:, m], bc(ci)[:, m], ALU.mult).then_inc(chain, 1)
                    link.n += 1
                v.wait_ge(chain, link.n)
                tt(kp[:, m0:m0 + 4, :, :], kp[:, m0:m0 + 4, :, :], kq[:, :, :, :], ALU.add)
            z = slice(0, 1)
            col = lambda t, p: r3(t)[p:p + 1, 0, :]
            tt(t1[z, 0:HEADS], col(qr, 0), skip[z, 0, :], ALU.add)
            tt(t1[z, 0:HEADS], t1[z, 0:HEADS], skip[z, 3, :], ALU.mult)
            link(v.tensor_scalar(t1[z, 0:HEADS], t1[z, 0:HEADS], 64.0, None, ALU.mult))
            tt(kp[z, 0, :, :], kp[z, 0, :, :], t1[z, 0:HEADS].unsqueeze(2).broadcast_to([1, HEADS, NI]), ALU.add)
            y = slice(64, 65)
            tt(t1[y, 0:HEADS], col(kr, 64), skip[y, 1, :], ALU.add)
            tt(kp[y, 0, :, :], xw[y, 0, :].unsqueeze(1).broadcast_to([1, HEADS, NI]),
               t1[y, 0:HEADS].unsqueeze(2).broadcast_to([1, HEADS, NI]), ALU.mult)
            tt(kp[y, 0, :, :], kp[y, 0, :, :], skip[y, 3, :].unsqueeze(2).broadcast_to([1, HEADS, NI]), ALU.add)
            link(v.tensor_scalar(t1[y, 0:HEADS], skip[y, 2, :], 64.0, None, ALU.mult))
            tt(kp[y, 0, :, :], kp[y, 0, :, :], t1[y, 0:HEADS].unsqueeze(2).broadcast_to([1, HEADS, NI]), ALU.mult)
            v.memset(xt[y, 0, :], 1.0).then_inc(k_ready, 1)
            tt(qk[:, :], skip[:, 0, :], skip[:, 1, :], ALU.mult)
            link(v.tensor_scalar(qk[:, :], qk[:, :], 1.0 / 64, None, ALU.mult))
            tt(sx[:, :, :], att.gram[:, :].unsqueeze(1).broadcast_to([64, HEADS, T]),
               qk[0:64, :].unsqueeze(2).broadcast_to([64, HEADS, T]), ALU.mult)
            v.wait_ge(scores_done, 1)
            for o in range(0, HEADS, 16):
                tt(sc[:, o:o + 16, :], ps[:, o:o + 16, :], sx[:, o:o + 16, :], ALU.add)
            link(v.tensor_reduce(mx[:, :], sc[:, :, :], AX.X, ALU.max))
            v.tensor_tensor(sc[:, :, :], sc[:, :, :], mx[:, :].unsqueeze(2).broadcast_to([64, HEADS, T]),
                            ALU.subtract).then_inc(shifted, 1)
            v.wait_ge(exped, 1)
            link(v.tensor_reduce(sm[:, :], sx[:, :, :], AX.X, ALU.add))
            link(v.reciprocal(rs[:, :], sm[:, :]))
            tt(sx[:, :, :], sx[:, :, :], rs[:, :].unsqueeze(2).broadcast_to([64, HEADS, T]), ALU.mult)
            v.transpose(pt[:, :, :].rearrange("p o t -> p (o t)"),
                        sx[:, :, :].rearrange("p o t -> p (o t)")).then_inc(turned, 1)
            tt(qk[:, :], vec[:, 0, :], vec[:, 1, :], ALU.mult)
            tt(sc[:, :, :], sx[:, :, :], qk[0:64, :].unsqueeze(2).broadcast_to([64, HEADS, T]), ALU.mult)
            link(v.tensor_reduce(mix[:, :], sc[:, :, :].rearrange("p o s -> p s o"), AX.X, ALU.add))
            link(v.transpose(mixt[:, :], mix[:, :]))
            link(v.memset(att.mix_t[:, :], 0.0))
            for half in range(2):
                for b in range(B):
                    p = 64 * half + 32 * b
                    link(v.tensor_copy(att.mix_t[p:p + 32, p:p + 32], mixt[32 * b:32 * b + 32, :]))
            tt(dct[:, :], dcv[:, 1, :], dcv[:, 2, :], ALU.add)
            tt(dct[:, :], dct[:, :], dcv[:, 0, :], ALU.mult)
            link(v.tensor_reduce(att.dc[:, :], dct[:, :], AX.X, ALU.add))
            tt(att.dc[:, :], att.dc[:, :], bp[:, :], ALU.add)

        @block.scalar
        def _(s):
            s.wait_ge(shifted, 1)
            s.activation(sx[:, :, :], sc[:, :, :], ACT.Exp).then_inc(exped, 1)

        @block.tensor
        def _(pe):
            pe.wait_ge(k_ready, 1)
            pe.wait_ge(loaded, 19 * 16)
            for b in range(B):
                for o in range(0, HEADS, 16):
                    for m in range(8):
                        mm = pe.matmul(ps[T * b:T * b + T, o:o + 16, :], xt[:, m, T * b:T * b + T],
                                       kp[:, m, o:o + 16, T * b:T * b + T], start=(m == 0), stop=(m == 7))
            mm.then_inc(scores_done, 1)


def stage_value_tables(k):
    nc, a = k.nc, k.a
    with ExitStack() as ctx:
        sb = lambda name, shape: k.sb(name, shape, ctx=ctx)
        wv, wp = sb("s3_wv", [128, 4, 512]), sb("s3_wp", [128, 2, 512])
        herm = sb("s3_herm", [128, 2, 512])
        fac = sb("s3_fac", [128, 2])
        d, t = sb("s3_d", [128, 2, 512]), sb("s3_t", [128, 3, 512])
        loaded, chain, stored = k.sem("s3_loaded"), k.sem("s3_chain"), k.sem("s3_stored")
        block = ctx.enter_context(nc.Block())

        @block.sync
        def _(sp):
            sp.dma_start(wv[:, :, :], a["wV"]).then_inc(loaded, 16)
            sp.dma_start(wp[:, :, :], a["wP"]).then_inc(loaded, 16)
            sp.dma_start(herm[:, :, :], a["herm_full"].rearrange("p (u f) -> p u f", u=2)).then_inc(loaded, 16)
            for j, name in enumerate(("wVs", "wPs")):
                sp.dma_start(fac[:, j:j + 1], sub(a[name], 0, [[1, HEADS], [0, 4], [1, 1]])).then_inc(loaded, 16)
            sp.wait_ge(chain, 15)
            for c in range(2):
                sp.dma_start(sub(a["d_d"], 2048 * c, [[4096, HEADS], [512, 4], [1, 512]]), d[:, c, :]).then_inc(stored, 16)
            sp.wait_ge(stored, 32)

        @block.vector
        def _(v):
            link = Chain(v, chain)
            tt = lambda o, x, y, op: link(v.tensor_tensor(o, x, y, op))
            v.wait_ge(loaded, 80)
            for j in range(4):
                tt(wv[:, j, :], wv[:, j, :], herm[:, j // 2, :], ALU.mult)
            tt(wv[:, 0, :], wv[:, 0, :], wv[:, 2, :], ALU.add)
            tt(wv[:, 1, :], wv[:, 1, :], wv[:, 3, :], ALU.subtract)
            vr, vi, pr, pi = wv[:, 0, :], wv[:, 1, :], wp[:, 0, :], wp[:, 1, :]
            link(v.tensor_scalar(t[:, 0, :], vr, fac[:, 0:1], None, ALU.add))
            tt(d[:, 0, :], pr, t[:, 0, :], ALU.mult)
            tt(t[:, 1, :], pi, vi, ALU.mult)
            tt(d[:, 0, :], d[:, 0, :], t[:, 1, :], ALU.subtract)
            link(v.scalar_tensor_tensor(out=d[:, 0, :], in0=vr, scalar=fac[:, 1:2], in1=d[:, 0, :],
                                        op0=ALU.mult, op1=ALU.add))
            tt(d[:, 1, :], pr, vi, ALU.mult)
            tt(t[:, 2, :], pi, t[:, 0, :], ALU.mult)
            tt(d[:, 1, :], d[:, 1, :], t[:, 2, :], ALU.add)
            link(v.scalar_tensor_tensor(out=d[:, 1, :], in0=vi, scalar=fac[:, 1:2], in1=d[:, 1, :],
                                        op0=ALU.mult, op1=ALU.add))


def stage_mix(k, att):
    nc, a = k.nc, k.a
    with ExitStack() as ctx:
        sb = lambda name, shape: k.sb(name, shape, ctx=ctx)
        HALF = NN * NM // 2
        x4 = sb("s4_x4", [128, B, 2, HALF])
        dd = sb("s4_dd", [128, 2, 2, HALF])
        y = sb("s4_y", [128, 2, 2, HALF])
        tv, tp = sb("s4_tv", [128, HALF]), sb("s4_tp", [128, HALF])
        z = sb("s4_z", [64, 4 * 512])
        xin, xout = sb("s4_xin", [128, 4, 512]), sb("s4_xout", [128, 4, 512])
        psz = k.ps("s4_psz", [64, 4 * 512], ctx)
        pss = k.ps("s4_pss", [128, 4, 512], ctx)
        x4_loaded, d_loaded = k.sem("s4_x4_loaded"), [k.sem("s4_d0_loaded"), k.sem("s4_d1_loaded")]
        re_ready, im_ready = k.sem("s4_re_ready"), k.sem("s4_im_ready")
        chain_v, chain_p = k.sem("s4_chain_v"), k.sem("s4_chain_p")
        mixed, z_copied, z_stored = k.sem("s4_mixed"), k.sem("s4_z_copied"), k.sem("s4_z_stored")
        xin_loaded, skip_done = k.sem("s4_xin_loaded"), k.sem("s4_skip_done")
        skip_copied, skip_stored = k.sem("s4_skip_copied"), k.sem("s4_skip_stored")
        block = ctx.enter_context(nc.Block())
        STEPS = HEADS // 4 * B

        @block.sync
        def _(sp):
            with sp.Fori(0, 2) as nh:
                sp.wait_ge(mixed, nh * STEPS)
                for b in range(B):
                    for o in range(4):
                        sp.dma_start(x4[32 * o:32 * o + 32, b, :, :],
                                     sub(a["xf_d"], nh * HALF + b * T * 4096,
                                         [[4096, T], [2048, 2], [1, HALF]])).then_inc(x4_loaded, 16)
                for oc in range(HEADS // 4):
                    if oc >= 2:
                        sp.wait_ge(re_ready, nh * STEPS + 2 * (oc - 1))
                        sp.wait_ge(im_ready, nh * STEPS + 2 * (oc - 1))
                    for o in range(4):
                        sp.dma_start(dd[32 * o:32 * o + 32, oc % 2, :, :],
                                     sub(a["d_d"], nh * HALF + (4 * oc + o) * 4096,
                                         [[0, 32], [2048, 2], [1, HALF]])).then_inc(d_loaded[oc % 2], 16)
                sp.wait_ge(z_copied, nh + 1)
                sp.dma_start(sub(a["z_d"], nh * HALF, [[4096, NI], [2048, 2], [1, HALF]]),
                             z[:, :].rearrange("p (c f) -> p c f", c=2)).then_inc(z_stored, 16)
            sp.wait_ge(z_stored, 32)

        @block.gpsimd
        def _(p):
            with p.Fori(0, 2) as nh:
                p.wait_ge(x4_loaded, 128 * nh + 128)
                for j in range(STEPS):
                    oc, b = j // 2, j % 2
                    p.wait_ge(d_loaded[oc % 2], 256 * nh + 64 * (oc // 2) + 64)
                    if j >= 2:
                        p.wait_ge(mixed, nh * STEPS + (j - 1))
                    dr, di, xr, xi = dd[:, oc % 2, 0, :], dd[:, oc % 2, 1, :], x4[:, b, 0, :], x4[:, b, 1, :]
                    p.tensor_tensor(tp[:, :], di, xr, ALU.mult).then_inc(chain_p, 1)
                    p.tensor_tensor(y[:, j % 2, 1, :], dr, xi, ALU.mult).then_inc(chain_p, 1)
                    p.wait_ge(chain_p, nh * 2 * STEPS + (2 * j + 2))
                    p.tensor_tensor(y[:, j % 2, 1, :], y[:, j % 2, 1, :], tp[:, :], ALU.add).then_inc(im_ready, 1)
                    p.wait_ge(im_ready, nh * STEPS + (j + 1))

        @block.vector
        def _(v):
            with v.Fori(0, 2) as nh:
                v.wait_ge(x4_loaded, 128 * nh + 128)
                for j in range(STEPS):
                    oc, b = j // 2, j % 2
                    v.wait_ge(d_loaded[oc % 2], 256 * nh + 64 * (oc // 2) + 64)
                    if j >= 2:
                        v.wait_ge(mixed, nh * STEPS + (j - 1))
                    dr, di, xr, xi = dd[:, oc % 2, 0, :], dd[:, oc % 2, 1, :], x4[:, b, 0, :], x4[:, b, 1, :]
                    v.tensor_tensor(tv[:, :], di, xi, ALU.mult).then_inc(chain_v, 1)
                    v.tensor_tensor(y[:, j % 2, 0, :], dr, xr, ALU.mult).then_inc(chain_v, 1)
                    v.wait_ge(chain_v, nh * 2 * STEPS + (2 * j + 2))
                    v.tensor_tensor(y[:, j % 2, 0, :], y[:, j % 2, 0, :], tv[:, :], ALU.subtract).then_inc(re_ready, 1)
                    v.wait_ge(re_ready, nh * STEPS + (j + 1))

        @block.scalar
        def _(s):
            with s.Fori(0, 4) as i:
                for half in range(2):
                    s.dma_start(xin[64 * half:64 * half + 64, :, :],
                                sub(a["xn_d"], half * (PIX // 2) + i * 2048,
                                    [[PIX, NI], [512, 4], [1, 512]])).then_inc(xin_loaded, 16)
                s.wait_ge(skip_done, i + 1)
                for j in range(4):
                    ins = s.activation(xout[:, j, :], pss[:, j, :], ACT.Copy)
                ins.then_inc(skip_copied, 1)
                s.wait_ge(skip_copied, i + 1)
                for half in range(2):
                    s.dma_start(sub(a["sk_d"], half * (PIX // 2) + i * 2048, [[PIX, NI], [512, 4], [1, 512]]),
                                xout[64 * half:64 * half + 64, :, :]).then_inc(skip_stored, 16)
                s.wait_ge(skip_stored, 32 * i + 32)
            with s.Fori(0, 2) as nh:
                s.wait_ge(mixed, nh * STEPS + STEPS)
                for j in range(4):
                    ins = s.activation(z[:, 512 * j:512 * j + 512], psz[:, 512 * j:512 * j + 512], ACT.Copy)
                ins.then_inc(z_copied, 1)
                s.wait_ge(z_stored, 16 * nh + 16)

        @block.tensor
        def _(pe):
            with pe.Fori(0, 4) as i:
                pe.wait_ge(xin_loaded, 32 * i + 32)
                pe.wait_ge(skip_copied, i)
                for j in range(4):
                    mm = pe.matmul(pss[:, j, :], att.mix_t[:, :], xin[:, j, :], start=True, stop=True)
                mm.then_inc(skip_done, 1)
            with pe.Fori(0, 2) as nh:
                pe.wait_ge(z_copied, nh)
                for j in range(STEPS):
                    oc, b = j // 2, j % 2
                    pe.wait_ge(re_ready, nh * STEPS + (j + 1))
                    pe.wait_ge(im_ready, nh * STEPS + (j + 1))
                    for q in range(4):
                        mm = pe.matmul(psz[T * b:T * b + T, 512 * q:512 * q + 512], att.prob_t[:, oc, b, :],
                                       y[:, j % 2, q // 2, 512 * (q % 2):512 * (q % 2) + 512],
                                       start=(oc == 0), stop=(oc == HEADS // 4 - 1))
                    mm.then_inc(mixed, 1)


def pe_inverse(pe, z, icols, irows, ps_b, bs, ps_o, z_ready, n_z, cols_done, bs_ready, n_b, out_done):
    pe.wait_ge(z_ready, n_z)
    for i in range(GROUP):
        mm = pe.matmul(ps_b[:, i, :], z[:, i, :, :], icols[:, :], start=True, stop=True)
    mm.then_inc(cols_done, 1)
    pe.wait_ge(bs_ready, n_b)
    for i in range(0, GROUP, 4):
        mm = pe.matmul(ps_o[:, i:i + 4, :], irows[:, :], bs[:, i:i + 4, :], start=True, stop=True)
    mm.then_inc(out_done, 1)


def stage_project(k, att):
    nc, a = k.nc, k.a
    with ExitStack() as ctx:
        sb = lambda name, shape: k.sb(name, shape, ctx=ctx)
        zs, zw = sb("s5_zs", [64, NI, NM]), sb("s5_zw", [64, NI, NM])
        sign = sb("s5_sign", [64, 1])
        sk = sb("s5_sk", [128, GROUP, HW])
        z = sb("s5_z", [64, GROUP, 2, NM])
        icols, irows = sb("s5_icols", [64, 128]), sb("s5_irows", [128, 128])
        dc = sb("s5_dc", [64, 1])
        bs = sb("s5_bs", [128, GROUP, HW])
        ps_b, ps_o = k.ps("s5_psb", [128, GROUP, HW], ctx), k.ps("s5_pso", [128, GROUP, HW], ctx)
        loaded, sk_loaded, dc_added = k.sem("s5_loaded"), k.sem("s5_sk_loaded"), k.sem("s5_dc_added")
        z_ready, cols_done, bs_ready = k.sem("s5_z_ready"), k.sem("s5_cols_done"), k.sem("s5_bs_ready")
        out_done, out_added, sk_added = k.sem("s5_out_done"), k.sem("s5_out_added"), k.sem("s5_sk_added")
        block = ctx.enter_context(nc.Block())

        @block.sync
        def _(sp):
            sp.dma_start(zs[:, :, :], sub(a["z_d"], 0, [[NM, 64], [4096, NI], [1, NM]])).then_inc(loaded, 16)
            for c in range(2):
                sp.dma_start(zw[32 * c:32 * c + 32, :, :],
                             sub(a["z_d"], 2048 * (1 - c), [[NM, 32], [4096, NI], [1, NM]])).then_inc(loaded, 16)
            sp.dma_start(sign[:, :], a["im_sign"][32:96]).then_inc(loaded, 16)
            sp.dma_start(icols[:, :], a["idft_cols"]).then_inc(loaded, 16)
            sp.dma_start(irows[:, :], a["idft_rows"]).then_inc(loaded, 16)
            with sp.Fori(0, NG) as g:
                sp.wait_ge(sk_added, g)
                sp.dma_start(sk[:, :, :], a["sk_d"][bass.ds(g * GROUP, GROUP)].rearrange("i h w -> h i w"))\
                  .then_inc(sk_loaded, 16)
            sp.wait_ge(sk_loaded, 16 * NG)

        @block.vector
        def _(v):
            v.wait_ge(loaded, 96)
            v.tensor_scalar(zs[0:1, :, 0], zs[0:1, :, 0], att.dc[0:1, 0:1], None, ALU.add).then_inc(dc_added, 1)
            v.tensor_copy(dc[32:33, :], att.dc[0:1, 0:1]).then_inc(dc_added, 1)
            v.wait_ge(dc_added, 2)
            v.tensor_scalar(zw[32:33, :, 0], zw[32:33, :, 0], dc[32:33, 0:1], None, ALU.add).then_inc(dc_added, 1)
            v.wait_ge(dc_added, 3)
            with v.Fori(0, NG) as g:
                v.wait_ge(cols_done, g)
                v.tensor_copy(z[:, :, 0, :], zs[:, bass.ds(g * GROUP, GROUP), :])
                v.tensor_scalar(z[:, :, 1, :], zw[:, bass.ds(g * GROUP, GROUP), :], sign[:, 0:1], None, ALU.mult)\
                 .then_inc(z_ready, 1)
                v.wait_ge(sk_loaded, 16 * g + 16)
                xg = k.xa[:, bass.ds(g * GROUP, GROUP), :]
                v.tensor_tensor(xg, xg, sk[:, :, :], ALU.add).then_inc(sk_added, 1)
                v.wait_ge(sk_added, g + 1)
                v.wait_ge(out_done, g + 1)
                for i in range(0, GROUP, 4):
                    xg = k.xa[:, bass.ds(g * GROUP + i, 4), :]
                    ins = v.tensor_tensor(xg, ps_o[:, i:i + 4, :], xg, ALU.add)
                ins.then_inc(out_added, 1)

        @block.scalar
        def _(s):
            with s.Fori(0, NG) as g:
                s.wait_ge(cols_done, g + 1)
                s.wait_ge(out_done, g)
                for i in range(0, GROUP, 4):
                    ins = s.activation(bs[:, i:i + 4, :], ps_b[:, i:i + 4, :], ACT.Copy)
                ins.then_inc(bs_ready, 1)

        @block.tensor
        def _(pe):
            pe.wait_ge(loaded, 96)
            with pe.Fori(0, NG) as g:
                pe.wait_ge(out_added, g)
                pe_inverse(pe, z, icols, irows, ps_b, bs, ps_o, z_ready, g + 1, cols_done, bs_ready, g + 1, out_done)


STEP = 4
NS = NI // STEP


def run_slots(eng, slot, steady, total):
    for t in range(4):
        slot(t, t % 2)
    with eng.Fori(0, (steady - 4) // 2) as i:
        for u in range(2):
            slot(2 * i + (4 + u), u)
    for t in range(steady, total):
        slot(t, t % 2)


def during(t, lo, hi=NS):
    return not isinstance(t, int) or lo <= t < hi


def wait_count(eng, sem, n):
    if not isinstance(n, int) or n > 0:
        eng.wait_ge(sem, n)


def images(t):
    return bass.ds(STEP * t, STEP)


def v_moments(v, link, st, mom, tmp, ready):
    link(v.memset(tmp, 0.0))
    row_stats(v, link, st, mom[:, 0, :], mom[:, 1, :], tmp)
    link(v.tensor_tensor(tmp, mom[:, 0, :], mom[:, 0, :], ALU.mult))
    v.tensor_tensor(mom[:, 1, :], mom[:, 1, :], tmp, ALU.add).then_inc(ready, 1)


def v_image_norm(v, link, ps, mom_done, n, mean, var, scale, bias, tmp, veps, root, gain, shift, var_ready, root_ready, nr):
    v.wait_ge(mom_done, n)
    link(v.tensor_copy(mean, ps[:, 0:NI]))
    link(v.tensor_tensor(tmp, mean, mean, ALU.mult))
    link(v.tensor_tensor(var, ps[:, NI:2 * NI], tmp, ALU.subtract))
    v.tensor_scalar(veps, var, 0.0, 1e-5, ALU.max, ALU.add).then_inc(var_ready, 1)
    v.wait_ge(var_ready, nr)
    newton_rsqrt(v, link, veps, root, scale, tmp, root_ready, nr)
    link(v.tensor_scalar(scale, scale, gain, None, ALU.mult))
    link(v.tensor_tensor(tmp, mean, scale, ALU.mult))
    link(v.tensor_scalar(bias, tmp, -1.0, shift, ALU.mult, ALU.add))


def stage_mixer(k):
    nc, a = k.nc, k.a
    with ExitStack() as ctx:
        sb = lambda name, shape: k.sb(name, shape, ctx=ctx)
        f, m = sb("s6_f", [HW, NI, HW]), sb("s6_m", [HW, NI, HW])
        st = sb("s6_st", [128, NI, 6])
        mom = sb("s6_mom", [128, 2, NI])
        names = ("mean", "var", "scale", "bias", "tmp", "veps", "root", "as", "ab", "cs", "cb", "fs", "fb", "ws", "wb")
        mean, var, scale, bias, tmp, veps, root, a_s, a_b, c_s, c_b, f_s, f_b, w_s, w_b = \
            (sb(f"s6_{n}", [128, NI]) for n in names)
        rows, cols = sb("s6_rows", [128, 128]), sb("s6_cols", [128, 256])
        icols, irows = sb("s6_icols", [128, 128]), sb("s6_irows", [128, 128])
        w = sb("s6_w", [128, 2, 2, NM])
        sk = sb("s6_sk", [128, 2, 2])
        pre = sb("s6_pre", [128, 2, STEP, HW])
        xg, yt, bs = (sb(f"s6_{n}", [128, 2, STEP, HW]) for n in ("xg", "yt", "bs"))
        z = sb("s6_z", [128, 2, STEP, 2, NM])
        ps_a, ps_b, ps_o = (k.ps(f"s6_{n}", [128, 2, STEP, HW], ctx) for n in ("psa", "psb", "pso"))
        ps_x = k.ps("s6_psx", [128, 2, 512], ctx)
        loaded, chain = k.sem("s6_loaded"), k.sem("s6_chain")
        mom_ready, mom_done = k.sem("s6_mom_ready"), k.sem("s6_mom_done")
        var_ready, root_ready = k.sem("s6_var_ready"), k.sem("s6_root_ready")
        xg_ready, rows_done, yt_ready = k.sem("s6_xg_ready"), k.sem("s6_rows_done"), k.sem("s6_yt_ready")
        spec_done, z_ready = k.sem("s6_spec_done"), k.sem("s6_z_ready")
        cols_done, bs_ready, out_done = k.sem("s6_cols_done"), k.sem("s6_bs_ready"), k.sem("s6_out_done")
        f_ready, part_ready, pre_ready = k.sem("s6_f_ready"), k.sem("s6_part_ready"), k.sem("s6_pre_ready")
        m_kept, xa_ready, w_signed = k.sem("s6_m_kept"), k.sem("s6_xa_ready"), k.sem("s6_w_signed")
        skip_ready, skip_added, g_ready = k.sem("s6_skip_ready"), k.sem("s6_skip_added"), k.sem("s6_g_ready")
        x_added = k.sem("s6_x_added")
        block = ctx.enter_context(nc.Block())

        @block.sync
        def _(sp):
            sp.dma_start(rows[:, :], a["dft_rows"][:, 0:128]).then_inc(loaded, 16)
            sp.dma_start(cols[:, :], a["dft_cols"]).then_inc(loaded, 16)
            sp.dma_start(irows[:, :], a["idft_rows"]).then_inc(loaded, 16)
            for h in range(2):
                sp.dma_start(icols[64 * h:64 * h + 64, :], a["idft_cols"]).then_inc(loaded, 16)
            for j in range(2):
                sp.dma_start(w[0:64, j, :, :], a[f"wM{j}"]).then_inc(loaded, 16)
                for c in range(2):
                    sp.dma_start(w[64:128, j, 1 - c, :], a[f"wM{j}"][:, c, :]).then_inc(loaded, 16)
                sp.dma_start(sk[:, j, 0:1], sub(a[f"wM{j}s"], 0, [[0, 128], [1, 1]])).then_inc(loaded, 16)
                sp.dma_start(sk[:, j, 1:2], sub(a[f"bM{j}s"], 0, [[0, 128], [1, 1]])).then_inc(loaded, 16)
            sp.wait_ge(loaded, 15 * 16)

        @block.vector
        def _(v):
            link = Chain(v, chain)
            tt = lambda o, x, y, op: link(v.tensor_tensor(o, x, y, op))
            norm = lambda n, s_, b_: v_image_norm(
                v, link, ps_x[:, 0, :], mom_done, n, mean[:, :], var[:, :], s_[:, :], b_[:, :], tmp[:, :], veps[:, :],
                root[:, :], k.norm_g[:, order[n - 1]:order[n - 1] + 1], k.norm_b[:, order[n - 1]:order[n - 1] + 1],
                var_ready, root_ready, n + (n > 1))
            order = (1, 3, 4, 5)
            with v.Fori(0, NI) as i:
                v.bn_stats(st[:, bass.ds(i, 1), :], k.xa[:, bass.ds(i, 1), :])
            v.wait_ge(loaded, 15 * 16)
            v_moments(v, link, st, mom, tmp[:, :], mom_ready)
            v.tensor_scalar(w[64:128, :, 1, :], w[64:128, :, 1, :], -1.0, None, ALU.mult).then_inc(w_signed, 1)
            norm(1, scale, bias)
            tt(tmp[:, :], scale[:, :], scale[:, :], ALU.mult)
            tt(veps[:, :], var[:, :], tmp[:, :], ALU.mult)
            v.tensor_scalar(veps[:, :], veps[:, :], 1e-5, None, ALU.add).then_inc(var_ready, 1)
            v.wait_ge(var_ready, 2)
            newton_rsqrt(v, link, veps[:, :], root[:, :], a_s[:, :], tmp[:, :], root_ready, 2)
            link(v.tensor_scalar(a_s[:, :], a_s[:, :], k.norm_g[:, 2:3], None, ALU.mult))
            link(v.tensor_scalar(tmp[:, :], a_s[:, :], k.norm_b[:, 1:2], None, ALU.mult))
            link(v.tensor_scalar(a_b[:, :], tmp[:, :], -1.0, k.norm_b[:, 2:3], ALU.mult, ALU.add))
            tt(c_s[:, :], scale[:, :], a_s[:, :], ALU.mult)
            tt(tmp[:, :], bias[:, :], a_s[:, :], ALU.mult)
            tt(c_b[:, :], tmp[:, :], a_b[:, :], ALU.add)
            v.wait_ge(w_signed, 1)

            def multiply(s, u, n0):
                v.wait_ge(spec_done, s + (n0 + 1))
                wait_count(v, cols_done, s + (n0 - 1))
                src = ps_x[:, u, 0:STEP * NM].rearrange("p (i m) -> p i m", m=NM)
                for c in range(2):
                    ins = v.tensor_tensor(z[:, u, :, c, :], src,
                                          w[:, n0 // NS, c:c + 1, :].broadcast_to([128, STEP, NM]), ALU.mult)
                ins.then_inc(z_ready, 1)

            def stats(s, n0):
                v.wait_ge(f_ready, s + (n0 + 1))
                for j in range(STEP):
                    one = bass.ds(STEP * s + j, 1)
                    v.bn_stats(st[:, one, :], f[:, one, :])

            def norm_in(s, u):
                wait_count(v, rows_done, s + (-1))
                for j in range(STEP):
                    one = bass.ds(STEP * s + j, 1)
                    ins = v.tensor_scalar(xg[:, u, j, :], k.xa[:, one, :], c_s[:, one], c_b[:, one], ALU.mult, ALU.add)
                ins.then_inc(xg_ready, 1)

            def slot0(s, u):
                if during(s, 0):
                    multiply(s, u, 0)
                if during(s + 2, 2):
                    norm_in(s + 2, u)
                if during(s + (-3), 0):
                    stats(s + (-3), 0)

            norm_in(0, 0)
            norm_in(1, 1)
            run_slots(v, slot0, NS - 2, NS + 3)
            v_moments(v, link, st, mom, tmp[:, :], mom_ready)
            norm(2, f_s, f_b)
            link(v.tensor_scalar(w_s[:, :], a_s[:, :], sk[:, 0, 0:1], None, ALU.mult))
            link(v.tensor_scalar(tmp[:, :], a_b[:, :], sk[:, 0, 0:1], sk[:, 0, 1:2], ALU.mult, ALU.add))
            v.tensor_tensor(w_b[:, :], f_b[:, :], tmp[:, :], ALU.add).then_inc(skip_ready, 1)

            def skip(s, u):
                v.wait_ge(part_ready, s + 1)
                wait_count(v, xg_ready, s + (NS - 1))
                for j in range(STEP):
                    one = bass.ds(STEP * s + j, 1)
                    ins = v.scalar_tensor_tensor(out=pre[:, u, j, :], in0=k.xa[:, one, :], scalar=w_s[:, one],
                                                 in1=f[:, one, :], op0=ALU.mult, op1=ALU.add)
                ins.then_inc(pre_ready, 1)

            def slot1(s, u):
                if during(s, 0):
                    multiply(s, u, NS)
                if during(s + 3, 3):
                    skip(s + 3, 1 - u)
                if during(s + (-3), 0):
                    stats(s + (-3), NS)

            v.wait_ge(xa_ready, NS)
            v.wait_ge(skip_ready, 1)
            for s in range(3):
                skip(s, s % 2)
            run_slots(v, slot1, NS - 4, NS + 3)
            v_moments(v, link, st, mom, tmp[:, :], mom_ready)
            norm(3, f_s, f_b)
            v.tensor_scalar(w_b[:, :], f_b[:, :], sk[:, 1, 1:2], None, ALU.add).then_inc(skip_ready, 1)
            v.wait_ge(m_kept, NS)
            with v.Fori(0, NS) as s:
                v.wait_ge(part_ready, s + (NS + 1))
                fg = f[:, images(s), :]
                v.scalar_tensor_tensor(out=fg, in0=m[:, images(s), :], scalar=sk[:, 1, 0:1], in1=fg,
                                       op0=ALU.mult, op1=ALU.add).then_inc(skip_added, 1)
                v.wait_ge(skip_added, s + 1)
                for j in range(STEP):
                    one = bass.ds(STEP * s + j, 1)
                    v.bn_stats(st[:, one, :], f[:, one, :])
            v_moments(v, link, st, mom, tmp[:, :], mom_ready)
            norm(4, scale, bias)
            v.memset(tmp[:, :], 0.0).then_inc(skip_ready, 1)
            v.wait_ge(x_added, 1)
            with v.Fori(0, NS) as s:
                v.wait_ge(g_ready, s + 1)
                xs = k.x[:, images(s), :]
                v.tensor_tensor(xs, xs, f[:, images(s), :], ALU.add)

        @block.gpsimd
        def _(p):
            with p.Fori(0, NS // 2) as i:
                for u in range(2):
                    p.wait_ge(xg_ready, 2 * i + (u + NS + 1))
                    p.tensor_copy(m[:, images(2 * i + u), :], xg[:, u, :, :]).then_inc(m_kept, 1)
            p.tensor_tensor(k.x[:, :, :], k.x[:, :, :], k.xa[:, :, :], ALU.add).then_inc(x_added, 1)

        @block.scalar
        def _(s_):
            def root_step(n):
                s_.wait_ge(var_ready, n)
                s_.activation(root[:, :], veps[:, :], ACT.Sqrt).then_inc(root_ready, 1)

            def affine(dst, s, scale_, bias_, done):
                for j in range(STEP):
                    one = bass.ds(STEP * s + j, 1)
                    ins = s_.activation(dst[:, one, :], dst[:, one, :], ACT.Identity, scale=scale_[:, one], bias=bias_[:, one])
                ins.then_inc(done, 1)

            def copies(t, u, n0):
                if during(t, 0):
                    s_.wait_ge(rows_done, t + (n0 + 1))
                    wait_count(s_, spec_done, t + (n0 - 1))
                    s_.activation(yt[:, u, :, :], ps_a[:, u, :, :], ACT.Copy).then_inc(yt_ready, 1)

            def copies_back(t, u, n0):
                if during(t + (-2), 0):
                    s_.wait_ge(cols_done, t + (n0 - 1))
                    wait_count(s_, out_done, t + (n0 - 3))
                    s_.activation(bs[:, u, :, :], ps_b[:, u, :, :], ACT.Copy).then_inc(bs_ready, 1)
                if during(t + (-3), 0):
                    s_.wait_ge(out_done, t + (n0 - 2))
                    s_.activation(f[:, images(t + (-3)), :], ps_o[:, 1 - u, :, :], ACT.Copy).then_inc(f_ready, 1)

            def slot0(t, u):
                copies(t, u, 0)
                if during(t, 0):
                    s_.wait_ge(xg_ready, t + 1)
                    affine(k.xa, t, scale, bias, xa_ready)
                copies_back(t, u, 0)

            def part(s):
                affine(f, s, f_s, w_b, part_ready)

            def gelu(s, u):
                s_.wait_ge(pre_ready, s + 1)
                wait_count(s_, rows_done, s + (NS - 1))
                wait_count(s_, m_kept, s + (-1))
                s_.activation(xg[:, u, :, :], pre[:, u, :, :], ACT.Gelu).then_inc(xg_ready, 1)

            def slot1(t, u):
                copies(t, u, NS)
                if during(t + 2, 2):
                    gelu(t + 2, u)
                if during(t + 4, 4):
                    part(t + 4)
                copies_back(t, u, NS)

            root_step(1)
            root_step(2)
            run_slots(s_, slot0, NS, NS + 3)
            root_step(3)
            s_.wait_ge(skip_ready, 1)
            part(0)
            part(1)
            gelu(0, 0)
            part(2)
            gelu(1, 1)
            part(3)
            run_slots(s_, slot1, NS - 4, NS + 3)
            root_step(4)
            s_.wait_ge(skip_ready, 2)
            with s_.Fori(0, NS) as s:
                part(s)
            root_step(5)
            s_.wait_ge(skip_ready, 3)
            with s_.Fori(0, NS) as s:
                affine(f, s, scale, bias, g_ready)

        @block.tensor
        def _(pe):
            def moments(n):
                pe.wait_ge(mom_ready, n)
                pe.matmul(ps_x[:, 0, 0:128], k.ones[:, :], mom[:, :, :], start=True, stop=True).then_inc(mom_done, 1)

            def slot(t, u, n0):
                if during(t, 0):
                    pe.wait_ge(xg_ready, t + (n0 + 1))
                    wait_count(pe, yt_ready, t + (n0 - 1))
                    for j in range(STEP):
                        mm = pe.matmul(ps_a[:, u, j, :], xg[:, u, j, :], rows[:, :], start=True, stop=True)
                    mm.then_inc(rows_done, 1)
                if during(t + (-1), 0):
                    pe.wait_ge(yt_ready, t + n0)
                    wait_count(pe, z_ready, t + (n0 - 2))
                    out = ps_x[:, 1 - u, 0:STEP * NM]
                    pe.matmul(out, cols[:, 0:128], yt[:, 1 - u, :, 0:64], start=True, stop=False)
                    pe.matmul(out, cols[:, 128:256], yt[:, 1 - u, :, 64:128], start=False, stop=True).then_inc(spec_done, 1)
                if during(t + (-2), 0):
                    pe.wait_ge(z_ready, t + (n0 - 1))
                    wait_count(pe, bs_ready, t + (n0 - 3))
                    for j in range(STEP):
                        mm = pe.matmul(ps_b[:, u, j, :], z[:, u, j, :, :], icols[:, :], start=True, stop=True)
                    mm.then_inc(cols_done, 1)
                if during(t + (-3), 0):
                    pe.wait_ge(bs_ready, t + (n0 - 2))
                    wait_count(pe, f_ready, t + (n0 - 4))
                    pe.matmul(ps_o[:, 1 - u, :, :], irows[:, :], bs[:, 1 - u, :, :], start=True, stop=True).then_inc(out_done, 1)

            moments(1)
            pe.wait_ge(loaded, 15 * 16)
            pe.wait_ge(w_signed, 1)
            run_slots(pe, lambda t, u: slot(t, u, 0), NS, NS + 3)
            moments(2)
            run_slots(pe, lambda t, u: slot(t, u, NS), NS, NS + 3)
            moments(3)
            moments(4)


NK = FT + 2
NF = 2 * NK


def stage_stu_setup(k, stu):
    nc, a = k.nc, k.a
    with ExitStack() as ctx:
        sb = lambda name, shape: k.sb(name, shape, ctx=ctx)
        st = sb("s7_st", [128, NI, 6])
        mean, var, rstd, root, tmp, veps = (sb(f"s7_{n}", [128, NI]) for n in ("mean", "var", "rstd", "root", "tmp", "veps"))
        ug = sb("s7_u", [128, GROUP, HW])
        mload = sb("s7_mload", [128, 2, FT * 128])
        mp, mm_ = sb("s7_mp", [128, FT * 128]), sb("s7_mm", [128, FT * 128])
        mu, mut = sb("s7_mu", [128, 4, 3, 128]), sb("s7_mut", [128, 3, 128])
        lw, oh, ys = sb("s7_lw", [128, 2, 4]), sb("s7_oh", [128, 4]), sb("s7_ys", [128, 4])
        z4, t4, u4 = sb("s7_z4", [128, 4]), sb("s7_t4", [128, 4]), sb("s7_u4", [128, 4])
        one = sb("s7_one", [128, 2])
        masks = sb("s7_masks", [128, 4, NI])
        sig, sq, sr, s_t = (sb(f"s7_{n}", [128, FT]) for n in ("sig", "sq", "sr", "st4"))
        phi = sb("s7_phi", [33, NF, 128])
        fb = sb("s7_fb", [33, 128])
        gt = sb("s7_gt", [64, NF, 128, 2])
        ps = k.ps("s7_ps", [128, 2, 512], ctx)
        loaded, m_loaded = k.sem("s7_loaded"), [k.sem("s7_m0_loaded"), k.sem("s7_m1_loaded")]
        chain, var_ready, root_ready = k.sem("s7_chain"), k.sem("s7_var_ready"), k.sem("s7_root_ready")
        u_ready, u_stored, m_used = k.sem("s7_u_ready"), k.sem("s7_u_stored"), k.sem("s7_m_used")
        exp_in, exp_done = k.sem("s7_exp_in"), k.sem("s7_exp_done")
        g_done, g_copied, g_stored = k.sem("s7_g_done"), k.sem("s7_g_copied"), k.sem("s7_g_stored")
        m_ready, m_high = k.sem("s7_m_ready"), k.sem("s7_m_high")
        block = ctx.enter_context(nc.Block())
        filters = lambda s: mload[:, s, :].rearrange("d (k e) -> d k e", e=128)
        both = lambda pair, ks: tuple(m[:, ks, :] for m in pair)
        parts = [(both(stu.me, slice(0, FT)), filters(0)), (both(stu.mo, slice(0, FT)), filters(1)),
                 (both(stu.me, slice(FT, FT + 2)), mut[:, 0:3:2, :]), (both(stu.mo, slice(FT, FT + 1)), mut[:, 1:2, :])]

        @block.sync
        def _(sp):
            sp.dma_start(phi[:, :, :], a["phi"]).then_inc(loaded, 16)
            sp.dma_start(fb[:, :], a["filter_dft"]).then_inc(loaded, 16)
            sp.dma_start(lw[:, 0, :], sub(a["log_weights"], 0, [[0, 128], [1, 4]])).then_inc(loaded, 16)
            sp.dma_start(lw[:, 1, :], sub(a["gumbel"], 0, [[0, 128], [1, 4]])).then_inc(loaded, 16)
            sp.dma_start(sig[:, :], sub(a["sigma"], 0, [[0, 128], [1, FT]])).then_inc(loaded, 16)
            sp.dma_start(masks[:, :, :], sub(a["masks"], 0, [[0, 128], [NI, 4], [1, NI]])).then_inc(loaded, 16)
            sp.dma_start(mu[:, :, :, :].rearrange("d i t e -> d (i t) e"),
                         a["M_u"].rearrange("i t d e -> d (i t) e")).then_inc(loaded, 16)
            for j in range(8):
                src = a["M_phi_plus"] if j % 2 == 0 else a["M_phi_minus"]
                if j >= 2:
                    sp.wait_ge(m_used, j - 1)
                sp.dma_start(mload[:, j % 2, :].rearrange("d (k e) -> d k e", e=128),
                             src[j // 2].rearrange("k d e -> d k e")).then_inc(m_loaded[j % 2], 16)
            with sp.Fori(0, NG) as g:
                sp.wait_ge(u_ready, g + 1)
                sp.dma_start(a["u_d"][bass.ds(g * GROUP, GROUP)].rearrange("i h w -> h i w"), ug[:, :, :])\
                  .then_inc(u_stored, 16)
            sp.wait_ge(u_stored, 16 * NG)
            sp.wait_ge(g_copied, 9)
            for c in range(2):
                sp.dma_start(sub(a["tc_d"], c * NF * 256, [[2 * NF * 256, NQ], [1, NF * 256]]),
                             gt[32 * c:32 * c + 32, :, :, :].rearrange("p f x c -> p (f x c)")).then_inc(g_stored, 16)
            sp.wait_ge(g_stored, 32)

        @block.vector
        def _(v):
            link = Chain(v, chain)
            tt = lambda o, x, y, op: link(v.tensor_tensor(o, x, y, op))
            ts = lambda o, x, s1, s2, op0, op1=None: link(v.tensor_scalar(o, x, s1, s2, op0, op1) if op1 is not None
                                                          else v.tensor_scalar(o, x, s1, s2, op0))
            v.wait_ge(loaded, 112)
            tt(z4[:, :], lw[:, 0, :], lw[:, 1, :], ALU.add)
            link(v.tensor_reduce(one[:, 0:1], z4[:, :], AX.X, ALU.max))
            v.tensor_scalar(z4[:, :], z4[:, :], one[:, 0:1], None, ALU.subtract).then_inc(exp_in, 1)
            v.wait_ge(exp_done, 1)
            link(v.tensor_reduce(one[:, 0:1], t4[:, :], AX.X, ALU.add))
            link(v.reciprocal(one[:, 1:2], one[:, 0:1]))
            ts(ys[:, :], t4[:, :], one[:, 1:2], None, ALU.mult)
            link(v.tensor_reduce(one[:, 0:1], ys[:, :], AX.X, ALU.max))
            ts(u4[:, :], ys[:, :], one[:, 0:1], None, ALU.is_equal)
            link(v.memset(one[:, 1:2], 1.0))
            for i in range(4):
                tt(oh[:, i:i + 1], u4[:, i:i + 1], one[:, 1:2], ALU.mult)
                tt(one[:, 1:2], one[:, 1:2], oh[:, i:i + 1], ALU.subtract)
            tt(t4[:, :], oh[:, :], ys[:, :], ALU.subtract)
            tt(t4[:, :], t4[:, :], ys[:, :], ALU.add)
            for i in range(4):
                if i == 0:
                    ts(stu.mask[:, :], masks[:, i, :], oh[:, i:i + 1], None, ALU.mult)
                else:
                    link(v.scalar_tensor_tensor(out=stu.mask[:, :], in0=masks[:, i, :], scalar=oh[:, i:i + 1],
                                                in1=stu.mask[:, :], op0=ALU.mult, op1=ALU.add))
            ts(sq[:, :], sig[:, :], 1.0, None, ALU.mult)
            for n in range(2):
                v.tensor_scalar(s_t[:, :], sq[:, :], 1.0, None, ALU.mult).then_inc(var_ready, 1)
                v.wait_ge(root_ready, n + 1)
                ts(s_t[:, :], sr[:, :], 1e-30, None, ALU.max)
                link(v.reciprocal(s_t[:, :], s_t[:, :]))
                tt(s_t[:, :], s_t[:, :], sq[:, :], ALU.mult)
                tt(s_t[:, :], s_t[:, :], sr[:, :], ALU.add)
                ts(sq[:, :], s_t[:, :], 0.5, None, ALU.mult)
            for j in range(8):
                acc = mp if j % 2 == 0 else mm_
                v.wait_ge(m_loaded[j % 2], 16 * (j // 2) + 16)
                if j < 2:
                    v.tensor_scalar(acc[:, :], mload[:, j % 2, :], t4[:, 0:1], None, ALU.mult).then_inc(m_used, 1)
                else:
                    v.scalar_tensor_tensor(out=acc[:, :], in0=mload[:, j % 2, :], scalar=t4[:, j // 2:j // 2 + 1],
                                           in1=acc[:, :], op0=ALU.mult, op1=ALU.add).then_inc(m_used, 1)
                v.wait_ge(m_used, j + 1)
            for s_, op in enumerate((ALU.add, ALU.subtract)):
                tt(mload[:, s_, :], mp[:, :], mm_[:, :], op)
                tt(filters(s_), filters(s_), sq[:, :].unsqueeze(2).broadcast_to([128, FT, 128]), ALU.mult)
            for i in range(4):
                if i == 0:
                    ts(mut[:, :, :], mu[:, i, :, :], t4[:, 0:1], None, ALU.mult)
                else:
                    link(v.scalar_tensor_tensor(out=mut[:, :, :], in0=mu[:, i, :, :], scalar=t4[:, i:i + 1],
                                                in1=mut[:, :, :], op0=ALU.mult, op1=ALU.add))
            v.memset(one[:, 0:1], 0.0).then_inc(m_ready, 1)
            v.wait_ge(m_high, 1)
            for (high, low), raw in parts:
                v.tensor_tensor(low, raw, high.bitcast(F32), ALU.subtract)
            with v.Fori(0, NI) as i:
                v.bn_stats(st[:, bass.ds(i, 1), :], k.x[:, bass.ds(i, 1), :])
            link(v.memset(tmp[:, :], 0.0))
            row_stats(v, link, st, mean[:, :], var[:, :], tmp[:, :])
            ts(tmp[:, :], var[:, :], 1e-5, None, ALU.add)
            v.tensor_copy(veps[:, :], tmp[:, :]).then_inc(var_ready, 1)
            v.wait_ge(var_ready, 3)
            newton_rsqrt(v, link, veps[:, :], root[:, :], rstd[:, :], tmp[:, :], root_ready, 3)
            with v.Fori(0, NG) as g:
                v.wait_ge(u_stored, 16 * g)
                for i in range(GROUP):
                    o = bass.ds(g * GROUP + i, 1)
                    ins = v.tensor_scalar(ug[:, i, :], k.x[:, o, :], mean[:, o], rstd[:, o], ALU.subtract, ALU.mult)
                ins.then_inc(u_ready, 1)

        @block.scalar
        def _(s):
            s.wait_ge(exp_in, 1)
            s.activation(t4[:, :], z4[:, :], ACT.Exp).then_inc(exp_done, 1)
            for n in range(2):
                s.wait_ge(var_ready, n + 1)
                s.activation(sr[:, :], s_t[:, :], ACT.Sqrt).then_inc(root_ready, 1)
            for n in range(9):
                s.wait_ge(g_done, n + 1)
                for r in range(4):
                    dst = gt[32 * (r // 2):32 * (r // 2) + 32, 4 * n:4 * n + 4, :, r % 2]
                    ins = s.activation(dst, ps[32 * r:32 * r + 32, n % 2, :].rearrange("p (f x) -> p f x", x=128), ACT.Copy)
                ins.then_inc(g_copied, 1)
            s.wait_ge(m_ready, 1)
            for (high, low), raw in parts:
                ins = s.activation(high, raw, ACT.Copy)
            ins.then_inc(m_high, 1)
            s.wait_ge(var_ready, 3)
            s.activation(root[:, :], veps[:, :], ACT.Sqrt).then_inc(root_ready, 1)

        @block.tensor
        def _(pe):
            pe.wait_ge(loaded, 112)
            for n in range(9):
                if n >= 2:
                    pe.wait_ge(g_copied, n - 1)
                pe.matmul(ps[:, n % 2, :], fb[:, :], phi[:, 4 * n:4 * n + 4, :], start=True, stop=True).then_inc(g_done, 1)


def stage_stu_blocks(k, stu):
    nc, a = k.nc, k.a
    with ExitStack() as ctx:
        ug = k.sb("s8_u", [64, 2, GROUP, HW], ctx=ctx)
        xt = k.sb("s8_xt", [128, NQ, 2, 4, 64], ctx=ctx)
        fwd = k.sb("s8_fwd", [64, 2, 128], ctx=ctx)
        ps = k.ps("s8_ps", [128, 2, 2, 4, 128], ctx)
        psl = k.ps("s8_psl", [128, 128], ctx)
        loaded, u_loaded = k.sem("s8_loaded"), [k.sem("s8_u0_loaded"), k.sem("s8_u1_loaded")]
        done, copied, last = k.sem("s8_done"), k.sem("s8_copied"), k.sem("s8_last")
        stored = k.sem("s8_stored")
        block = ctx.enter_context(nc.Block())

        @block.sync
        def _(sp):
            sp.dma_start(fwd[:, :, :], a["block_dft"].rearrange("p (u f) -> p u f", u=2)).then_inc(loaded, 16)
            with sp.Fori(0, 8) as i:
                for u in range(2):
                    sp.wait_ge(done, 2 * i + (1 + u))
                    sp.dma_start(ug[:, u, :, :],
                                 sub(a["u_d"], (2 * i + u) * GROUP * HW, [[PIX, NI], [HW, GROUP], [1, HW]]))\
                      .then_inc(u_loaded[u], 16)
            sp.wait_ge(copied, 2 + 32)
            for n in range(4):
                sp.dma_start(sub(a["xt_d"], n * 8 * 65536, [[512, 128], [65536, 8], [1, 512]]),
                             xt[:, 8 * n:8 * n + 8, :, :, :].rearrange("d q s f t -> d q (s f t)")).then_inc(stored, 16)
            sp.wait_ge(stored, 64)

        @block.tensor
        def _(pe):
            pe.sem_inc(done, 2)
            pe.wait_ge(loaded, 16)
            with pe.Fori(0, 8) as i:
                for u in range(2):
                    pe.wait_ge(u_loaded[u], 16 * i + 16)
                    pe.wait_ge(copied, 4 * i + 2)
                    for j in range(GROUP):
                        mm = pe.matmul(ps[:, u, j % 2, j // 2, :], ug[:, u, j, :], fwd[:, 0, :], start=True, stop=True)
                    mm.then_inc(done, 1)
            pe.matmul(psl[:, :], ug[:, 1, GROUP - 1, :], fwd[:, 1, :], start=True, stop=True).then_inc(last, 1)

        def copy_rows(eng, put, s):
            with eng.Fori(0, 8) as i:
                for u in range(2):
                    eng.wait_ge(done, 2 * i + (u + 3))
                    dst = xt[:, :, s, :, bass.ds((2 * i + u) * 4, 4)].rearrange("d q f t -> d t f q")
                    put(dst, ps[:, u, s, :, :].rearrange("d t (f q) -> d t f q", q=NQ)).then_inc(copied, 1)

        @block.vector
        def _(v):
            v.sem_inc(copied, 2)
            copy_rows(v, v.tensor_copy, 1)

        @block.scalar
        def _(s):
            copy_rows(s, lambda o, x: s.activation(o, x, ACT.Copy), 0)
            s.wait_ge(last, 1)
            s.activation(stu.xl[:, :], psl[:, :], ACT.Copy)


def stage_stu_filter(k, stu):
    nc, a = k.nc, k.a
    CH = [4, 4, 4, 4, 2]
    NC = len(CH)
    UN = 8 * NC
    BANKS = 5
    with ExitStack() as ctx:
        sb = lambda name, shape, dt=F32: k.sb(name, shape, dt, ctx=ctx)
        raw = sb("s9_raw", [128, 2, 8, 128])
        tc = [sb(f"s9_tc_{n}", [128, 2, 8, 128], F32R) for n in ("high", "low")]
        xq = sb("s9_xq", [128, 2, 2, 4, 64])
        xs = [sb(f"s9_xs_{n}", [128, 2, 3, 4, 64], F32R) for n in ("high", "low")]
        w = [sb(f"s9_w_{n}", [128, 2, 4, 2, 2, B, 128], F32R) for n in ("high", "low")]
        y = sb("s9_y", [128, 2, 512])
        psw = k.ps("s9_psw", [128, BANKS, 512], ctx)
        psy = k.ps("s9_psy", [128, 2, 512], ctx)
        raw_loaded, xq_loaded = [k.sem(f"s9_raw{u}_loaded") for u in range(2)], [k.sem(f"s9_xq{u}_loaded") for u in range(2)]
        y_stored = [k.sem(f"s9_y{u}_stored") for u in range(2)]
        xs_high, xs_ready = k.sem("s9_xs_high"), k.sem("s9_xs_ready")
        w_done, w_high, w_ready = k.sem("s9_w_done"), k.sem("s9_w_high"), k.sem("s9_w_ready")
        tc_high, tc_ready = k.sem("s9_tc_high"), k.sem("s9_tc_ready")
        filt_done, y_copied = k.sem("s9_filt_done"), k.sem("s9_y_copied")
        block = ctx.enter_context(nc.Block())

        def source(p, s):
            return s if p == 0 else 2 - 2 * s

        def passes(mm, out, lhs, rhs, start, stop):
            mm(out, lhs[0], rhs[0], start=start, stop=False)
            mm(out, lhs[1], rhs[0], start=False, stop=False)
            return mm(out, lhs[0], rhs[1], start=False, stop=stop)

        @block.sync
        def _(sp):
            for u in range(2):
                sp.sem_inc(y_stored[u], 1)
            with sp.Fori(0, NQ // 2) as i:
                for u in range(2):
                    q = 2 * i + u
                    sp.wait_ge(xs_ready, q + 1)
                    sp.dma_start(xq[:, u, :, :, :].rearrange("d s f t -> d (s f t)"),
                                 sub(a["xt_d"], q * 65536, [[512, 128], [1, 512]])).then_inc(xq_loaded[u], 16)
                    for c in range(NC):
                        n = u * NC + c
                        sp.wait_ge(tc_ready, i * (2 * NC) + (n + 1))
                        for h in range(2):
                            sp.dma_start(raw[64 * h:64 * h + 64, n % 2, 0:2 * CH[c], :],
                                         sub(a["tc_d"], (2 * q + h) * (NF * 256) + c * (8 * 256),
                                             [[2, 64], [256, 2 * CH[c]], [1, 128]])).then_inc(raw_loaded[n % 2], 16)
            for u in range(2):
                sp.wait_ge(y_stored[u], 16 * NQ + 1)

        @block.gpsimd
        def _(p):
            xl = stu.xl[:, :].rearrange("d (f q) -> d f q", f=4)

            def split(u, q, turn):
                p.wait_ge(xq_loaded[u], turn)
                p.tensor_copy(xs[0][:, u, 2, :, 0:1], xl[:, :, bass.ds(q, 1)])
                p.tensor_copy(xs[0][:, u, 0:2, :, :], xq[:, u, :, :, :])
                p.tensor_copy(xs[0][:, u, 2, :, 1:64], xq[:, u, 1, :, 0:63]).then_inc(xs_high, 1)
                p.wait_ge(xs_high, q + 1)
                high = xs[0][:, :, :, :, :].bitcast(F32)
                p.tensor_tensor(xs[1][:, u, 0:2, :, :], xq[:, u, :, :, :], high[:, u, 0:2, :, :], ALU.subtract)
                p.tensor_tensor(xs[1][:, u, 2, :, 1:64], xq[:, u, 1, :, 0:63], high[:, u, 2, :, 1:64], ALU.subtract)
                p.tensor_tensor(xs[1][:, u, 2, :, 0:1], xl[:, :, bass.ds(q, 1)], high[:, u, 2, :, 0:1], ALU.subtract)\
                 .then_inc(xs_ready, 1)

            p.sem_inc(xs_ready, 2)
            split(0, 0, 16)
            split(1, 1, 16)
            with p.Fori(0, NQ // 2 - 1) as i:
                for u in range(2):
                    p.wait_ge(w_done, (2 * i + u) * UN + UN)
                    split(u, 2 * i + (u + 2), 16 * i + 32)

        @block.tensor
        def _(pe):
            pe.sem_inc(filt_done, 2)
            with pe.Fori(0, NQ // 2) as i:
                for u in range(2):
                    q = 2 * i + u
                    pe.wait_ge(xs_ready, q + 3)
                    for c in range(NC + 1):
                        if c < NC:
                            for j in range(8):
                                pr, s, b = j // 4, j // 2 % 2, j % 2
                                n = 8 * c + j
                                pe.wait_ge(w_ready, q * UN + (n + 1))
                                m = stu.me if pr == 0 else stu.mo
                                kk = CH[c] - (c == NC - 1) * pr
                                passes(pe.matmul, psw[:, n % BANKS, 0:128 * kk],
                                       [x[:, u, source(pr, s), 2 * b:2 * b + 2, :] for x in xs],
                                       [x[:, 4 * c:4 * c + kk, :] for x in m], True, True).then_inc(w_done, 1)
                        if c == 1:
                            pe.wait_ge(y_copied, q + 1)
                        if c > 0:
                            g = c - 1
                            slot = (u * NC + g) % 2
                            pe.wait_ge(tc_ready, q * NC + (g + 3))
                            pe.wait_ge(w_ready, q * UN + (8 * c + BANKS))
                            for kk in range(CH[g]):
                                for pr in range(2):
                                    f = 2 * (4 * g + kk) + pr
                                    if f == NF - 1:
                                        continue
                                    mm = passes(pe.matmul, psy[:, u, :], [x[:, slot, 2 * kk + pr, :] for x in tc],
                                                [x[:, slot, kk, pr, :, :, :] for x in w], f == 0, f == NF - 2)
                            mm.then_inc(filt_done, 1)

        def products(c):
            for j in range(8):
                pr, s, b = j // 4, j // 2 % 2, j % 2
                yield 8 * c + j, CH[c] - (c == NC - 1) * pr, (pr, s, b)

        @block.scalar
        def _(s):
            s.sem_inc(y_copied, 2)
            with s.Fori(0, NQ // 2) as i:
                for u in range(2):
                    q = 2 * i + u
                    for c in range(NC):
                        n = u * NC + c
                        s.wait_ge(filt_done, i * (2 * NC) + (n + 1))
                        s.wait_ge(raw_loaded[n % 2], 32 * NC * i + 32 * (n // 2 + 1))
                        s.activation(tc[0][:, n % 2, 0:2 * CH[c], :], raw[:, n % 2, 0:2 * CH[c], :], ACT.Copy)\
                         .then_inc(tc_high, 1)
                        for m, kk, at in products(c):
                            s.wait_ge(w_done, q * UN + (m + 1))
                            s.activation(w[0][:, n % 2, 0:kk, at[0], at[1], at[2], :],
                                         psw[:, m % BANKS, 0:128 * kk].rearrange("p (k e) -> p k e", e=128),
                                         ACT.Copy).then_inc(w_high, 1)
                    s.wait_ge(filt_done, q * NC + (NC + 2))
                    s.wait_ge(y_stored[u], 32 * i + 1)
                    s.activation(y[:, u, :], psy[:, u, :], ACT.Copy).then_inc(y_copied, 1)
                    s.wait_ge(y_copied, q + 3)
                    for c in range(2):
                        s.dma_start(sub(a["yh_d"], (2 * q + c) * (64 * 512), [[512, 64], [1, 512]]), y[c::2, u, :])\
                         .then_inc(y_stored[u], 16)

        @block.vector
        def _(v):
            v.sem_inc(w_ready, BANKS)
            v.sem_inc(tc_ready, 2)
            with v.Fori(0, NQ // 2) as i:
                for u in range(2):
                    q = 2 * i + u
                    for c in range(NC):
                        n = u * NC + c
                        v.wait_ge(tc_high, i * (2 * NC) + (n + 1))
                        raw_c, high = raw[:, n % 2, 0:2 * CH[c], :], tc[0][:, n % 2, 0:2 * CH[c], :]
                        v.tensor_tensor(tc[1][:, n % 2, 0:2 * CH[c], :], raw_c, high.bitcast(F32), ALU.subtract)\
                         .then_inc(tc_ready, 1)
                        for m, kk, at in products(c):
                            v.wait_ge(w_high, q * UN + (m + 1))
                            v.tensor_tensor(w[1][:, n % 2, 0:kk, at[0], at[1], at[2], :],
                                            psw[:, m % BANKS, 0:128 * kk].rearrange("p (k e) -> p k e", e=128),
                                            w[0][:, n % 2, 0:kk, at[0], at[1], at[2], :].bitcast(F32),
                                            ALU.subtract).then_inc(w_ready, 1)


def stage_stu_output(k, stu):
    nc, a = k.nc, k.a
    with ExitStack() as ctx:
        sb = lambda name, shape: k.sb(name, shape, ctx=ctx)
        zq = sb("s10_zq", [128, 2, 16, HW])
        yn = sb("s10_yn", [64, 2, 16, HW])
        inv = sb("s10_inv", [128, 64])
        yg = sb("s10_yg", [128, 2, GROUP, HW])
        ps = k.ps("s10_ps", [64, 2, 16, HW], ctx)
        loaded, z_loaded = k.sem("s10_loaded"), [k.sem(f"s10_z{u}_loaded") for u in range(2)]
        done, copied, stored = k.sem("s10_done"), k.sem("s10_copied"), k.sem("s10_stored")
        y_loaded, added = [k.sem(f"s10_y{u}_loaded") for u in range(2)], k.sem("s10_added")
        block = ctx.enter_context(nc.Block())

        @block.sync
        def _(sp):
            sp.dma_start(inv[:, :], a["block_idft"]).then_inc(loaded, 16)
            with sp.Fori(0, 4) as i:
                for u in range(2):
                    sp.wait_ge(done, 2 * i)
                    for b in range(B):
                        for c in range(2):
                            sp.dma_start(zq[64 * b + 32 * c:64 * b + 32 * c + 32, u, :, :],
                                         sub(a["yh_d"], c * 32768 + b * 128 + (2 * i + u) * (8 * 512),
                                             [[65536, NQ], [256, 16], [1, 128]])).then_inc(z_loaded[u], 16)
            sp.wait_ge(stored, 16 * 8)
            with sp.Fori(0, 4) as i:
                for u in range(2):
                    sp.wait_ge(added, 2 * i)
                    sp.dma_start(yg[:, u, :, :],
                                 a["y_d"][bass.ds((2 * i + u) * GROUP, GROUP)].rearrange("i h w -> h i w"))\
                      .then_inc(y_loaded[u], 16)
            sp.wait_ge(added, 8)

        @block.tensor
        def _(pe):
            pe.wait_ge(loaded, 16)
            with pe.Fori(0, 4) as i:
                for u in range(2):
                    pe.wait_ge(z_loaded[u], 64 * i + 64)
                    pe.wait_ge(copied, 2 * i)
                    for j in range(0, 16, 4):
                        mm = pe.matmul(ps[:, u, j:j + 4, :], inv[:, :], zq[:, u, j:j + 4, :], start=True, stop=True)
                    mm.then_inc(done, 1)

        @block.scalar
        def _(s):
            with s.Fori(0, 4) as i:
                for u in range(2):
                    s.wait_ge(done, 2 * i + (u + 1))
                    s.wait_ge(stored, 32 * i)
                    for j in range(8):
                        ins = s.activation(yn[:, u, 14 - 2 * j:16 - 2 * j, :], ps[:, u, 2 * j:2 * j + 2, :], ACT.Copy)
                    ins.then_inc(copied, 1)
                    s.wait_ge(copied, 2 * i + (u + 1))
                    s.dma_start(sub(a["y_d"], (112 - 16 * (2 * i + u)) * HW, [[PIX, NI], [HW, 16], [1, HW]]), yn[:, u, :, :])\
                     .then_inc(stored, 16)

        @block.vector
        def _(v):
            with v.Fori(0, 4) as i:
                for u in range(2):
                    v.wait_ge(y_loaded[u], 16 * i + 16)
                    for j in range(GROUP):
                        o = bass.ds((2 * i + u) * GROUP + j, 1)
                        ins = v.scalar_tensor_tensor(out=k.x[:, o, :], in0=yg[:, u, j, :], scalar=stu.mask[:, o],
                                                     in1=k.x[:, o, :], op0=ALU.mult, op1=ALU.add)
                    ins.then_inc(added, 1)


class Stu:

    def __init__(self, k, ctx):
        pair = lambda name, n: tuple(k.sb(f"stu_{name}_{part}", [128, n, 128], F32R, ctx=ctx) for part in ("high", "low"))
        self.mask = k.sb("stu_mask", [128, NI], ctx=ctx)
        self.xl = k.sb("stu_xl", [128, 128], ctx=ctx)
        self.me = pair("me", NK)
        self.mo = pair("mo", NK - 1)


def v_row_norm(v, link, x, st, mean, var, rstd, root, tmp, eps, var_ready, root_ready):
    with v.Fori(0, NI) as i:
        v.bn_stats(st[:, bass.ds(i, 1), :], x[:, bass.ds(i, 1), :])
    link(v.memset(tmp, 0.0))
    row_stats(v, link, st, mean, var, tmp)
    link(v.tensor_scalar(tmp, var, eps, None, ALU.add))
    v.tensor_copy(var, tmp).then_inc(var_ready, 1)
    v.wait_ge(var_ready, 1)
    newton_rsqrt(v, link, var, root, rstd, tmp, root_ready, 1)


WU = 13
PADW = HW + 6
GAIN = float(np.sqrt(2.0))


def stage_resample_conv(k):
    nc, a = k.nc, k.a
    ROUNDS = NI // 8
    with ExitStack() as ctx:
        sb = lambda name, shape, dt=F32: k.sb(name, shape, dt, ctx=ctx)
        pair = lambda name, shape: [sb(f"{name}_{part}", shape, F32R) for part in ("high", "low")]
        st = sb("s11_st", [128, NI, 6])
        mean, var, rstd, root, tmp, bias = (sb(f"s11_{n}", [128, NI]) for n in ("mean", "var", "rstd", "root", "tmp", "bias"))
        v_raw = sb("s11_v_raw", [128, 2, 4, HW])
        v_in = pair("s11_v", [128, 2, 4, PADW])
        m_raw = sb("s11_m_raw", [128, 4, 4, HW])
        mid = pair("s11_mid", [128, 2, 4, 4, PADW])
        up_f, dn_f = sb("s11_upf", [TAPS, TAPS]), sb("s11_dnf", [TAPS, TAPS])
        sel = sb("s11_sel", [TAPS, WU])
        pu, pd = sb("s11_pu", [TAPS, 512]), sb("s11_pd", [TAPS, 512])
        upc = sb("s11_upc", [TAPS, WU])
        gu, gd = sb("s11_gu", [WU, 512]), sb("s11_gd", [TAPS, 512])
        bands = sb("s11_bands", [128, 2 * WU + 2 * TAPS, 128])
        band = pair("s11_band", [128, 2 * WU + 2 * TAPS, 128])
        bu, bd = [t[:, 0:2 * WU, :] for t in band], [t[:, 2 * WU:, :] for t in band]
        ps_m = k.ps("s11_psm", [128, 4, 512], ctx)
        ps_z = k.ps("s11_psz", [128, 2, 512], ctx)
        loaded, taps_done, taps_copied = k.sem("s11_loaded"), k.sem("s11_taps_done"), k.sem("s11_taps_copied")
        bands_stored, bands_loaded = k.sem("s11_bands_stored"), k.sem("s11_bands_loaded")
        bands_high, bands_ready = k.sem("s11_bands_high"), k.sem("s11_bands_ready")
        chain, var_ready, root_ready = k.sem("s11_chain"), k.sem("s11_var_ready"), k.sem("s11_root_ready")
        v_normed, v_high, v_ready, padded = k.sem("s11_v_normed"), k.sem("s11_v_high"), k.sem("s11_v_ready"), k.sem("s11_padded")
        mid_done, mid_copied, mid_leaky = k.sem("s11_mid_done"), k.sem("s11_mid_copied"), k.sem("s11_mid_leaky")
        mid_high, mid_ready = k.sem("s11_mid_high"), k.sem("s11_mid_ready")
        z_done, z_added = k.sem("s11_z_done"), k.sem("s11_z_added")
        block = ctx.enter_context(nc.Block())

        def passes(mm, out, lhs, rhs, start, stop):
            mm(out, lhs[0], rhs[0], start=start, stop=False)
            mm(out, lhs[1], rhs[0], start=False, stop=False)
            return mm(out, lhs[0], rhs[1], start=False, stop=stop)

        @block.sync
        def _(sp):
            for t, n in ((up_f, "up_t"), (dn_f, "dn"), (sel, "up_sel"), (pu, "up_pos"), (pd, "dn_pos")):
                sp.dma_start(t[:, :], a[n]).then_inc(loaded, 16)
            sp.dma_start(bias[:, :], sub(a["bias"], 0, [[0, 128], [1, NI]])).then_inc(loaded, 16)
            sp.wait_ge(taps_copied, 3)
            sp.dma_start(a["gu_d"], gu[:, :]).then_inc(bands_stored, 16)
            sp.dma_start(a["gd_d"], gd[:, :]).then_inc(bands_stored, 16)
            sp.wait_ge(bands_stored, 32)
            sp.dma_start(bands[:, 0:2 * WU, :], sub(a["gu_d"], 0, [[1, 128], [256, 2 * WU], [1, 128]]))\
              .then_inc(bands_loaded, 16)
            sp.dma_start(bands[:, 2 * WU:, :], sub(a["gd_d"], 0, [[1, 128], [256, 2 * TAPS], [1, 128]]))\
              .then_inc(bands_loaded, 16)
            sp.wait_ge(bands_loaded, 32)

        @block.gpsimd
        def _(p):
            for t in v_in:
                p.memset(t[:, :, :, :].bitcast(F32), 0.0).then_inc(padded, 1)
            for t in mid:
                p.memset(t[:, :, :, :, :].bitcast(F32), 0.0).then_inc(padded, 1)

        @block.vector
        def _(v):
            link = Chain(v, chain)

            def norm_rows(u, first, n):
                for j in range(4):
                    o = bass.ds(first + j, 1)
                    ins = v.tensor_scalar(v_raw[:, u, j, :], k.x[:, o, :], rstd[:, o], bias[:, o], ALU.mult, ALU.add)
                ins.then_inc(v_normed, 1)
                v.wait_ge(v_high, n)
                v.tensor_tensor(v_in[1][:, u, :, 3:3 + HW], v_raw[:, u, :, :],
                                v_in[0][:, u, :, 3:3 + HW].bitcast(F32), ALU.subtract).then_inc(v_ready, 1)

            def low(i, m):
                v.wait_ge(mid_high, 8 * i + (m + 1))
                v.tensor_tensor(mid[1][:, m // 4, m % 4, :, 3:3 + HW], m_raw[:, m % 4, :, :],
                                mid[0][:, m // 4, m % 4, :, 3:3 + HW].bitcast(F32), ALU.subtract).then_inc(mid_ready, 1)

            def round_(i, last):
                for m in range(8):
                    v.wait_ge(mid_copied, 8 * i + (m + 5))
                    y = m_raw[:, m % 4, :, :]
                    v.scalar_tensor_tensor(out=y, in0=y, scalar=0.2, in1=y, op0=ALU.mult, op1=ALU.max)\
                     .then_inc(mid_leaky, 1)
                    if m:
                        low(i, m - 1)
                low(i, 7)
                if not last:
                    for u in range(2):
                        norm_rows(u, 8 * i + (8 + 4 * u), 2 * i + (u + 3))
                for u in range(2):
                    v.wait_ge(z_done, 2 * i + (u + 2))
                    xg = k.x[:, bass.ds((2 * i + u) * 4, 4), :]
                    v.tensor_tensor(xg, ps_z[:, u, :].rearrange("p (i w) -> p i w", w=HW), xg, ALU.add).then_inc(z_added, 1)

            v_row_norm(v, link, k.x, st, mean[:, :], var[:, :], rstd[:, :], root[:, :], tmp[:, :], 1e-6, var_ready, root_ready)
            v.wait_ge(loaded, 96)
            link(v.tensor_tensor(tmp[:, :], mean[:, :], rstd[:, :], ALU.mult))
            link(v.tensor_tensor(bias[:, :], bias[:, :], tmp[:, :], ALU.subtract))
            v.wait_ge(bands_high, 1)
            v.tensor_tensor(band[1][:, :, :], bands[:, :, :], band[0][:, :, :].bitcast(F32), ALU.subtract).then_inc(bands_ready, 1)
            v.wait_ge(padded, 4)
            v.sem_inc(mid_ready, 4)
            v.sem_inc(z_added, 2)
            for u in range(2):
                norm_rows(u, 4 * u, u + 1)
            with v.Fori(0, ROUNDS - 1) as i:
                round_(i, False)
            round_(ROUNDS - 1, True)

        @block.scalar
        def _(s):
            def high_rows(u, n):
                s.wait_ge(v_normed, n)
                s.activation(v_in[0][:, u, :, 3:3 + HW], v_raw[:, u, :, :], ACT.Copy).then_inc(v_high, 1)

            def high(i, m):
                s.wait_ge(mid_leaky, 8 * i + (m + 1))
                s.activation(mid[0][:, m // 4, m % 4, :, 3:3 + HW], m_raw[:, m % 4, :, :], ACT.Copy).then_inc(mid_high, 1)

            def round_(i, last):
                s.wait_ge(z_done, 2 * i + 1)
                for m in range(8):
                    s.wait_ge(mid_done, 8 * i + (m + 1))
                    s.wait_ge(mid_ready, 8 * i + (m + 1))
                    s.activation(m_raw[:, m % 4, :, :], ps_m[:, m % 4, :].rearrange("p (i w) -> p i w", w=HW), ACT.Copy,
                                 scale=GAIN).then_inc(mid_copied, 1)
                    if m:
                        high(i, m - 1)
                high(i, 7)
                if not last:
                    for u in range(2):
                        high_rows(u, 2 * i + (u + 3))

            s.wait_ge(taps_done, 1)
            s.activation(upc[:, :], ps_m[0:TAPS, 0, 0:WU], ACT.Copy).then_inc(taps_copied, 1)
            s.wait_ge(taps_done, 3)
            s.activation(gu[:, :], ps_m[0:WU, 1, :], ACT.Copy).then_inc(taps_copied, 1)
            s.activation(gd[:, :], ps_m[0:TAPS, 2, :], ACT.Copy).then_inc(taps_copied, 1)
            s.wait_ge(var_ready, 1)
            s.activation(root[:, :], var[:, :], ACT.Sqrt).then_inc(root_ready, 1)
            s.wait_ge(bands_loaded, 32)
            s.activation(band[0][:, :, :], bands[:, :, :], ACT.Copy).then_inc(bands_high, 1)
            s.wait_ge(padded, 4)
            s.sem_inc(mid_copied, 4)
            for u in range(2):
                high_rows(u, u + 1)
            with s.Fori(0, ROUNDS - 1) as i:
                round_(i, False)
            round_(ROUNDS - 1, True)

        @block.tensor
        def _(pe):
            pe.wait_ge(loaded, 96)
            pe.matmul(ps_m[0:TAPS, 0, 0:WU], up_f[:, :], sel[:, :], start=True, stop=True).then_inc(taps_done, 1)
            pe.matmul(ps_m[0:TAPS, 2, :], dn_f[:, :], pd[:, :], start=True, stop=True).then_inc(taps_done, 1)
            pe.wait_ge(taps_copied, 1)
            pe.matmul(ps_m[0:WU, 1, :], upc[:, :], pu[:, :], start=True, stop=True).then_inc(taps_done, 1)
            pe.wait_ge(taps_copied, 3)
            pe.wait_ge(bands_ready, 1)
            pe.sem_inc(z_done, 1)
            with pe.Fori(0, ROUNDS) as i:
                for u in range(2):
                    pe.wait_ge(v_ready, 2 * i + (u + 1))
                    for pq in range(4):
                        p, q = pq // 2, pq % 2
                        pe.wait_ge(mid_copied, 8 * i + (4 * u + pq + 1))
                        shifts = list(range(-3, 4)) if q == 0 else list(range(-2, 4))
                        for n, dc in enumerate(shifts):
                            mm = passes(pe.matmul, ps_m[:, pq, :], [t[:, 2 * (7 * q + n) + p, :] for t in bu],
                                        [t[:, u, :, 3 + dc:3 + dc + HW] for t in v_in], n == 0, n == len(shifts) - 1)
                        mm.then_inc(mid_done, 1)
                for u in range(2):
                    pe.wait_ge(mid_ready, 8 * i + (4 * u + 8))
                    pe.wait_ge(z_added, 2 * i + (u + 1))
                    for n in range(2 * TAPS):
                        j, p = n // 2, n % 2
                        q = 0 if j % 2 else 1
                        dc = (j - 5 - q) // 2
                        mm = passes(pe.matmul, ps_z[:, u, :], [t[:, n, :] for t in bd],
                                    [t[:, u, 2 * p + q, :, 3 + dc:3 + dc + HW] for t in mid], n == 0, n == 2 * TAPS - 1)
                    mm.then_inc(z_done, 1)


def stage_experts(k):
    nc, a = k.nc, k.a
    STEPS = NI // 8
    EG = 128 // EXP
    with ExitStack() as ctx:
        sb = lambda name, shape, dt=F32: k.sb(name, shape, dt, ctx=ctx)
        pair = lambda name, shape: [sb(f"{name}_{part}", shape, F32R) for part in ("high", "low")]
        st = sb("s12_st", [128, NI, 6])
        mean, var, rstd, root, tmp = (sb(f"s12_{n}", [128, NI]) for n in ("mean", "var", "rstd", "root", "tmp"))
        tn = sb("s12_tn", [128, 2, 4, HW])
        tt_ = pair("s12_tt", [128, 2, 4, HW])
        tt_all = [sb(f"s12_tt_all_{part}", [128, NI, HW]) for part in ("high", "low")]
        w_raw = sb("s12_w_raw", [128, EXP * 128 + EXP])
        w = pair("s12_w", [128, EXP * 128 + EXP])
        rb, order = sb("s12_rb", [128, EXP]), sb("s12_order", [128, EXP])
        eb = sb("s12_eb", [128, EG * 128])
        lg, ex, eq, oh, g1 = (sb(f"s12_{n}", [128, NI, EXP]) for n in ("lg", "ex", "eq", "oh", "g1"))
        m0, m1, m2, r0 = (sb(f"s12_{n}", [128, NI]) for n in ("m0", "m1", "m2", "r0"))
        gt = sb("s12_gt", [128, NI // EG, 128])
        part_a, part_b = sb("s12_part_a", [128, 4, 4, HW]), sb("s12_part_b", [128, 4, 4, HW])
        half, quarter = sb("s12_half", [128, 4, 2, HW]), sb("s12_quarter", [128, 2, 4, HW])
        ps_t = k.ps("s12_pst", [128, 2, 4, 128], ctx)
        ps_l = k.ps("s12_psl", [128, NI, EXP], ctx)
        ps_e = k.ps("s12_pse", [128, 2, 2, 4, 128], ctx)
        loaded, chain = k.sem("s12_loaded"), k.sem("s12_chain")
        w_high, w_ready = k.sem("s12_w_high"), k.sem("s12_w_ready")
        var_ready, root_ready = k.sem("s12_var_ready"), k.sem("s12_root_ready")
        tn_ready, turned = k.sem("s12_tn_ready"), k.sem("s12_turned")
        tt_high, tt_ready, logits = k.sem("s12_tt_high"), k.sem("s12_tt_ready"), k.sem("s12_logits")
        kept = [k.sem(f"s12_kept{u}") for u in range(2)]
        exp_in, exp_done, gates, gt_done = k.sem("s12_exp_in"), k.sem("s12_exp_done"), k.sem("s12_gates"), k.sem("s12_gt_done")
        gt_copied, base, based = k.sem("s12_gt_copied"), k.sem("s12_base"), k.sem("s12_based")
        fetched = [k.sem(f"s12_fetched{u}") for u in range(2)]
        exp_ready, a_scaled, b_scaled = k.sem("s12_exp_ready"), k.sem("s12_a_scaled"), k.sem("s12_b_scaled")
        joined, halved, quartered = k.sem("s12_joined"), k.sem("s12_halved"), k.sem("s12_quartered")
        used, out_stored = k.sem("s12_used"), k.sem("s12_out_stored")
        block = ctx.enter_context(nc.Block())
        NE = EXP * 128

        def passes(mm, out, lhs, rhs):
            mm(out, lhs[0], rhs[0], start=True, stop=False)
            mm(out, lhs[1], rhs[0], start=False, stop=False)
            return mm(out, lhs[0], rhs[1], start=False, stop=True)

        @block.sync
        def _(sp):
            sp.dma_start(w_raw[:, 0:NE].rearrange("d (e c) -> d e c", c=128), a["expert_w"].rearrange("e d c -> d e c"))\
              .then_inc(loaded, 16)
            sp.dma_start(w_raw[:, NE:], a["router_w"]).then_inc(loaded, 16)
            sp.dma_start(rb[:, :], sub(a["router_b"], 0, [[0, 128], [1, EXP]])).then_inc(loaded, 16)
            sp.dma_start(order[:, :], sub(a["order"], 0, [[0, 128], [1, EXP]])).then_inc(loaded, 16)
            sp.dma_start(eb[:, :], a["expert_b"]).then_inc(loaded, 16)
            with sp.Fori(0, STEPS) as i:
                for u in range(2):
                    sp.wait_ge(tt_ready, 2 * i + (u + 3))
                    for h in range(2):
                        sp.dma_start(tt_all[h][:, bass.ds((2 * i + u) * 4, 4), :], tt_[h][:, u, :, :].bitcast(F32)).then_inc(kept[u], 16)
            for u in range(2):
                sp.wait_ge(kept[u], 1 + 32 * STEPS)
            sp.wait_ge(logits, 2 + 2 * STEPS)

            def fetch(i, first):
                for u in range(2):
                    sp.wait_ge(exp_ready, first + 8 * u)
                    for h in range(2):
                        sp.dma_start(tt_[h][:, u, :, :].bitcast(F32), tt_all[h][:, bass.ds((2 * i + u) * 4, 4), :])\
                          .then_inc(fetched[u], 16)

            def store(i):
                sp.wait_ge(used, 2 * i + 4)
                sp.dma_start(a["out"][bass.ds(8 * i, 8)].rearrange("i h w -> h i w"), k.x[:, bass.ds(8 * i, 8), :])\
                  .then_inc(out_stored, 16)

            fetch(0, 1)
            with sp.Fori(0, STEPS - 1) as i:
                fetch(i + 1, 16 * i + 17)
                store(i)
            store(STEPS - 1)
            sp.wait_ge(out_stored, 16 * STEPS)

        @block.vector
        def _(v):
            link = Chain(v, chain)
            tt = lambda o, x, y, op: link(v.tensor_tensor(o, x, y, op))
            wide = lambda t: t.unsqueeze(2).broadcast_to([128, NI, EXP])
            each = lambda t: t.unsqueeze(1).broadcast_to([128, NI, EXP])
            v_row_norm(v, link, k.x, st, mean[:, :], var[:, :], rstd[:, :], root[:, :], tmp[:, :], 1e-5, var_ready, root_ready)
            v.wait_ge(w_high, 1)
            v.tensor_tensor(w[1][:, :], w_raw[:, :], w[0][:, :].bitcast(F32), ALU.subtract).then_inc(w_ready, 1)

            def norm_rows(u, first):
                for j in range(4):
                    o = bass.ds(first + j, 1)
                    ins = v.tensor_scalar(tn[:, u, j, :], k.x[:, o, :], mean[:, o], rstd[:, o], ALU.subtract, ALU.mult)
                ins.then_inc(tn_ready, 1)

            def turn_low(i, last):
                for u in range(2):
                    v.wait_ge(tt_high, 2 * i + (u + 1))
                    v.tensor_tensor(tt_[1][:, u, :, :], ps_t[:, u, :, :], tt_[0][:, u, :, :].bitcast(F32), ALU.subtract)\
                     .then_inc(tt_ready, 1)
                    if not last:
                        norm_rows(u, 8 * i + (8 + 4 * u))

            v.sem_inc(tt_ready, 2)
            for u in range(2):
                norm_rows(u, 4 * u)
            with v.Fori(0, STEPS - 1) as i:
                turn_low(i, False)
            turn_low(STEPS - 1, True)

            v.wait_ge(logits, 2 + 2 * STEPS)
            tt(lg[:, :, :], ps_l[:, :, :], each(rb[:, :]), ALU.add)
            link(v.tensor_reduce(m0[:, :], lg[:, :, :], AX.X, ALU.max))
            v.tensor_tensor(lg[:, :, :], lg[:, :, :], wide(m0[:, :]), ALU.subtract).then_inc(exp_in, 1)
            v.wait_ge(exp_done, 1)
            link(v.tensor_reduce(m0[:, :], ex[:, :, :], AX.X, ALU.add))
            link(v.reciprocal(r0[:, :], m0[:, :]))
            tt(ex[:, :, :], ex[:, :, :], wide(r0[:, :]), ALU.mult)
            for n, m in enumerate((m1, m2)):
                link(v.tensor_reduce(m[:, :], ex[:, :, :], AX.X, ALU.max))
                tt(eq[:, :, :], ex[:, :, :], wide(m[:, :]), ALU.is_equal)
                tt(eq[:, :, :], eq[:, :, :], each(order[:, :]), ALU.mult)
                link(v.tensor_reduce(r0[:, :], eq[:, :, :], AX.X, ALU.max))
                tt(oh[:, :, :], eq[:, :, :], wide(r0[:, :]), ALU.is_equal)
                if n == 0:
                    tt(g1[:, :, :], oh[:, :, :], wide(m[:, :]), ALU.mult)
                    link(v.scalar_tensor_tensor(out=ex[:, :, :], in0=oh[:, :, :], scalar=-2.0, in1=ex[:, :, :],
                                                op0=ALU.mult, op1=ALU.add))
                else:
                    tt(oh[:, :, :], oh[:, :, :], wide(m[:, :]), ALU.mult)
            tt(m1[:, :], m1[:, :], m2[:, :], ALU.add)
            link(v.reciprocal(r0[:, :], m1[:, :]))
            tt(g1[:, :, :], g1[:, :, :], oh[:, :, :], ALU.add)
            v.tensor_tensor(g1[:, :, :], g1[:, :, :], wide(r0[:, :]), ALU.mult).then_inc(gates, 1)
            v.wait_ge(gates, 1)
            for n in range(NI // 4):
                v.wait_ge(base, n + 1)
                v.tensor_tensor(k.x[:, 4 * n:4 * n + 4, :], ps_t[:, n % 2, :, :], k.x[:, 4 * n:4 * n + 4, :], ALU.add)\
                 .then_inc(based, 1)
            v.sem_inc(a_scaled, 2)
            v.sem_inc(used, 2)

            def join(i, j):
                v.wait_ge(a_scaled, 8 * i + (j + 3))
                v.wait_ge(b_scaled, 8 * i + (j + 3))
                v.tensor_tensor(part_a[:, j % 4, :, :], part_a[:, j % 4, :, :], part_b[:, j % 4, :, :], ALU.add)\
                 .then_inc(joined, 1)

            def add_rows(u, step):
                v.wait_ge(quartered, 4 * step + 4)
                xg = k.x[:, bass.ds(4 * step, 4), :]
                v.tensor_tensor(xg, quarter[:, u, :, :], xg, ALU.add).then_inc(used, 1)

            def round_(i, first):
                for j in range(8):
                    v.wait_ge(exp_ready, 16 * i + (2 * j + 10))
                    v.wait_ge(halved, 8 * i + (j + 1))
                    v.tensor_tensor(part_a[:, j % 4, :, :], ps_e[:, j % 2, 0, :, :],
                                    g1[:, bass.ds(8 * i + j, 1), 0:4].rearrange("p i e -> p (i e)").unsqueeze(2)
                                    .broadcast_to([128, 4, HW]), ALU.mult).then_inc(a_scaled, 1)
                    if j:
                        join(i, j - 1)
                    if j == 2 and not first:
                        add_rows(1, i * 2 - 1)
                    if j == 6:
                        add_rows(0, i * 2)
                join(i, 7)

            round_(0, True)
            with v.Fori(0, STEPS - 1) as i:
                round_(i + 1, False)
            add_rows(1, NI // 4 - 1)

        @block.scalar
        def _(s):
            s.wait_ge(var_ready, 1)
            s.activation(root[:, :], var[:, :], ACT.Sqrt).then_inc(root_ready, 1)
            s.wait_ge(loaded, 80)
            s.activation(w[0][:, :], w_raw[:, :], ACT.Copy).then_inc(w_high, 1)
            for u in range(2):
                s.sem_inc(kept[u], 1)
            s.sem_inc(logits, 2)
            with s.Fori(0, STEPS) as i:
                for u in range(2):
                    s.wait_ge(turned, 2 * i + (u + 1))
                    s.wait_ge(logits, 2 * i + (u + 1))
                    s.wait_ge(kept[u], 32 * i + 1)
                    s.activation(tt_[0][:, u, :, :], ps_t[:, u, :, :], ACT.Copy).then_inc(tt_high, 1)
            s.wait_ge(exp_in, 1)
            s.activation(ex[:, :, :], lg[:, :, :], ACT.Exp).then_inc(exp_done, 1)
            s.wait_ge(gt_done, NI // EG)
            s.activation(gt[:, :, :], ps_l[:, :, :].rearrange("p (n i) e -> p n (i e)", i=EG), ACT.Copy).then_inc(gt_copied, 1)
            s.sem_inc(b_scaled, 2)
            with s.Fori(0, STEPS) as i:
                for j in range(8):
                    s.wait_ge(exp_ready, 16 * i + (2 * j + 11))
                    s.wait_ge(halved, 8 * i + (j + 1))
                    for e in range(4):
                        ins = s.activation(part_b[:, j % 4, e, :], ps_e[:, j % 2, 1, e, :], ACT.Copy,
                                           scale=g1[:, bass.ds(8 * i + j, 1), 4 + e:5 + e].rearrange("p i e -> p (i e)"))
                    ins.then_inc(b_scaled, 1)

        @block.gpsimd
        def _(p):
            p.sem_inc(halved, 4)
            with p.Fori(0, STEPS) as i:
                for j in range(8):
                    p.wait_ge(joined, 8 * i + (j + 1))
                    p.tensor_tensor(half[:, j % 4, :, :], part_a[:, j % 4, 0:2, :], part_a[:, j % 4, 2:4, :], ALU.add)\
                     .then_inc(halved, 1)
                    p.wait_ge(halved, 8 * i + (j + 5))
                    if j % 4 == 0:
                        p.wait_ge(used, 2 * i + (j // 4 + 1))
                    p.tensor_tensor(quarter[:, j // 4, j % 4, :], half[:, j % 4, 0, :], half[:, j % 4, 1, :], ALU.add)\
                     .then_inc(quartered, 1)

        @block.tensor
        def _(pe):
            def turn(u, n):
                pe.wait_ge(tn_ready, n + 1)
                pe.wait_ge(tt_ready, n + 1)
                for j in range(4):
                    mm = pe.transpose(ps_t[:, u, j, :], tn[:, u, j, :], k.ident[:, :])
                mm.then_inc(turned, 1)

            def route(i, last):
                for u in range(2):
                    pe.wait_ge(tt_ready, 2 * i + (u + 3))
                    for j in range(4):
                        mm = passes(pe.matmul, ps_l[:, bass.ds(8 * i + (4 * u + j), 1), :], [t[:, u, j, :] for t in tt_],
                                    [t[:, NE:NE + EXP] for t in w])
                    mm.then_inc(logits, 1)
                    if not last:
                        turn(u, 2 * i + (u + 2))

            turn(0, 0)
            turn(1, 1)
            pe.wait_ge(w_ready, 1)
            with pe.Fori(0, STEPS - 1) as i:
                route(i, False)
            route(STEPS - 1, True)
            pe.sem_inc(exp_ready, 9)
            pe.wait_ge(gates, 1)
            for n in range(NI // EG):
                pe.transpose(ps_l[:, 16 * n:16 * n + 16, :].rearrange("p i e -> p (i e)"),
                             g1[:, 16 * n:16 * n + 16, :].rearrange("p i e -> p (i e)"), k.ident[:, :]).then_inc(gt_done, 1)
            pe.wait_ge(gt_copied, 1)
            for n in range(NI // 4):
                if n >= 2:
                    pe.wait_ge(based, n - 1)
                pe.matmul(ps_t[:, n % 2, :, :], gt[:, n // 4, :], eb[:, 512 * (n % 4):512 * (n % 4) + 512],
                          start=True, stop=True).then_inc(base, 1)
            with pe.Fori(0, STEPS) as i:
                for u in range(2):
                    pe.wait_ge(fetched[u], 32 * i + 32)
                    for j in range(4):
                        n = 4 * u + j
                        for h, scaled in enumerate((a_scaled, b_scaled)):
                            pe.wait_ge(scaled, 8 * i + (n + 1))
                            passes(pe.matmul, ps_e[:, n % 2, h, :, :], [t[:, u, j, :] for t in tt_],
                                   [t[:, 512 * h:512 * h + 512] for t in w]).then_inc(exp_ready, 1)




def low_modes(w):
    w = np.concatenate([w[0, 0], w[1, 0]], 1)
    rev = np.zeros_like(w)
    rev[:, 1:LM // 2, 0] = w[:, :LM // 2:-1, 0]
    rev[:, LM // 2 + 1:, 0] = w[:, LM // 2 - 1:0:-1, 0]
    rev[:, 0, 0] = w[:, 0, 0]
    parts = [x[..., c].transpose(2, 1, 0).reshape(64, 256) for x in (w, rev) for c in range(2)]
    one = np.stack(parts, 1)
    return np.concatenate([one, one], 0)


def full_modes(w):
    full = np.zeros((HEADS, NM, NN, 2), w.dtype)
    full[:, :LM // 2, :LN] = w[0, 0]
    full[:, NM - LM // 2:, :LN] = w[1, 0]
    rev = np.zeros_like(full)
    idx = (-np.arange(NM)) % NM
    keep = np.arange(NM) != NM // 2
    rev[:, keep, 0] = full[:, idx[keep], 0]
    parts = [x[..., c].transpose(0, 2, 1).reshape(128, 512) for x in (full, rev) for c in range(2)]
    return np.stack(parts, 1)


def layout(inputs):
    r = {}
    g = {n: np.asarray(v) for n, v in inputs.items()}
    r["x"] = g["x"].reshape(NI, HW, HW)
    c = "L0_conv_"
    r["norm_g"], r["norm_b"] = g[c + "norm_g"], g[c + "norm_b"]
    for n in "KQ":
        r["w" + n] = low_modes(g[c + "w" + n])
    for n in "KQV":
        r[f"w{n}s"] = g[f"{c}w{n}s"].reshape(HEADS)
        r[f"b{n}s"] = g[f"{c}b{n}s"]
    r["wV"] = full_modes(g[c + "wV"])
    wp = np.concatenate([g[c + "wP"][0, :, 0], g[c + "wP"][1, :, 0]], 1)
    r["wP"] = np.stack([wp[..., j].transpose(0, 2, 1).reshape(128, 512) for j in range(2)], 1)
    r["wP00"] = wp[:, 0, 0, 0]
    r["wPs"] = g[c + "wPs"].reshape(HEADS)
    r["bPs"] = g[c + "bPs"]
    for n in ("M0", "M1"):
        w = np.concatenate([g[f"{c}w{n}"][0, 0, 0], g[f"{c}w{n}"][1, 0, 0]], 0).transpose(1, 0, 2)
        r["w" + n] = np.stack([np.concatenate([w[..., j]] * 2, 0) for j in range(2)], 1)
        r[f"w{n}s"] = g[f"{c}w{n}s"].reshape(1)
        r[f"b{n}s"] = g[f"{c}b{n}s"]
    f = "L0_ffn_"
    for n in ("sigma", "log_weights", "gumbel", "M_u", "M_phi_plus", "M_phi_minus"):
        r[n] = g[f + n]
    at = HB * np.arange(NQ + 1)[:, None] + (HB - 1) - np.arange(128)[None]
    inside = (at >= 0) & (at < PIX // 8)
    phi = np.zeros((NQ + 1, NF, 128), np.float32)
    for p in range(2):
        phi[:, p:2 * FT:2] = np.where(inside[..., None], g[f + "phi"][p::2][np.where(inside, at, 0)], 0).transpose(0, 2, 1)
    phi[:, 2 * FT] = phi[:, 2 * FT + 1] = at == 0
    phi[:, 2 * FT + 2] = at == 1
    r["phi"] = phi
    r["bias"] = np.tile(g["L1_conv_bias"].reshape(T), B)
    r["up_t"], r["dn"] = g["L1_conv_up_filter"][0, 0].T, g["L1_conv_dn_filter"][0, 0]
    for n in ("router_w", "router_b", "expert_w"):
        r[n] = g["L1_ffn_" + n]
    eg = 128 // EXP
    eb = np.zeros((eg, EXP, eg, 128), np.float32)
    eb[np.arange(eg), :, np.arange(eg)] = g["L1_ffn_expert_b"]
    r["expert_b"] = eb.reshape(128, eg * 128)
    r.update(tables())
    return {n: np.ascontiguousarray(v) for n, v in r.items()}


SCRATCH = {
    "u_d": (NI, HW, HW), "xt_d": (NQ, 128, 2, 256), "tc_d": (NQ, 2, NF, 128, 2), "yh_d": (NQ, 2, 64, 512), "y_d": (NI, HW, HW),
    "gu_d": (13, 512), "gd_d": (TAPS, 512),
    "xn_d": (NI, HW, HW), "xf_d": (NI, 2, NN, NM), "xl_d": (2 * LN, LM, NI),
    "d_d": (HEADS, 2, NN, NM), "z_d": (NI, 2, NN, NM), "sk_d": (NI, HW, HW),
}


def program(nc, a):
    with ExitStack() as ctx:
        k = Core(nc, ctx, a)
        with ExitStack() as conv:
            k.image_buffer(conv)
            with ExitStack() as attn:
                att = Attention(k, attn)
                stage_spectrum(k, att)
                stage_attention(k, att)
                stage_value_tables(k)
                stage_mix(k, att)
                stage_project(k, att)
            stage_mixer(k)
        k.recycle_sems()
        with ExitStack() as ffn:
            stu = Stu(k, ffn)
            stage_stu_setup(k, stu)
            stage_stu_blocks(k, stu)
            stage_stu_filter(k, stu)
            stage_stu_output(k, stu)
        stage_resample_conv(k)
        stage_experts(k)


def kernel(**inputs):
    import concourse.bacc as bacc
    from concourse.bass_utils import run_bass_kernel_spmd

    nc = bacc.Bacc("TRN2", target_bir_lowering=False, num_devices=1)
    arrays, a = {}, {}
    for name, v in layout(inputs).items():
        arrays[f"in_{name}"] = v
        a[name] = nc.dram_tensor(f"in_{name}", v.shape, mybir.dt.from_np(v.dtype), kind="ExternalInput").ap()
    for name, shape in SCRATCH.items():
        a[name] = nc.dram_tensor(name, shape, F32, kind="Internal").ap()
    a["out"] = nc.dram_tensor("out_x", (NI, HW, HW), F32, kind="ExternalOutput").ap()
    program(nc, a)
    r = run_bass_kernel_spmd(nc, [arrays], core_ids=[0])
    return r.results[0]["out_x"].reshape(B, T, HW, HW)
```

```python
from contextlib import ExitStack

import concourse.bass as bass
import numpy as np
from concourse import mybir

F32 = mybir.dt.float32
F32R = mybir.dt.float32r
ALU = mybir.AluOpType
ACT = mybir.ActivationFunctionType
AX = mybir.AxisListType

B, T, HW = 2, 32, 128
NI = B * T
GROUP = 8
NG = NI // GROUP
HEADS = 32
NM, NN = 64, 32
LM, LN = 32, 16
DS = 64
PIX = HW * HW
FT = 16
HB = 64
NQ = 32
TAPS = 12
WU = 13
EXP = 8


def tables():
    t = {}
    h = np.arange(HW)
    m = np.concatenate([np.arange(NM // 2), np.arange(-NM // 2, 0)])
    n = np.arange(NN)
    ang = 2 * np.pi * np.outer(h, m) / HW
    rows = [np.cos(ang), -np.sin(ang)]
    hd = np.arange(DS)
    rel = hd[None, :, None] / DS - h[:, None, None] / HW
    a1 = np.cos(2 * np.pi * rel * m).sum(-1) / HW
    a2 = np.sin(2 * np.pi * rel * m).sum(-1) / HW
    nn = np.arange(DS // 2 + 1)
    wt = np.where((nn == 0) | (nn == DS // 2), 1.0, 2.0)
    b1 = (wt * np.cos(2 * np.pi * rel * nn)).sum(-1) / HW
    b2 = (wt * np.sin(2 * np.pi * rel * nn)).sum(-1) / HW
    t["dft_rows"] = np.concatenate(rows + [a1, a2], 1)
    an = 2 * np.pi * np.outer(h, n) / HW
    c, s = np.cos(an) / PIX, np.sin(an) / PIX
    t["dft_cols"] = np.concatenate([c, -s, s, c, s, c, -c, s], 1)
    t["down_cols"] = np.concatenate([b1, -b2], 1)
    w2 = np.where(n == 0, 1.0, 2.0)[:, None]
    ca, sa = w2 * np.cos(an.T), w2 * np.sin(an.T)
    t["idft_cols"] = np.concatenate([ca, -sa], 0)
    t["idft_rows"] = np.concatenate([np.cos(ang.T), -np.sin(ang.T)], 0)
    ml = np.concatenate([np.arange(LM // 2), np.arange(-LM // 2, 0)])
    w = np.where(np.arange(LN)[:, None] == 0, 1.0, 2.0) * np.ones((1, LM))
    w[0, ml == -LM // 2] = 2.0
    w *= 64.0
    w = np.tile(w.reshape(LN * 4, LM // 4), (2, 1))
    t["parseval"] = np.repeat(w[:, :, None], HEADS, 2).reshape(128, 256)
    n0 = np.zeros((2, LN, 4, LM // 4, HEADS))
    n0[:, 0] = 1.0
    n0 = n0.reshape(128, 256)
    t["herm_low"] = np.concatenate([1 - 0.5 * n0, 0.5 * n0], 1)
    t["im_sign"] = np.concatenate([np.ones((64, 1)), -np.ones((64, 1))], 0)
    f0 = np.zeros((HEADS, NN, NM))
    f0[:, 0] = 1.0
    f0 = f0.reshape(128, 512)
    t["herm_full"] = np.concatenate([1 - 0.5 * f0, 0.5 * f0], 1)
    t["identity"] = np.eye(128)
    q, j = np.arange(NQ), np.arange(NQ + 1)
    aj = 2 * np.pi * np.outer(j, q) / (2 * NQ)
    re, im, re_b = np.cos(aj), -np.sin(aj), np.cos(aj)
    re_b[:, 0] = (-1.0) ** j
    t["filter_dft"] = np.concatenate([re, im, -im, re_b], 1)
    im_p = im.copy()
    im_p[:, 0] = (-1.0) ** j
    both = np.stack([re, im_p], 1).reshape(NQ + 1, 2 * NQ)
    t["block_dft"] = np.concatenate([np.kron(np.eye(B), both[:NQ]), np.kron(np.eye(B), both[1:])], 1)
    wt = np.where(q == 0, 1.0, 2.0)[:, None] / (2 * NQ)
    inv = np.concatenate([wt * re[:NQ].T, wt * im_p[:NQ].T], 0)
    t["block_idft"] = np.kron(np.eye(B), inv)
    t["masks"] = np.stack([(np.arange(NI) % T < T // f) for f in (1, 2, 4, 8)]).astype(float)
    i = np.arange(TAPS)
    sel = np.zeros((TAPS, 13))
    for q in range(2):
        sel[i, 7 * q + (q + i - 5) // 2 + (3 if q == 0 else 2)] = 1.0
    t["up_sel"] = sel
    pu, pd = np.zeros((TAPS, 2, 256)), np.zeros((TAPS, 2, 256))
    for p in range(2):
        pu[i, p, HW - 1 + (p + i - 5) // 2] = 1.0
        j = i[(i + 1) % 2 == p]
        pd[j, p, HW - 1 - (j - 5 - p) // 2] = 1.0
    t["up_pos"], t["dn_pos"] = pu.reshape(TAPS, 512), pd.reshape(TAPS, 512)
    t["order"] = EXP - np.arange(EXP)
    return {k: np.ascontiguousarray(v, np.float32) for k, v in t.items()}


class Chain:

    def __init__(self, eng, sem):
        self.eng, self.sem, self.n = eng, sem, 0

    def __call__(self, ins):
        self.n += 1
        ins.then_inc(self.sem, 1)
        self.eng.wait_ge(self.sem, self.n)


def passes(matmul, out, lhs, rhs, start=True, stop=True):
    matmul(out, lhs[0], rhs[0], start=start, stop=False)
    matmul(out, lhs[1], rhs[0], start=False, stop=False)
    return matmul(out, lhs[0], rhs[1], start=False, stop=stop)


def sub(ap, offset, dims):
    return bass.AP(ap.tensor, offset, dims)


def row_stats(v, link, st, mean, var, tmp):
    link(v.tensor_tensor(tmp, st[:, :, 1], st[:, :, 4], ALU.subtract))
    link(v.tensor_tensor(mean, st[:, :, 1], st[:, :, 4], ALU.add))
    link(v.tensor_tensor(var, st[:, :, 2], st[:, :, 5], ALU.add))
    link(v.tensor_tensor(tmp, tmp, tmp, ALU.mult))
    link(v.tensor_scalar(var, var, 1.0 / HW, None, ALU.mult))
    link(v.scalar_tensor_tensor(out=var, in0=tmp, scalar=0.25, in1=var, op0=ALU.mult, op1=ALU.add))
    link(v.tensor_scalar(mean, mean, 0.5, None, ALU.mult))


def newton_rsqrt(v, link, var, root, out, tmp, root_ready, n):
    v.wait_ge(root_ready, n)
    link(v.reciprocal(out, root))
    link(v.tensor_tensor(tmp, out, out, ALU.mult))
    link(v.tensor_tensor(tmp, tmp, var, ALU.mult))
    link(v.tensor_scalar(tmp, tmp, -0.5, 1.5, ALU.mult, ALU.add))
    link(v.tensor_tensor(out, out, tmp, ALU.mult))


def v_stats(v, st, x, first, last):
    with v.Fori(first // 8, last // 8) as i:
        for j in range(8):
            one = bass.ds(8 * i + j, 1)
            v.bn_stats(st[:, one, :], x[:, one, :])


STEP = 4
NS = NI // STEP


def run_slots(eng, slot, steady, total):
    for t in range(4):
        slot(t, t % 2)
    with eng.Fori(0, (steady - 4) // 2) as i:
        for u in range(2):
            slot(2 * i + (4 + u), u)
    for t in range(steady, total):
        slot(t, t % 2)


def during(t, lo, hi=NS):
    return not isinstance(t, int) or lo <= t < hi


def wait_count(eng, sem, n):
    if not isinstance(n, int) or n > 0:
        eng.wait_ge(sem, n)


def images(t):
    return bass.ds(STEP * t, STEP)


class Core:

    def __init__(self, nc, ctx, a):
        self.nc, self.ctx, self.a = nc, ctx, a
        self.sems = []
        self.x = self.sb("acts", [HW, NI, HW])
        self.st = self.sb("st", [HW, NI, 6])
        self.ones = self.sb("ones", [128, 128])
        self.ident = self.sb("ident", [128, 128])
        self.norm_g = self.sb("norm_g", [128, 6])
        self.norm_b = self.sb("norm_b", [128, 6])

    def image_buffer(self, ctx):
        self.xa = self.sb("xa", [HW, NI, HW], ctx=ctx)

    def sb(self, name, shape, dt=F32, ctx=None):
        return (ctx or self.ctx).enter_context(self.nc.sbuf_tensor(name, shape, dt))

    def ps(self, name, shape, ctx):
        return ctx.enter_context(self.nc.psum_tensor(name, shape, F32))

    def sem(self, name):
        self.sems.append(self.nc.alloc_semaphore(name))
        return self.sems[-1]

    def recycle_sems(self):
        self.nc.clear_and_free_semaphores(self.sems)
        self.nc.all_engine_barrier()
        self.sems = []


class ValueTables:

    def __init__(self, k, ctx):
        sb = lambda name, shape: k.sb(name, shape, ctx=ctx)
        self.a = k.a
        self.wv, self.wp = sb("s1b_wv", [128, 4, 512]), sb("s1b_wp", [128, 2, 512])
        self.herm = sb("s1b_herm", [128, 2, 512])
        self.fac = sb("s1b_fac", [128, 2])
        self.d, self.t = sb("s1b_d", [128, 2, 512]), sb("s1b_t", [128, 3, 512])
        self.loaded, self.chain, self.stored = k.sem("s1b_loaded"), k.sem("s1b_chain"), k.sem("s1b_stored")

    def run(self, p):
        a, wv, wp, herm, fac, d, t = self.a, self.wv, self.wp, self.herm, self.fac, self.d, self.t
        p.dma_start(wv[:, :, :], a["wV"]).then_inc(self.loaded, 16)
        p.dma_start(wp[:, :, :], a["wP"]).then_inc(self.loaded, 16)
        p.dma_start(herm[:, :, :], a["herm_full"].rearrange("p (u f) -> p u f", u=2)).then_inc(self.loaded, 16)
        for j, name in enumerate(("wVs", "wPs")):
            p.dma_start(fac[:, j:j + 1], sub(a[name], 0, [[1, HEADS], [0, 4], [1, 1]])).then_inc(self.loaded, 16)
        link = Chain(p, self.chain)
        tt = lambda o, x, y, op: link(p.tensor_tensor(o, x, y, op))
        p.wait_ge(self.loaded, 80)
        for j in range(4):
            tt(wv[:, j, :], wv[:, j, :], herm[:, j // 2, :], ALU.mult)
        tt(wv[:, 0, :], wv[:, 0, :], wv[:, 2, :], ALU.add)
        tt(wv[:, 1, :], wv[:, 1, :], wv[:, 3, :], ALU.subtract)
        vr, vi, pr, pi = wv[:, 0, :], wv[:, 1, :], wp[:, 0, :], wp[:, 1, :]
        wvs, wps = (fac[:, j:j + 1].broadcast_to([128, 512]) for j in range(2))
        tt(t[:, 0, :], vr, wvs, ALU.add)
        tt(d[:, 0, :], pr, t[:, 0, :], ALU.mult)
        tt(t[:, 1, :], pi, vi, ALU.mult)
        tt(d[:, 0, :], d[:, 0, :], t[:, 1, :], ALU.subtract)
        tt(t[:, 1, :], vr, wps, ALU.mult)
        tt(d[:, 0, :], d[:, 0, :], t[:, 1, :], ALU.add)
        tt(d[:, 1, :], pr, vi, ALU.mult)
        tt(t[:, 2, :], pi, t[:, 0, :], ALU.mult)
        tt(d[:, 1, :], d[:, 1, :], t[:, 2, :], ALU.add)
        tt(t[:, 2, :], vi, wps, ALU.mult)
        tt(d[:, 1, :], d[:, 1, :], t[:, 2, :], ALU.add)
        for c in range(2):
            p.dma_start(sub(a["d_d"], 2048 * c, [[4096, HEADS], [512, 4], [1, 512]]), d[:, c, :]).then_inc(self.stored, 16)
        p.wait_ge(self.stored, 32)


def stage_spectrum(k, att):
    nc, a = k.nc, k.a
    with ExitStack() as ctx:
        sb = lambda name, shape: k.sb(name, shape, ctx=ctx)
        x, xa = k.x, k.xa
        st = sb("s1_st", [128, NI, 6])
        mean, var, rstd, root, tmp, scale = (sb(f"s1_{n}", [128, NI]) for n in ("mean", "var", "rstd", "root", "tmp", "scale"))
        rows = sb("s1_rows", [128, 256])
        cols = sb("s1_cols", [128, 128])
        down = sb("s1_down", [128, 128])
        xn = sb("s1_xn", [128, 2, STEP, HW])
        yt = sb("s1_yt", [128, 2, STEP, 256])
        xfs = sb("s1_xf", [64, NI, NM])
        xls = sb("s1_xl", [64, LM, NI])
        xds = sb("s1_xd", [64, NI, DS])
        ps_a = k.ps("s1_psa", [128, 2, STEP, 256], ctx)
        ps_x = k.ps("s1_psx", [64, 2, 512], ctx)
        ps_d = k.ps("s1_psd", [64, 2, 512], ctx)
        loaded, x_loaded = k.sem("s1_loaded"), [k.sem(f"s1_x{q}_loaded") for q in range(4)]
        chain = k.sem("s1_chain")
        ones_set = k.sem("s1_ones_set")
        var_ready, root_ready = k.sem("s1_var_ready"), k.sem("s1_root_ready")
        rowvar_ready, imgvar_ready = k.sem("s1_rowvar_ready"), k.sem("s1_imgvar_ready")
        xn_ready, xn_stored = k.sem("s1_xn_ready"), [k.sem(f"s1_xn{u}_stored") for u in range(2)]
        rows_done, yt_ready = k.sem("s1_rows_done"), k.sem("s1_yt_ready")
        spec_done = k.sem("s1_spec_done")
        spec_copied, down_copied = k.sem("s1_spec_copied"), k.sem("s1_down_copied")
        gram_done, stored = k.sem("s1_gram_done"), k.sem("s1_stored")

        tables = ValueTables(k, ctx)
        ps_s = ps_a[:, 0, 0:2, :].rearrange("p i m -> p (i m)")
        block = ctx.enter_context(nc.Block())

        @block.sync
        def _(sp):
            for q in range(4):
                sp.dma_start(x[:, 16 * q:16 * q + 16, :],
                             a["x"][16 * q:16 * q + 16].rearrange("i h w -> h i w")).then_inc(x_loaded[q], 16)
            sp.dma_start(rows[:, :], a["dft_rows"]).then_inc(loaded, 16)
            sp.dma_start(cols[:, :], a["dft_cols"][:, 0:128]).then_inc(loaded, 16)
            sp.dma_start(down[:, :], a["down_cols"]).then_inc(loaded, 16)
            sp.dma_start(k.ident[:, :], a["identity"]).then_inc(loaded, 16)
            sp.dma_start(k.norm_g[:, :], sub(a["norm_g"], 0, [[0, 128], [1, 6]])).then_inc(loaded, 16)
            sp.dma_start(k.norm_b[:, :], sub(a["norm_b"], 0, [[0, 128], [1, 6]])).then_inc(loaded, 16)
            with sp.Fori(0, NS // 2) as i:
                for u in range(2):
                    sp.wait_ge(xn_ready, 2 * i + (u + 1))
                    sp.dma_start(a["xn_d"][images(2 * i + u)].rearrange("i h w -> h i w"), xn[:, u, :, :])\
                      .then_inc(xn_stored[u], 16)
            for u in range(2):
                sp.wait_ge(xn_stored[u], 8 * NS)
            sp.wait_ge(spec_copied, NS)
            sp.dma_start(sub(a["xf_d"], 0, [[NM, 64], [64 * NM, NI], [1, NM]]), xfs[:, :, :]).then_inc(stored, 16)
            for c in range(2):
                sp.dma_start(a["xl_d"][c * LN:(c + 1) * LN], xls[c * NN:c * NN + LN, :, :]).then_inc(stored, 16)
            sp.wait_ge(stored, 48)

        @block.gpsimd
        def _(p):
            tables.run(p)

        @block.vector
        def _(v):
            link = Chain(v, chain)
            v.memset(k.ones[:, :], 1.0 / HW).then_inc(ones_set, 1)
            for q in range(4):
                v.wait_ge(x_loaded[q], 16)
                v_stats(v, st, x, 16 * q, 16 * q + 16)
            v.wait_ge(loaded, 96)
            link(v.memset(tmp[:, :], 0.0))
            row_stats(v, link, st, mean[:, :], var[:, :], tmp[:, :])
            link(v.tensor_scalar(rstd[:, :], var[:, :], 1e-6, None, ALU.add))
            v.tensor_copy(scale[:, :], rstd[:, :]).then_inc(var_ready, 1)
            v.wait_ge(var_ready, 1)
            newton_rsqrt(v, link, scale[:, :], root[:, :], rstd[:, :], tmp[:, :], root_ready, 1)
            link(v.tensor_tensor(tmp[:, :], rstd[:, :], rstd[:, :], ALU.mult))
            v.tensor_tensor(var[:, :], var[:, :], tmp[:, :], ALU.mult).then_inc(rowvar_ready, 1)
            with v.Fori(0, NI // 8) as i:
                for j in range(8):
                    one = bass.ds(8 * i + j, 1)
                    v.tensor_scalar(xa[:, one, :], x[:, one, :], mean[:, one], rstd[:, one], ALU.subtract, ALU.mult)
            v.wait_ge(imgvar_ready, 1)
            link(v.tensor_scalar(tmp[:, :], ps_s[:, 0:NI], 1e-5, None, ALU.add))
            v.tensor_copy(var[:, :], tmp[:, :]).then_inc(var_ready, 1)
            v.wait_ge(var_ready, 2)
            newton_rsqrt(v, link, var[:, :], root[:, :], scale[:, :], tmp[:, :], root_ready, 2)
            link(v.tensor_scalar(scale[:, :], scale[:, :], k.norm_g[:, 0:1], None, ALU.mult))

            def norm_in(s, u):
                wait_count(v, rows_done, s + (-1))
                wait_count(v, xn_stored[u], 8 * s + (-8 * u))
                for j in range(STEP):
                    one = bass.ds(STEP * s + j, 1)
                    ins = v.tensor_scalar(xn[:, u, j, :], xa[:, one, :], scale[:, one], k.norm_b[:, 0:1], ALU.mult, ALU.add)
                ins.then_inc(xn_ready, 1)

            def slot(s, u):
                if during(s + 2, 2):
                    norm_in(s + 2, u)
                if during(s, 0):
                    v.wait_ge(spec_done, s + 1)
                    src = ps_x[:, u, 0:STEP * NM].rearrange("p (i m) -> p i m", m=NM)
                    v.tensor_copy(xfs[:, images(s), :], src)
                    dst = xls[:, :, images(s)].rearrange("p m i -> p i m")
                    v.tensor_copy(dst[:, :, 0:16], src[:, :, 0:16])
                    v.tensor_copy(dst[:, :, 16:32], src[:, :, 48:64]).then_inc(spec_copied, 1)

            norm_in(0, 0)
            norm_in(1, 1)
            run_slots(v, slot, NS - 2, NS)
            v.wait_ge(gram_done, 1)
            for b in range(B):
                ins = v.tensor_copy(att.gram[T * b:T * b + T, :], ps_s[T * b:T * b + T, T * b:T * b + T])
            ins.then_inc(chain, 1)

        @block.scalar
        def _(s):
            s.wait_ge(var_ready, 1)
            s.activation(root[:, :], scale[:, :], ACT.Sqrt).then_inc(root_ready, 1)
            s.wait_ge(var_ready, 2)
            s.activation(root[:, :], var[:, :], ACT.Sqrt).then_inc(root_ready, 1)

            def slot(t, u):
                if during(t, 0):
                    s.wait_ge(rows_done, t + 1)
                    wait_count(s, spec_done, t + (-1))
                    for h in range(2):
                        ins = s.activation(yt[:, u, 2 * h:2 * h + 2, :], ps_a[:, u, 2 * h:2 * h + 2, :], ACT.Copy)
                    ins.then_inc(yt_ready, 1)
                if during(t + (-1), 0):
                    s.wait_ge(spec_done, t + 0)
                    s.activation(xds[:, images(t + (-1)), :],
                                 ps_d[:, 1 - u, 0:STEP * DS].rearrange("p (i m) -> p i m", m=DS), ACT.Copy)\
                     .then_inc(down_copied, 1)

            run_slots(s, slot, NS, NS + 1)

        @block.tensor
        def _(pe):
            pe.wait_ge(ones_set, 1)
            pe.wait_ge(rowvar_ready, 1)
            pe.matmul(ps_s[:, 0:NI], k.ones[:, :], var[:, :], start=True, stop=True).then_inc(imgvar_ready, 1)

            def slot(t, u):
                if during(t, 0):
                    pe.wait_ge(xn_ready, t + 1)
                    wait_count(pe, yt_ready, t + (-1))
                    for j in range(STEP):
                        mm = pe.matmul(ps_a[:, u, j, :], xn[:, u, j, :], rows[:, :], start=True, stop=True)
                    mm.then_inc(rows_done, 1)
                if during(t + (-1), 0):
                    pe.wait_ge(yt_ready, t + 0)
                    wait_count(pe, spec_copied, t + (-2))
                    wait_count(pe, down_copied, t + (-2))
                    b = 1 - u
                    out, low = ps_x[:, b, 0:STEP * NM], ps_d[:, b, 0:STEP * DS]
                    pe.matmul(low, down[:, 0:64], yt[:, b, :, 128:192], start=True, stop=False)
                    pe.matmul(low, down[:, 64:128], yt[:, b, :, 192:256], start=False, stop=True)
                    pe.matmul(out, cols[:, 0:64], yt[:, b, :, 0:64], start=True, stop=False)
                    pe.matmul(out, cols[:, 64:128], yt[:, b, :, 64:128], start=False, stop=True).then_inc(spec_done, 1)

            run_slots(pe, slot, NS, NS + 1)
            pe.wait_ge(down_copied, NS)
            for r in range(DS):
                mm = pe.matmul(ps_s[0:64, 0:NI], xds[:, :, r], xds[:, :, r], start=(r == 0), stop=(r == DS - 1))
            mm.then_inc(gram_done, 1)


class Attention:

    def __init__(self, k, ctx):
        self.gram = k.sb("gram", [64, T], ctx=ctx)
        self.mix_t = k.sb("mix_t", [128, 128], ctx=ctx)
        self.prob_t = k.sb("prob_t", [128, HEADS // 4, B, T], ctx=ctx)
        self.dc = k.sb("dc", [1, 1], ctx=ctx)


def stage_attention(k, att):
    nc, a = k.nc, k.a
    with ExitStack() as ctx:
        sb = lambda name, shape: k.sb(name, shape, ctx=ctx)
        xl = sb("s2_xl", [128, 8, NI])
        xt = sb("s2_xt", [128, 8, NI])
        xw = sb("s2_xw", [128, 8, NI])
        herm = sb("s2_herm", [128, 2, 256])
        pars = sb("s2_pars", [128, 256])
        sign = sb("s2_sign", [128, 1])
        wk, wq = sb("s2_wk", [128, 4, 256]), sb("s2_wq", [128, 4, 256])
        skip = sb("s2_skip", [128, 4, HEADS])
        vec = sb("s2_vec", [128, 2, HEADS])
        cr, ci, t1 = (sb(f"s2_{n}", [128, 256]) for n in ("cr", "ci", "t1"))
        kp = sb("s2_kp", [128, 8, HEADS, NI])
        kq = sb("s2_kq", [128, 4, HEADS, NI])
        sc = sb("s2_sc", [64, HEADS, T])
        sx = sb("s2_sx", [64, HEADS, T])
        mx, sm, rs = (sb(f"s2_{n}", [64, HEADS]) for n in ("mx", "sm", "rs"))
        qk = sb("s2_qk", [128, HEADS])
        mix = sb("s2_mix", [64, T])
        mixt = sb("s2_mixt", [64, T])
        pt = sb("s2_pt", [64, HEADS, T])
        dcv = sb("s2_dcv", [1, 3, HEADS])
        bp = sb("s2_bp", [1, 1])
        dct = sb("s2_dct", [1, HEADS])
        ps = k.ps("s2_ps", [64, HEADS, T], ctx)
        loaded, chain = k.sem("s2_loaded"), k.sem("s2_chain")
        ci_ready, kp_ready = k.sem("s2_ci_ready"), k.sem("s2_kp_ready")
        kq_ready, kq_added = k.sem("s2_kq_ready"), k.sem("s2_kq_added")
        k_ready, scores_done = k.sem("s2_k_ready"), k.sem("s2_scores_done")
        shifted, exped, turned, moved = k.sem("s2_shifted"), k.sem("s2_exped"), k.sem("s2_turned"), k.sem("s2_moved")

        block = ctx.enter_context(nc.Block())

        @block.sync
        def _(sp):
            n = LN * 4 * 512
            src = sub(a["xl_d"], 0, [[512, 128], [NI, 8], [1, NI]])
            sp.dma_start(xl[:, :, :], src).then_inc(loaded, 16)
            sp.dma_start(xt[:, :, :], src).then_inc(loaded, 16)
            sp.dma_start(xw[0:64, :, :], sub(a["xl_d"], n, [[512, 64], [NI, 8], [1, NI]])).then_inc(loaded, 16)
            sp.dma_start(xw[64:128, :, :], sub(a["xl_d"], 0, [[512, 64], [NI, 8], [1, NI]])).then_inc(loaded, 16)
            sp.dma_start(herm[:, :, :], a["herm_low"].rearrange("p (u f) -> p u f", u=2)).then_inc(loaded, 16)
            sp.dma_start(pars[:, :], a["parseval"]).then_inc(loaded, 16)
            sp.dma_start(sign[:, :], a["im_sign"]).then_inc(loaded, 16)
            sp.dma_start(wk[:, :, :], a["wK"]).then_inc(loaded, 16)
            sp.dma_start(wq[:, :, :], a["wQ"]).then_inc(loaded, 16)
            for j, name in enumerate(("wQs", "wKs", "bQs", "bKs")):
                sp.dma_start(skip[:, j, :], sub(a[name], 0, [[0, 128], [1, HEADS]])).then_inc(loaded, 16)
            for j, name in enumerate(("wVs", "wPs")):
                sp.dma_start(vec[:, j, :], sub(a[name], 0, [[0, 128], [1, HEADS]])).then_inc(loaded, 16)
            sp.dma_start(dcv[:, 0, :], sub(a["bVs"], 0, [[0, 1], [1, HEADS]])).then_inc(loaded, 16)
            sp.dma_start(dcv[:, 1, :], sub(a["wPs"], 0, [[0, 1], [1, HEADS]])).then_inc(loaded, 16)
            sp.dma_start(dcv[:, 2, :], sub(a["wP00"], 0, [[0, 1], [1, HEADS]])).then_inc(loaded, 16)
            sp.dma_start(bp[:, :], sub(a["bPs"], 0, [[0, 1], [1, 1]])).then_inc(loaded, 16)
            sp.wait_ge(turned, 1)
            for b in range(B):
                for o in range(4):
                    sp.dma_start(att.prob_t[32 * o:32 * o + 32, :, b, :],
                                 pt[32 * b:32 * b + 32, o::4, :]).then_inc(moved, 16)
            sp.wait_ge(moved, 128)

        def along(t, m):
            return t[:, m, :].unsqueeze(1).broadcast_to([128, HEADS, NI])

        def heads(t, m):
            return t[:, HEADS * m:HEADS * m + HEADS].unsqueeze(2).broadcast_to([128, HEADS, NI])

        @block.gpsimd
        def _(p):
            p.wait_ge(ci_ready, 1)
            for m in range(8):
                if m >= 4:
                    p.wait_ge(kq_added, m - 3)
                p.tensor_tensor(kq[:, m % 4, :, :], along(xw, m), heads(ci, m), ALU.mult).then_inc(kq_ready, 1)

        @block.vector
        def _(v):
            link = Chain(v, chain)
            tt = lambda o, x, y, op: link(v.tensor_tensor(o, x, y, op))
            v.wait_ge(loaded, 19 * 16)

            def head(j):
                return skip[:, j:j + 1, :].broadcast_to([128, 8, HEADS])

            r3 = lambda t: t.rearrange("p (m o) -> p m o", o=HEADS)
            for w in (wk, wq):
                tt(w[:, 0, :], w[:, 0, :], herm[:, 0, :], ALU.mult)
                tt(w[:, 1, :], w[:, 1, :], herm[:, 0, :], ALU.mult)
                tt(w[:, 2, :], w[:, 2, :], herm[:, 1, :], ALU.mult)
                tt(w[:, 3, :], w[:, 3, :], herm[:, 1, :], ALU.mult)
                tt(w[:, 0, :], w[:, 0, :], w[:, 2, :], ALU.add)
                tt(w[:, 1, :], w[:, 1, :], w[:, 3, :], ALU.subtract)
            kr, ki, qr, qi = wk[:, 0, :], wk[:, 1, :], wq[:, 0, :], wq[:, 1, :]
            tt(r3(cr[:, :]), r3(kr), head(0), ALU.mult)
            tt(r3(t1[:, :]), r3(qr), head(1), ALU.mult)
            tt(cr[:, :], cr[:, :], t1[:, :], ALU.add)
            tt(t1[:, :], qr, kr, ALU.mult)
            tt(cr[:, :], cr[:, :], t1[:, :], ALU.add)
            tt(t1[:, :], qi, ki, ALU.mult)
            tt(cr[:, :], cr[:, :], t1[:, :], ALU.add)
            tt(cr[:, :], cr[:, :], pars[:, :], ALU.mult)
            tt(r3(ci[:, :]), r3(qi), head(1), ALU.mult)
            tt(r3(t1[:, :]), r3(ki), head(0), ALU.mult)
            tt(ci[:, :], ci[:, :], t1[:, :], ALU.subtract)
            tt(t1[:, :], qi, kr, ALU.mult)
            tt(ci[:, :], ci[:, :], t1[:, :], ALU.add)
            tt(t1[:, :], qr, ki, ALU.mult)
            tt(ci[:, :], ci[:, :], t1[:, :], ALU.subtract)
            tt(ci[:, :], ci[:, :], pars[:, :], ALU.mult)
            v.tensor_scalar(ci[:, :], ci[:, :], sign[:, 0:1], None, ALU.mult).then_inc(ci_ready, 1)
            v.tensor_tensor(kp[:, 0, :, :], along(xl, 0), heads(cr, 0), ALU.mult).then_inc(kp_ready, 1)
            for m in range(8):
                if m < 7:
                    v.tensor_tensor(kp[:, m + 1, :, :], along(xl, m + 1), heads(cr, m + 1), ALU.mult).then_inc(kp_ready, 1)
                v.wait_ge(kp_ready, m + 1)
                v.wait_ge(kq_ready, m + 1)
                v.tensor_tensor(kp[:, m, :, :], kp[:, m, :, :], kq[:, m % 4, :, :], ALU.add).then_inc(kq_added, 1)
            v.wait_ge(kq_added, 8)
            z = slice(0, 1)
            col = lambda t, p: r3(t)[p:p + 1, 0, :]
            tt(t1[z, 0:HEADS], col(qr, 0), skip[z, 0, :], ALU.add)
            tt(t1[z, 0:HEADS], t1[z, 0:HEADS], skip[z, 3, :], ALU.mult)
            link(v.tensor_scalar(t1[z, 0:HEADS], t1[z, 0:HEADS], 64.0, None, ALU.mult))
            tt(kp[z, 0, :, :], kp[z, 0, :, :], t1[z, 0:HEADS].unsqueeze(2).broadcast_to([1, HEADS, NI]), ALU.add)
            y = slice(64, 65)
            tt(t1[y, 0:HEADS], col(kr, 64), skip[y, 1, :], ALU.add)
            tt(kp[y, 0, :, :], xw[y, 0, :].unsqueeze(1).broadcast_to([1, HEADS, NI]),
               t1[y, 0:HEADS].unsqueeze(2).broadcast_to([1, HEADS, NI]), ALU.mult)
            tt(kp[y, 0, :, :], kp[y, 0, :, :], skip[y, 3, :].unsqueeze(2).broadcast_to([1, HEADS, NI]), ALU.add)
            link(v.tensor_scalar(t1[y, 0:HEADS], skip[y, 2, :], 64.0, None, ALU.mult))
            tt(kp[y, 0, :, :], kp[y, 0, :, :], t1[y, 0:HEADS].unsqueeze(2).broadcast_to([1, HEADS, NI]), ALU.mult)
            v.memset(xt[y, 0, :], 1.0).then_inc(k_ready, 1)
            tt(qk[:, :], skip[:, 0, :], skip[:, 1, :], ALU.mult)
            link(v.tensor_scalar(qk[:, :], qk[:, :], 1.0 / 64, None, ALU.mult))
            tt(sx[:, :, :], att.gram[:, :].unsqueeze(1).broadcast_to([64, HEADS, T]),
               qk[0:64, :].unsqueeze(2).broadcast_to([64, HEADS, T]), ALU.mult)
            v.wait_ge(scores_done, 1)
            for o in range(0, HEADS, 16):
                tt(sc[:, o:o + 16, :], ps[:, o:o + 16, :], sx[:, o:o + 16, :], ALU.add)
            link(v.tensor_reduce(mx[:, :], sc[:, :, :], AX.X, ALU.max))
            v.tensor_tensor(sc[:, :, :], sc[:, :, :], mx[:, :].unsqueeze(2).broadcast_to([64, HEADS, T]),
                            ALU.subtract).then_inc(shifted, 1)
            v.wait_ge(exped, 1)
            link(v.tensor_reduce(sm[:, :], sx[:, :, :], AX.X, ALU.add))
            link(v.reciprocal(rs[:, :], sm[:, :]))
            tt(sx[:, :, :], sx[:, :, :], rs[:, :].unsqueeze(2).broadcast_to([64, HEADS, T]), ALU.mult)
            v.transpose(pt[:, :, :].rearrange("p o t -> p (o t)"),
                        sx[:, :, :].rearrange("p o t -> p (o t)")).then_inc(turned, 1)
            tt(qk[:, :], vec[:, 0, :], vec[:, 1, :], ALU.mult)
            tt(sc[:, :, :], sx[:, :, :], qk[0:64, :].unsqueeze(2).broadcast_to([64, HEADS, T]), ALU.mult)
            link(v.tensor_reduce(mix[:, :], sc[:, :, :].rearrange("p o s -> p s o"), AX.X, ALU.add))
            link(v.transpose(mixt[:, :], mix[:, :]))
            link(v.memset(att.mix_t[:, :], 0.0))
            for half in range(2):
                for b in range(B):
                    p = 64 * half + 32 * b
                    link(v.tensor_copy(att.mix_t[p:p + 32, p:p + 32], mixt[32 * b:32 * b + 32, :]))
            tt(dct[:, :], dcv[:, 1, :], dcv[:, 2, :], ALU.add)
            tt(dct[:, :], dct[:, :], dcv[:, 0, :], ALU.mult)
            link(v.tensor_reduce(att.dc[:, :], dct[:, :], AX.X, ALU.add))
            tt(att.dc[:, :], att.dc[:, :], bp[:, :], ALU.add)

        @block.scalar
        def _(s):
            s.wait_ge(shifted, 1)
            s.activation(sx[:, :, :], sc[:, :, :], ACT.Exp).then_inc(exped, 1)

        @block.tensor
        def _(pe):
            pe.wait_ge(k_ready, 1)
            pe.wait_ge(loaded, 19 * 16)
            for b in range(B):
                for o in range(0, HEADS, 16):
                    for m in range(8):
                        mm = pe.matmul(ps[T * b:T * b + T, o:o + 16, :], xt[:, m, T * b:T * b + T],
                                       kp[:, m, o:o + 16, T * b:T * b + T], start=(m == 0), stop=(m == 7))
            mm.then_inc(scores_done, 1)



def stage_mix(k, att):
    nc, a = k.nc, k.a
    with ExitStack() as ctx:
        sb = lambda name, shape: k.sb(name, shape, ctx=ctx)
        HALF = NN * NM // 2
        x4 = sb("s4_x4", [128, B, 2, HALF])
        dd = sb("s4_dd", [128, 2, 2, HALF])
        y = sb("s4_y", [128, 3, 2, HALF])
        tv, tp = sb("s4_tv", [128, HALF]), sb("s4_tp", [128, 3, HALF])
        z = sb("s4_z", [64, 4 * 512])
        xin, xout = sb("s4_xin", [128, 4, 4, 512]), sb("s4_xout", [128, 2, 4, 512])
        psz = k.ps("s4_psz", [64, 4 * 512], ctx)
        pss = k.ps("s4_pss", [128, 4, 512], ctx)
        x4_loaded, d_loaded = k.sem("s4_x4_loaded"), [k.sem("s4_d0_loaded"), k.sem("s4_d1_loaded")]
        re_ready, im_parts, im_ready = k.sem("s4_re_ready"), k.sem("s4_im_parts"), k.sem("s4_im_ready")
        chain_v = k.sem("s4_chain_v")
        mixed, z_copied, z_stored = k.sem("s4_mixed"), k.sem("s4_z_copied"), k.sem("s4_z_stored")
        xin_loaded, skip_done = k.sem("s4_xin_loaded"), k.sem("s4_skip_done")
        skip_copied, skip_stored = k.sem("s4_skip_copied"), [k.sem(f"s4_skip{u}_stored") for u in range(2)]
        block = ctx.enter_context(nc.Block())
        STEPS = HEADS // 4 * B

        @block.sync
        def _(sp):
            with sp.Fori(0, 2) as nh:
                sp.wait_ge(mixed, nh * STEPS + 3)
                for b in range(B):
                    for o in range(4):
                        sp.dma_start(x4[32 * o:32 * o + 32, b, :, :],
                                     sub(a["xf_d"], nh * HALF + b * T * 4096,
                                         [[4096, T], [2048, 2], [1, HALF]])).then_inc(x4_loaded, 16)
                for oc in range(HEADS // 4):
                    if oc >= 2:
                        sp.wait_ge(re_ready, nh * STEPS + 2 * (oc - 1))
                        sp.wait_ge(im_parts, nh * STEPS + 2 * (oc - 1))
                    for o in range(4):
                        sp.dma_start(dd[32 * o:32 * o + 32, oc % 2, :, :],
                                     sub(a["d_d"], nh * HALF + (4 * oc + o) * 4096,
                                         [[0, 32], [2048, 2], [1, HALF]])).then_inc(d_loaded[oc % 2], 16)
                sp.wait_ge(z_copied, nh + 2)
                sp.dma_start(sub(a["z_d"], nh * HALF, [[4096, NI], [2048, 2], [1, HALF]]),
                             z[:, :].rearrange("p (c f) -> p c f", c=2)).then_inc(z_stored, 16)
            sp.wait_ge(z_stored, 33)

        @block.gpsimd
        def _(p):
            with p.Fori(0, 2) as nh:
                p.wait_ge(x4_loaded, 128 * nh + 128)
                for j in range(STEPS):
                    oc, b = j // 2, j % 2
                    if j % 2 == 0:
                        p.wait_ge(d_loaded[oc % 2], 256 * nh + 64 * (oc // 2) + 64)
                    p.wait_ge(mixed, nh * STEPS + (j + 1))
                    dr, di, xr, xi = dd[:, oc % 2, 0, :], dd[:, oc % 2, 1, :], x4[:, b, 0, :], x4[:, b, 1, :]
                    p.tensor_tensor(tp[:, j % 3, :], di, xr, ALU.mult)
                    p.tensor_tensor(y[:, j % 3, 1, :], dr, xi, ALU.mult).then_inc(im_parts, 1)

        @block.vector
        def _(v):
            def im_sum(nh, j):
                v.wait_ge(im_parts, nh * STEPS + (j + 1))
                v.tensor_tensor(y[:, j % 3, 1, :], y[:, j % 3, 1, :], tp[:, j % 3, :], ALU.add).then_inc(im_ready, 1)

            with v.Fori(0, 2) as nh:
                v.wait_ge(x4_loaded, 128 * nh + 128)
                for j in range(STEPS):
                    oc, b = j // 2, j % 2
                    if j % 2 == 0:
                        v.wait_ge(d_loaded[oc % 2], 256 * nh + 64 * (oc // 2) + 64)
                    dr, di, xr, xi = dd[:, oc % 2, 0, :], dd[:, oc % 2, 1, :], x4[:, b, 0, :], x4[:, b, 1, :]
                    v.tensor_tensor(tv[:, :], di, xi, ALU.mult).then_inc(chain_v, 1)
                    v.wait_ge(mixed, nh * STEPS + (j + 1))
                    v.tensor_tensor(y[:, j % 3, 0, :], dr, xr, ALU.mult).then_inc(chain_v, 1)
                    v.wait_ge(chain_v, nh * 2 * STEPS + (2 * j + 2))
                    v.tensor_tensor(y[:, j % 3, 0, :], y[:, j % 3, 0, :], tv[:, :], ALU.subtract).then_inc(re_ready, 1)
                    if j:
                        im_sum(nh, j - 1)
                    v.wait_ge(re_ready, nh * STEPS + (j + 1))
                im_sum(nh, STEPS - 1)

        @block.scalar
        def _(s):
            for half in range(2):
                s.dma_start(xin[64 * half:64 * half + 64, :, :, :],
                            sub(a["xn_d"], half * (PIX // 2), [[PIX, NI], [1, PIX // 2]])).then_inc(xin_loaded, 16)
            s.sem_inc(z_copied, 1)
            s.sem_inc(z_stored, 1)
            for nh in range(2):
                s.wait_ge(mixed, nh * STEPS + (STEPS + 3))
                s.wait_ge(z_stored, 16 * nh + 1)
                for j in range(4):
                    ins = s.activation(z[:, 512 * j:512 * j + 512], psz[:, 512 * j:512 * j + 512], ACT.Copy)
                ins.then_inc(z_copied, 1)
                for i in range(4 * (1 - nh)):
                    s.wait_ge(skip_done, i + 1)
                    if i >= 2:
                        s.wait_ge(skip_stored[i % 2], 32)
                    for j in range(4):
                        ins = s.activation(xout[:, i % 2, j, :], pss[:, j, :], ACT.Copy)
                    ins.then_inc(skip_copied, 1)
                    s.wait_ge(skip_copied, i + 1)
                    for half in range(2):
                        s.dma_start(sub(a["sk_d"], half * (PIX // 2) + i * 2048, [[PIX, NI], [512, 4], [1, 512]]),
                                    xout[64 * half:64 * half + 64, i % 2, :, :]).then_inc(skip_stored[i % 2], 16)
            for u in range(2):
                s.wait_ge(skip_stored[u], 64)

        @block.tensor
        def _(pe):
            pe.sem_inc(mixed, 3)
            for nh in range(2):
                pe.wait_ge(z_copied, nh + 1)
                for j in range(STEPS):
                    oc, b = j // 2, j % 2
                    pe.wait_ge(re_ready, nh * STEPS + (j + 1))
                    pe.wait_ge(im_ready, nh * STEPS + (j + 1))
                    for q in range(4):
                        mm = pe.matmul(psz[T * b:T * b + T, 512 * q:512 * q + 512], att.prob_t[:, oc, b, :],
                                       y[:, j % 3, q // 2, 512 * (q % 2):512 * (q % 2) + 512],
                                       start=(oc == 0), stop=(oc == HEADS // 4 - 1))
                    mm.then_inc(mixed, 1)
                for i in range(4 * (1 - nh)):
                    pe.wait_ge(xin_loaded, 32)
                    if i:
                        pe.wait_ge(skip_copied, i)
                    for j in range(4):
                        mm = pe.matmul(pss[:, j, :], att.mix_t[:, :], xin[:, i, j, :], start=True, stop=True)
                    mm.then_inc(skip_done, 1)


def stage_project(k, att):
    nc, a = k.nc, k.a
    with ExitStack() as ctx:
        sb = lambda name, shape: k.sb(name, shape, ctx=ctx)
        zs, zw = sb("s5_zs", [64, NI, NM]), sb("s5_zw", [64, NI, NM])
        sign = sb("s5_sign", [64, 1])
        sk = sb("s5_sk", [128, 4, STEP, HW])
        z = sb("s5_z", [64, 2, STEP, 2, NM])
        icols, irows = sb("s5_icols", [64, 128]), sb("s5_irows", [128, 128])
        dc = sb("s5_dc", [64, 1])
        bs = sb("s5_bs", [128, 2, STEP, HW])
        ps_b, ps_o = k.ps("s5_psb", [128, 2, STEP, HW], ctx), k.ps("s5_pso", [128, 2, STEP, HW], ctx)
        up_f, dn_f = sb("s5_upf", [TAPS, TAPS]), sb("s5_dnf", [TAPS, TAPS])
        sel = sb("s5_sel", [TAPS, WU])
        pu, pd = sb("s5_pu", [TAPS, 512]), sb("s5_pd", [TAPS, 512])
        upc = sb("s5_upc", [TAPS, WU])
        gu, gd = sb("s5_gu", [WU, 512]), sb("s5_gd", [TAPS, 512])
        ps_k = k.ps("s5_psk", [TAPS + 1, 3, 512], ctx)
        taps_loaded, taps_done, taps_copied = k.sem("s5_taps_loaded"), k.sem("s5_taps_done"), k.sem("s5_taps_copied")
        taps_stored = k.sem("s5_taps_stored")
        loaded, sk_loaded, dc_added = k.sem("s5_loaded"), [k.sem(f"s5_sk{n}_loaded") for n in range(4)], k.sem("s5_dc_added")
        z_ready, cols_done, bs_ready = k.sem("s5_z_ready"), k.sem("s5_cols_done"), k.sem("s5_bs_ready")
        out_done, out_added, sk_added = k.sem("s5_out_done"), k.sem("s5_out_added"), k.sem("s5_sk_added")
        block = ctx.enter_context(nc.Block())

        @block.sync
        def _(sp):
            for t, n in ((up_f, "up_t"), (dn_f, "dn"), (sel, "up_sel"), (pu, "up_pos"), (pd, "dn_pos")):
                sp.dma_start(t[:, :], a[n]).then_inc(taps_loaded, 16)
            sp.dma_start(zs[:, :, :], sub(a["z_d"], 0, [[NM, 64], [4096, NI], [1, NM]])).then_inc(loaded, 16)
            for c in range(2):
                sp.dma_start(zw[32 * c:32 * c + 32, :, :],
                             sub(a["z_d"], 2048 * (1 - c), [[NM, 32], [4096, NI], [1, NM]])).then_inc(loaded, 16)
            sp.dma_start(sign[:, :], a["im_sign"][32:96]).then_inc(loaded, 16)
            sp.dma_start(icols[:, :], a["idft_cols"]).then_inc(loaded, 16)
            sp.dma_start(irows[:, :], a["idft_rows"]).then_inc(loaded, 16)
            with sp.Fori(0, NS // 4) as i:
                for n in range(4):
                    sp.wait_ge(sk_added, 4 * i + (n + 1))
                    sp.dma_start(sk[:, n, :, :], a["sk_d"][images(4 * i + n)].rearrange("i h w -> h i w"))\
                      .then_inc(sk_loaded[n], 16)
            for n in range(4):
                sp.wait_ge(sk_loaded[n], 4 * NS)
            sp.wait_ge(taps_copied, 3)
            sp.dma_start(a["gu_d"], gu[:, :]).then_inc(taps_stored, 16)
            sp.dma_start(a["gd_d"], gd[:, :]).then_inc(taps_stored, 16)
            sp.wait_ge(taps_stored, 32)

        @block.vector
        def _(v):
            v.sem_inc(sk_added, 4)
            v.wait_ge(loaded, 96)
            v.tensor_scalar(zs[0:1, :, 0], zs[0:1, :, 0], att.dc[0:1, 0:1], None, ALU.add).then_inc(dc_added, 1)
            v.tensor_copy(dc[32:33, :], att.dc[0:1, 0:1]).then_inc(dc_added, 1)
            v.wait_ge(dc_added, 2)
            v.tensor_scalar(zw[32:33, :, 0], zw[32:33, :, 0], dc[32:33, 0:1], None, ALU.add).then_inc(dc_added, 1)
            with v.Fori(0, NS // 4) as i:
                for n in range(4):
                    s = 4 * i + n
                    xg = k.xa[:, images(s), :]
                    v.wait_ge(sk_loaded[n], 16 * i + 16)
                    v.tensor_tensor(xg, sk[:, n, :, :], xg, ALU.add).then_inc(sk_added, 1)
                    v.wait_ge(sk_added, 4 * i + (n + 5))
                    v.wait_ge(out_done, 4 * i + (n + 1))
                    v.tensor_tensor(xg, ps_o[:, n % 2, :, :], xg, ALU.add).then_inc(out_added, 1)
                    v.wait_ge(out_added, 4 * i + (n + 1))
                    for j in range(STEP):
                        one = bass.ds(4 * STEP * i + (STEP * n + j), 1)
                        v.bn_stats(k.st[:, one, :], k.xa[:, one, :])

        @block.scalar
        def _(s):
            def spread(t, u):
                s.activation(z[:, u, :, 0, :], zs[:, images(t), :], ACT.Copy)
                s.activation(z[:, u, :, 1, :], zw[:, images(t), :], ACT.Copy, scale=sign[:, 0:1]).then_inc(z_ready, 1)

            def slot(t, u):
                s.wait_ge(cols_done, t + 1)
                wait_count(s, out_done, t + (-1))
                s.activation(bs[:, u, :, :], ps_b[:, u, :, :], ACT.Copy).then_inc(bs_ready, 1)
                if during(t + 2, 2):
                    spread(t + 2, u)

            s.wait_ge(taps_done, 1)
            s.activation(upc[:, :], ps_k[0:TAPS, 0, 0:WU], ACT.Copy).then_inc(taps_copied, 1)
            s.wait_ge(taps_done, 3)
            s.activation(gu[:, :], ps_k[0:WU, 1, :], ACT.Copy).then_inc(taps_copied, 1)
            s.activation(gd[:, :], ps_k[0:TAPS, 2, :], ACT.Copy).then_inc(taps_copied, 1)
            s.wait_ge(dc_added, 3)
            spread(0, 0)
            spread(1, 1)
            run_slots(s, slot, NS - 2, NS)

        @block.tensor
        def _(pe):
            def slot(t, u):
                if during(t, 0):
                    pe.wait_ge(z_ready, t + 1)
                    wait_count(pe, bs_ready, t + (-1))
                    for j in range(STEP):
                        mm = pe.matmul(ps_b[:, u, j, :], z[:, u, j, :, :], icols[:, :], start=True, stop=True)
                    mm.then_inc(cols_done, 1)
                if during(t + (-1), 0):
                    pe.wait_ge(bs_ready, t + 0)
                    wait_count(pe, out_added, t + (-2))
                    pe.matmul(ps_o[:, 1 - u, :, :], irows[:, :], bs[:, 1 - u, :, :], start=True, stop=True).then_inc(out_done, 1)

            pe.wait_ge(taps_loaded, 80)
            pe.matmul(ps_k[0:TAPS, 0, 0:WU], up_f[:, :], sel[:, :], start=True, stop=True).then_inc(taps_done, 1)
            pe.matmul(ps_k[0:TAPS, 2, :], dn_f[:, :], pd[:, :], start=True, stop=True).then_inc(taps_done, 1)
            pe.wait_ge(taps_copied, 1)
            pe.matmul(ps_k[0:WU, 1, :], upc[:, :], pu[:, :], start=True, stop=True).then_inc(taps_done, 1)
            pe.wait_ge(loaded, 96)
            run_slots(pe, slot, NS, NS + 1)


def v_moments(v, link, st, mom, tmp, ready):
    link(v.memset(tmp, 0.0))
    row_stats(v, link, st, mom[:, 0, :], mom[:, 1, :], tmp)
    link(v.tensor_tensor(tmp, mom[:, 0, :], mom[:, 0, :], ALU.mult))
    v.tensor_tensor(mom[:, 1, :], mom[:, 1, :], tmp, ALU.add).then_inc(ready, 1)


def v_image_norm(v, link, ps, mom_done, n, mean, var, scale, bias, tmp, veps, root, gain, shift, var_ready, root_ready, nr):
    v.wait_ge(mom_done, n)
    link(v.tensor_copy(mean, ps[:, 0:NI]))
    link(v.tensor_tensor(tmp, mean, mean, ALU.mult))
    link(v.tensor_tensor(var, ps[:, NI:2 * NI], tmp, ALU.subtract))
    v.tensor_scalar(veps, var, 0.0, 1e-5, ALU.max, ALU.add).then_inc(var_ready, 1)
    v.wait_ge(var_ready, nr)
    newton_rsqrt(v, link, veps, root, scale, tmp, root_ready, nr)
    link(v.tensor_scalar(scale, scale, gain, None, ALU.mult))
    link(v.tensor_tensor(tmp, mean, scale, ALU.mult))
    link(v.tensor_scalar(bias, tmp, -1.0, shift, ALU.mult, ALU.add))


def stage_mixer(k):
    nc, a = k.nc, k.a
    with ExitStack() as ctx:
        sb = lambda name, shape: k.sb(name, shape, ctx=ctx)
        f, m = sb("s6_f", [HW, NI, HW]), sb("s6_m", [HW, NI, HW])
        st = k.st
        mom = sb("s6_mom", [128, 2, NI])
        names = ("mean", "var", "scale", "bias", "tmp", "veps", "root", "as", "ab", "cs", "cb", "fs", "fb", "ws", "wb")
        mean, var, scale, bias, tmp, veps, root, a_s, a_b, c_s, c_b, f_s, f_b, w_s, w_b = \
            (sb(f"s6_{n}", [128, NI]) for n in names)
        rows, cols = sb("s6_rows", [128, 128]), sb("s6_cols", [128, 256])
        icols, irows = sb("s6_icols", [128, 128]), sb("s6_irows", [128, 128])
        w = sb("s6_w", [128, 2, 2, NM])
        sk = sb("s6_sk", [128, 2, 2])
        pre = sb("s6_pre", [128, 2, STEP, HW])
        xg, yt, bs = (sb(f"s6_{n}", [128, 2, STEP, HW]) for n in ("xg", "yt", "bs"))
        z = sb("s6_z", [128, 2, STEP, 2, NM])
        ps_a, ps_b, ps_o = (k.ps(f"s6_{n}", [128, 2, STEP, HW], ctx) for n in ("psa", "psb", "pso"))
        ps_x = k.ps("s6_psx", [128, 2, 512], ctx)
        loaded, chain = k.sem("s6_loaded"), k.sem("s6_chain")
        mom_ready, mom_done = k.sem("s6_mom_ready"), k.sem("s6_mom_done")
        var_ready, root_ready = k.sem("s6_var_ready"), k.sem("s6_root_ready")
        xg_ready, rows_done, yt_ready = k.sem("s6_xg_ready"), k.sem("s6_rows_done"), k.sem("s6_yt_ready")
        spec_done, z_ready = k.sem("s6_spec_done"), k.sem("s6_z_ready")
        cols_done, bs_ready, out_done = k.sem("s6_cols_done"), k.sem("s6_bs_ready"), k.sem("s6_out_done")
        f_ready, part_ready, pre_ready = k.sem("s6_f_ready"), k.sem("s6_part_ready"), k.sem("s6_pre_ready")
        m_kept, xa_ready, w_signed = k.sem("s6_m_kept"), k.sem("s6_xa_ready"), k.sem("s6_w_signed")
        skip_ready, skip_added, g_ready = k.sem("s6_skip_ready"), k.sem("s6_skip_added"), k.sem("s6_g_ready")
        x_added = k.sem("s6_x_added")
        block = ctx.enter_context(nc.Block())

        @block.sync
        def _(sp):
            sp.dma_start(rows[:, :], a["dft_rows"][:, 0:128]).then_inc(loaded, 16)
            sp.dma_start(cols[:, :], a["dft_cols"]).then_inc(loaded, 16)
            sp.dma_start(irows[:, :], a["idft_rows"]).then_inc(loaded, 16)
            for h in range(2):
                sp.dma_start(icols[64 * h:64 * h + 64, :], a["idft_cols"]).then_inc(loaded, 16)
            for j in range(2):
                sp.dma_start(w[0:64, j, :, :], a[f"wM{j}"]).then_inc(loaded, 16)
                for c in range(2):
                    sp.dma_start(w[64:128, j, 1 - c, :], a[f"wM{j}"][:, c, :]).then_inc(loaded, 16)
                sp.dma_start(sk[:, j, 0:1], sub(a[f"wM{j}s"], 0, [[0, 128], [1, 1]])).then_inc(loaded, 16)
                sp.dma_start(sk[:, j, 1:2], sub(a[f"bM{j}s"], 0, [[0, 128], [1, 1]])).then_inc(loaded, 16)
            sp.wait_ge(loaded, 15 * 16)

        @block.vector
        def _(v):
            link = Chain(v, chain)
            tt = lambda o, x, y, op: link(v.tensor_tensor(o, x, y, op))
            norm = lambda n, s_, b_: v_image_norm(
                v, link, ps_x[:, 0, :], mom_done, n, mean[:, :], var[:, :], s_[:, :], b_[:, :], tmp[:, :], veps[:, :],
                root[:, :], k.norm_g[:, order[n - 1]:order[n - 1] + 1], k.norm_b[:, order[n - 1]:order[n - 1] + 1],
                var_ready, root_ready, n + (n > 1))
            order = (1, 3, 4, 5)
            v.wait_ge(loaded, 15 * 16)
            v_moments(v, link, st, mom, tmp[:, :], mom_ready)
            v.tensor_scalar(w[64:128, :, 1, :], w[64:128, :, 1, :], -1.0, None, ALU.mult).then_inc(w_signed, 1)
            norm(1, scale, bias)
            tt(tmp[:, :], scale[:, :], scale[:, :], ALU.mult)
            tt(veps[:, :], var[:, :], tmp[:, :], ALU.mult)
            v.tensor_scalar(veps[:, :], veps[:, :], 1e-5, None, ALU.add).then_inc(var_ready, 1)
            v.wait_ge(var_ready, 2)
            newton_rsqrt(v, link, veps[:, :], root[:, :], a_s[:, :], tmp[:, :], root_ready, 2)
            link(v.tensor_scalar(a_s[:, :], a_s[:, :], k.norm_g[:, 2:3], None, ALU.mult))
            link(v.tensor_scalar(tmp[:, :], a_s[:, :], k.norm_b[:, 1:2], None, ALU.mult))
            link(v.tensor_scalar(a_b[:, :], tmp[:, :], -1.0, k.norm_b[:, 2:3], ALU.mult, ALU.add))
            tt(c_s[:, :], scale[:, :], a_s[:, :], ALU.mult)
            tt(tmp[:, :], bias[:, :], a_s[:, :], ALU.mult)
            tt(c_b[:, :], tmp[:, :], a_b[:, :], ALU.add)
            v.wait_ge(w_signed, 1)

            def multiply(s, u, n0):
                v.wait_ge(spec_done, s + (n0 + 1))
                wait_count(v, cols_done, s + (n0 - 1))
                src = ps_x[:, u, 0:STEP * NM].rearrange("p (i m) -> p i m", m=NM)
                for c in range(2):
                    ins = v.tensor_tensor(z[:, u, :, c, :], src,
                                          w[:, n0 // NS, c:c + 1, :].broadcast_to([128, STEP, NM]), ALU.mult)
                ins.then_inc(z_ready, 1)

            def stats(s, n0):
                v.wait_ge(f_ready, s + (n0 + 1))
                for j in range(STEP):
                    one = bass.ds(STEP * s + j, 1)
                    v.bn_stats(st[:, one, :], f[:, one, :])

            def norm_in(s, u):
                wait_count(v, rows_done, s + (-1))
                for j in range(STEP):
                    one = bass.ds(STEP * s + j, 1)
                    ins = v.tensor_scalar(xg[:, u, j, :], k.xa[:, one, :], c_s[:, one], c_b[:, one], ALU.mult, ALU.add)
                ins.then_inc(xg_ready, 1)

            def slot0(s, u):
                if during(s, 0):
                    multiply(s, u, 0)
                if during(s + 2, 2):
                    norm_in(s + 2, u)
                if during(s + (-3), 0):
                    stats(s + (-3), 0)

            norm_in(0, 0)
            norm_in(1, 1)
            run_slots(v, slot0, NS - 2, NS + 3)
            v_moments(v, link, st, mom, tmp[:, :], mom_ready)
            norm(2, f_s, f_b)
            link(v.tensor_scalar(w_s[:, :], a_s[:, :], sk[:, 0, 0:1], None, ALU.mult))
            link(v.tensor_scalar(tmp[:, :], a_b[:, :], sk[:, 0, 0:1], sk[:, 0, 1:2], ALU.mult, ALU.add))
            v.tensor_tensor(w_b[:, :], f_b[:, :], tmp[:, :], ALU.add).then_inc(skip_ready, 1)

            def skip(s, u):
                v.wait_ge(part_ready, s + 1)
                wait_count(v, xg_ready, s + (NS - 1))
                for j in range(STEP):
                    one = bass.ds(STEP * s + j, 1)
                    ins = v.scalar_tensor_tensor(out=pre[:, u, j, :], in0=k.xa[:, one, :], scalar=w_s[:, one],
                                                 in1=f[:, one, :], op0=ALU.mult, op1=ALU.add)
                ins.then_inc(pre_ready, 1)

            def slot1(s, u):
                if during(s, 0):
                    multiply(s, u, NS)
                if during(s + 3, 3):
                    skip(s + 3, 1 - u)
                if during(s + (-3), 0):
                    stats(s + (-3), NS)

            v.wait_ge(xa_ready, NS)
            v.wait_ge(skip_ready, 1)
            for s in range(3):
                skip(s, s % 2)
            run_slots(v, slot1, NS - 4, NS + 3)
            v_moments(v, link, st, mom, tmp[:, :], mom_ready)
            norm(3, f_s, f_b)
            v.tensor_scalar(w_b[:, :], f_b[:, :], sk[:, 1, 1:2], None, ALU.add).then_inc(skip_ready, 1)
            v.wait_ge(m_kept, NS)
            with v.Fori(0, NS) as s:
                v.wait_ge(part_ready, s + (NS + 1))
                fg = f[:, images(s), :]
                v.scalar_tensor_tensor(out=fg, in0=m[:, images(s), :], scalar=sk[:, 1, 0:1], in1=fg,
                                       op0=ALU.mult, op1=ALU.add).then_inc(skip_added, 1)
                v.wait_ge(skip_added, s + 1)
                for j in range(STEP):
                    one = bass.ds(STEP * s + j, 1)
                    v.bn_stats(st[:, one, :], f[:, one, :])
            v_moments(v, link, st, mom, tmp[:, :], mom_ready)
            norm(4, scale, bias)
            v.memset(tmp[:, :], 0.0).then_inc(skip_ready, 1)
            v.wait_ge(x_added, 1)
            with v.Fori(0, NS) as s:
                v.wait_ge(g_ready, s + 1)
                xs = k.x[:, images(s), :]
                v.tensor_tensor(xs, xs, f[:, images(s), :], ALU.add).then_inc(x_added, 1)
                v.wait_ge(x_added, s + 2)
                for j in range(STEP):
                    one = bass.ds(STEP * s + j, 1)
                    v.bn_stats(st[:, one, :], k.x[:, one, :])

        @block.gpsimd
        def _(p):
            with p.Fori(0, NS // 2) as i:
                for u in range(2):
                    p.wait_ge(xg_ready, 2 * i + (u + NS + 1))
                    p.tensor_copy(m[:, images(2 * i + u), :], xg[:, u, :, :]).then_inc(m_kept, 1)
            p.tensor_tensor(k.x[:, :, :], k.x[:, :, :], k.xa[:, :, :], ALU.add).then_inc(x_added, 1)

        @block.scalar
        def _(s_):
            def root_step(n):
                s_.wait_ge(var_ready, n)
                s_.activation(root[:, :], veps[:, :], ACT.Sqrt).then_inc(root_ready, 1)

            def affine(dst, s, scale_, bias_, done):
                for j in range(STEP):
                    one = bass.ds(STEP * s + j, 1)
                    ins = s_.activation(dst[:, one, :], dst[:, one, :], ACT.Identity, scale=scale_[:, one], bias=bias_[:, one])
                ins.then_inc(done, 1)

            def copies(t, u, n0):
                if during(t, 0):
                    s_.wait_ge(rows_done, t + (n0 + 1))
                    wait_count(s_, spec_done, t + (n0 - 1))
                    s_.activation(yt[:, u, :, :], ps_a[:, u, :, :], ACT.Copy).then_inc(yt_ready, 1)

            def copies_back(t, u, n0):
                if during(t + (-2), 0):
                    s_.wait_ge(cols_done, t + (n0 - 1))
                    wait_count(s_, out_done, t + (n0 - 3))
                    s_.activation(bs[:, u, :, :], ps_b[:, u, :, :], ACT.Copy).then_inc(bs_ready, 1)
                if during(t + (-3), 0):
                    s_.wait_ge(out_done, t + (n0 - 2))
                    s_.activation(f[:, images(t + (-3)), :], ps_o[:, 1 - u, :, :], ACT.Copy).then_inc(f_ready, 1)

            def slot0(t, u):
                copies(t, u, 0)
                if during(t, 0):
                    s_.wait_ge(xg_ready, t + 1)
                    affine(k.xa, t, scale, bias, xa_ready)
                copies_back(t, u, 0)

            def part(s):
                affine(f, s, f_s, w_b, part_ready)

            def gelu(s, u):
                s_.wait_ge(pre_ready, s + 1)
                wait_count(s_, rows_done, s + (NS - 1))
                wait_count(s_, m_kept, s + (-1))
                s_.activation(xg[:, u, :, :], pre[:, u, :, :], ACT.Gelu).then_inc(xg_ready, 1)

            def slot1(t, u):
                copies(t, u, NS)
                if during(t + 2, 2):
                    gelu(t + 2, u)
                if during(t + 4, 4):
                    part(t + 4)
                copies_back(t, u, NS)

            root_step(1)
            root_step(2)
            run_slots(s_, slot0, NS, NS + 3)
            root_step(3)
            s_.wait_ge(skip_ready, 1)
            part(0)
            part(1)
            gelu(0, 0)
            part(2)
            gelu(1, 1)
            part(3)
            run_slots(s_, slot1, NS - 4, NS + 3)
            root_step(4)
            s_.wait_ge(skip_ready, 2)
            with s_.Fori(0, NS) as s:
                part(s)
            root_step(5)
            s_.wait_ge(skip_ready, 3)
            with s_.Fori(0, NS) as s:
                affine(f, s, scale, bias, g_ready)

        @block.tensor
        def _(pe):
            def moments(n):
                pe.wait_ge(mom_ready, n)
                pe.matmul(ps_x[:, 0, 0:128], k.ones[:, :], mom[:, :, :], start=True, stop=True).then_inc(mom_done, 1)

            def slot(t, u, n0):
                if during(t, 0):
                    pe.wait_ge(xg_ready, t + (n0 + 1))
                    wait_count(pe, yt_ready, t + (n0 - 1))
                    for j in range(STEP):
                        mm = pe.matmul(ps_a[:, u, j, :], xg[:, u, j, :], rows[:, :], start=True, stop=True)
                    mm.then_inc(rows_done, 1)
                if during(t + (-1), 0):
                    pe.wait_ge(yt_ready, t + n0)
                    wait_count(pe, z_ready, t + (n0 - 2))
                    out = ps_x[:, 1 - u, 0:STEP * NM]
                    pe.matmul(out, cols[:, 0:128], yt[:, 1 - u, :, 0:64], start=True, stop=False)
                    pe.matmul(out, cols[:, 128:256], yt[:, 1 - u, :, 64:128], start=False, stop=True).then_inc(spec_done, 1)
                if during(t + (-2), 0):
                    pe.wait_ge(z_ready, t + (n0 - 1))
                    wait_count(pe, bs_ready, t + (n0 - 3))
                    for j in range(STEP):
                        mm = pe.matmul(ps_b[:, u, j, :], z[:, u, j, :, :], icols[:, :], start=True, stop=True)
                    mm.then_inc(cols_done, 1)
                if during(t + (-3), 0):
                    pe.wait_ge(bs_ready, t + (n0 - 2))
                    wait_count(pe, f_ready, t + (n0 - 4))
                    pe.matmul(ps_o[:, 1 - u, :, :], irows[:, :], bs[:, 1 - u, :, :], start=True, stop=True).then_inc(out_done, 1)

            moments(1)
            pe.wait_ge(loaded, 15 * 16)
            pe.wait_ge(w_signed, 1)
            run_slots(pe, lambda t, u: slot(t, u, 0), NS, NS + 3)
            moments(2)
            run_slots(pe, lambda t, u: slot(t, u, NS), NS, NS + 3)
            moments(3)
            moments(4)


NK = FT + 2
NF = 2 * NK


def stage_stu_setup(k, stu):
    nc, a = k.nc, k.a
    HALF = FT // 2
    NCH = NF // 4
    with ExitStack() as ctx:
        sb = lambda name, shape: k.sb(name, shape, ctx=ctx)
        st = k.st
        mean, var, rstd, root, tmp, veps = (sb(f"s7_{n}", [128, NI]) for n in ("mean", "var", "rstd", "root", "tmp", "veps"))
        un = sb("s7_un", [128, 4, STEP, HW])
        mload = sb("s7_mload", [128, 2, HALF * 128])
        mp, mm_ = sb("s7_mp", [128, HALF * 128]), sb("s7_mm", [128, HALF * 128])
        mu, mut = sb("s7_mu", [128, 4, 3, 128]), sb("s7_mut", [128, 3, 128])
        lw, oh, ys = sb("s7_lw", [128, 2, 4]), sb("s7_oh", [128, 4]), sb("s7_ys", [128, 4])
        z4, t4, u4 = sb("s7_z4", [128, 4]), sb("s7_t4", [128, 4]), sb("s7_u4", [128, 4])
        one = sb("s7_one", [128, 2])
        masks = sb("s7_masks", [128, 4, NI])
        sig, sq, sr, s_t = (sb(f"s7_{n}", [128, FT]) for n in ("sig", "sq", "sr", "st4"))
        phi = sb("s7_phi", [33, 2, 4, 128])
        fb = sb("s7_fb", [33, 128])
        gt = sb("s7_gt", [64, 2, 4, 128, 2])
        ug = sb("s7_ug", [64, 2, GROUP, HW])
        xt = sb("s7_xt", [128, NQ, 2, 4, 64])
        fwd = sb("s7_fwd", [64, 2, 128])
        ps_f = k.ps("s7_psf", [128, 2, 512], ctx)
        ps = k.ps("s7_ps", [128, 2, 2, 4, 128], ctx)
        psl = k.ps("s7_psl", [128, 128], ctx)
        loaded, phi_loaded = k.sem("s7_loaded"), [k.sem(f"s7_phi{u}_loaded") for u in range(2)]
        m_loaded = [k.sem("s7_m0_loaded"), k.sem("s7_m1_loaded")]
        chain, var_ready, root_ready = k.sem("s7_chain"), k.sem("s7_var_ready"), k.sem("s7_root_ready")
        u_ready, u_stored, m_used = k.sem("s7_u_ready"), [k.sem(f"s7_u{n}_stored") for n in range(4)], k.sem("s7_m_used")
        exp_in, exp_done = k.sem("s7_exp_in"), k.sem("s7_exp_done")
        g_done, g_copied = k.sem("s7_g_done"), k.sem("s7_g_copied")
        g_stored = [k.sem(f"s7_g{u}_stored") for u in range(2)]
        m_ready, m_high = k.sem("s7_m_ready"), k.sem("s7_m_high")
        u_loaded = [k.sem("s7_u0_loaded"), k.sem("s7_u1_loaded")]
        done, copied, last, stored = k.sem("s7_done"), k.sem("s7_copied"), k.sem("s7_last"), k.sem("s7_stored")
        block = ctx.enter_context(nc.Block())
        blocked = lambda t: t.rearrange("d (k e) -> d k e", e=128)
        both = lambda pair, ks: tuple(m[:, ks, :] for m in pair)
        tails = [(both(stu.me, slice(FT, FT + 2)), mut[:, 0:3:2, :]), (both(stu.mo, slice(FT, FT + 1)), mut[:, 1:2, :])]

        def parts(h):
            ks = slice(HALF * h, HALF * h + HALF)
            return [(both(stu.me, ks), blocked(mp[:, :])), (both(stu.mo, ks), blocked(mm_[:, :]))] + (tails if h else [])

        @block.sync
        def _(sp):
            sp.dma_start(fb[:, :], a["filter_dft"]).then_inc(loaded, 16)
            sp.dma_start(lw[:, 0, :], sub(a["log_weights"], 0, [[0, 128], [1, 4]])).then_inc(loaded, 16)
            sp.dma_start(lw[:, 1, :], sub(a["gumbel"], 0, [[0, 128], [1, 4]])).then_inc(loaded, 16)
            sp.dma_start(sig[:, :], sub(a["sigma"], 0, [[0, 128], [1, FT]])).then_inc(loaded, 16)
            sp.dma_start(masks[:, :, :], sub(a["masks"], 0, [[0, 128], [NI, 4], [1, NI]])).then_inc(loaded, 16)
            sp.dma_start(mu[:, :, :, :].rearrange("d i t e -> d (i t) e"),
                         a["M_u"].rearrange("i t d e -> d (i t) e")).then_inc(loaded, 16)
            sp.dma_start(fwd[:, :, :], a["block_dft"].rearrange("p (u f) -> p u f", u=2)).then_inc(loaded, 16)
            for n in range(NCH):
                if n >= 2:
                    sp.wait_ge(g_done, n - 1)
                sp.dma_start(phi[:, n % 2, :, :], a["phi"][:, 4 * n:4 * n + 4, :]).then_inc(phi_loaded[n % 2], 16)
            with sp.Fori(0, NS // 4) as i:
                for n in range(4):
                    sp.wait_ge(u_ready, 4 * i + (n + 1))
                    sp.dma_start(a["u_d"][images(4 * i + n)].rearrange("i h w -> h i w"), un[:, n, :, :])\
                      .then_inc(u_stored[n], 16)
            for n in range(4):
                sp.wait_ge(u_stored[n], 4 * NS + 1)
            with sp.Fori(0, 8) as i:
                for u in range(2):
                    sp.wait_ge(done, 2 * i + (1 + u))
                    sp.dma_start(ug[:, u, :, :],
                                 sub(a["u_d"], (2 * i + u) * GROUP * HW, [[PIX, NI], [HW, GROUP], [1, HW]]))\
                      .then_inc(u_loaded[u], 16)
            sp.wait_ge(copied, 2 + 32)
            for n in range(4):
                sp.dma_start(sub(a["xt_d"], n * 8 * 65536, [[512, 128], [65536, 8], [1, 512]]),
                             xt[:, 8 * n:8 * n + 8, :, :, :].rearrange("d q s f t -> d q (s f t)")).then_inc(stored, 16)
            sp.wait_ge(stored, 64)

        @block.gpsimd
        def _(p):
            for n in range(16):
                h, i, src = n // 8, n // 2 % 4, a["M_phi_plus"] if n % 2 == 0 else a["M_phi_minus"]
                if n >= 2:
                    p.wait_ge(m_used, n - 1)
                p.dma_start(blocked(mload[:, n % 2, :]), src[i, HALF * h:HALF * h + HALF].rearrange("k d e -> d k e"))\
                 .then_inc(m_loaded[n % 2], 16)

        @block.vector
        def _(v):
            link = Chain(v, chain)
            tt = lambda o, x, y, op: link(v.tensor_tensor(o, x, y, op))
            ts = lambda o, x, s1, s2, op0, op1=None: link(v.tensor_scalar(o, x, s1, s2, op0, op1) if op1 is not None
                                                          else v.tensor_scalar(o, x, s1, s2, op0))
            link(v.memset(tmp[:, :], 0.0))
            row_stats(v, link, st, mean[:, :], var[:, :], tmp[:, :])
            v.tensor_scalar(veps[:, :], var[:, :], 1e-5, None, ALU.add).then_inc(var_ready, 1)
            v.wait_ge(var_ready, 1)
            newton_rsqrt(v, link, veps[:, :], root[:, :], rstd[:, :], tmp[:, :], root_ready, 1)
            for n in range(4):
                v.sem_inc(u_stored[n], 1)
            with v.Fori(0, NS // 4) as i:
                for n in range(4):
                    v.wait_ge(u_stored[n], 16 * i + 1)
                    for j in range(STEP):
                        o = bass.ds(STEP * (4 * i + n) + j, 1)
                        ins = v.tensor_scalar(un[:, n, j, :], k.x[:, o, :], mean[:, o], rstd[:, o], ALU.subtract, ALU.mult)
                    ins.then_inc(u_ready, 1)
            v.wait_ge(loaded, 112)
            tt(z4[:, :], lw[:, 0, :], lw[:, 1, :], ALU.add)
            link(v.tensor_reduce(one[:, 0:1], z4[:, :], AX.X, ALU.max))
            v.tensor_scalar(z4[:, :], z4[:, :], one[:, 0:1], None, ALU.subtract).then_inc(exp_in, 1)
            v.wait_ge(exp_done, 1)
            link(v.tensor_reduce(one[:, 0:1], t4[:, :], AX.X, ALU.add))
            link(v.reciprocal(one[:, 1:2], one[:, 0:1]))
            ts(ys[:, :], t4[:, :], one[:, 1:2], None, ALU.mult)
            link(v.tensor_reduce(one[:, 0:1], ys[:, :], AX.X, ALU.max))
            ts(u4[:, :], ys[:, :], one[:, 0:1], None, ALU.is_equal)
            link(v.memset(one[:, 1:2], 1.0))
            for i in range(4):
                tt(oh[:, i:i + 1], u4[:, i:i + 1], one[:, 1:2], ALU.mult)
                tt(one[:, 1:2], one[:, 1:2], oh[:, i:i + 1], ALU.subtract)
            tt(t4[:, :], oh[:, :], ys[:, :], ALU.subtract)
            tt(t4[:, :], t4[:, :], ys[:, :], ALU.add)
            for i in range(4):
                if i == 0:
                    ts(stu.mask[:, :], masks[:, i, :], oh[:, i:i + 1], None, ALU.mult)
                else:
                    link(v.scalar_tensor_tensor(out=stu.mask[:, :], in0=masks[:, i, :], scalar=oh[:, i:i + 1],
                                                in1=stu.mask[:, :], op0=ALU.mult, op1=ALU.add))
            ts(sq[:, :], sig[:, :], 1.0, None, ALU.mult)
            for n in range(2):
                v.tensor_scalar(s_t[:, :], sq[:, :], 1.0, None, ALU.mult).then_inc(var_ready, 1)
                v.wait_ge(root_ready, n + 2)
                ts(s_t[:, :], sr[:, :], 1e-30, None, ALU.max)
                link(v.reciprocal(s_t[:, :], s_t[:, :]))
                tt(s_t[:, :], s_t[:, :], sq[:, :], ALU.mult)
                tt(s_t[:, :], s_t[:, :], sr[:, :], ALU.add)
                ts(sq[:, :], s_t[:, :], 0.5, None, ALU.mult)
            for h in range(2):
                for j in range(8):
                    n, acc = 8 * h + j, mp if j % 2 == 0 else mm_
                    v.wait_ge(m_loaded[j % 2], 16 * (n // 2) + 16)
                    if j < 2:
                        v.tensor_scalar(acc[:, :], mload[:, j % 2, :], t4[:, 0:1], None, ALU.mult).then_inc(m_used, 1)
                    else:
                        v.scalar_tensor_tensor(out=acc[:, :], in0=mload[:, j % 2, :], scalar=t4[:, j // 2:j // 2 + 1],
                                               in1=acc[:, :], op0=ALU.mult, op1=ALU.add).then_inc(m_used, 1)
                    v.wait_ge(m_used, n + 1)
                half_sq = sq[:, HALF * h:HALF * h + HALF].unsqueeze(2).broadcast_to([128, HALF, 128])
                for acc in (mp, mm_):
                    tt(blocked(acc[:, :]), blocked(acc[:, :]), half_sq, ALU.mult)
                tt(mp[:, :], mp[:, :], mm_[:, :], ALU.add)
                link(v.scalar_tensor_tensor(out=mm_[:, :], in0=mm_[:, :], scalar=-2.0, in1=mp[:, :],
                                            op0=ALU.mult, op1=ALU.add))
                if h:
                    for i in range(4):
                        if i == 0:
                            ts(mut[:, :, :], mu[:, i, :, :], t4[:, 0:1], None, ALU.mult)
                        else:
                            link(v.scalar_tensor_tensor(out=mut[:, :, :], in0=mu[:, i, :, :], scalar=t4[:, i:i + 1],
                                                        in1=mut[:, :, :], op0=ALU.mult, op1=ALU.add))
                v.memset(one[:, 0:1], 0.0).then_inc(m_ready, 1)
                v.wait_ge(m_high, h + 1)
                for (high, low), raw in parts(h):
                    ins = v.tensor_tensor(low, raw, high.bitcast(F32), ALU.subtract)
                link(ins)

        @block.scalar
        def _(s):
            s.wait_ge(var_ready, 1)
            s.activation(root[:, :], veps[:, :], ACT.Sqrt).then_inc(root_ready, 1)
            for n in range(NCH):
                s.wait_ge(g_done, n + 1)
                if n >= 2:
                    s.wait_ge(g_stored[n % 2], 32 * (n // 2))
                for r in range(4):
                    dst = gt[32 * (r // 2):32 * (r // 2) + 32, n % 2, :, :, r % 2]
                    ins = s.activation(dst, ps_f[32 * r:32 * r + 32, n % 2, :].rearrange("p (f x) -> p f x", x=128), ACT.Copy)
                ins.then_inc(g_copied, 1)
                s.wait_ge(g_copied, n + 1)
                for c in range(2):
                    s.dma_start(sub(a["tc_d"], c * NF * 256 + n * 1024, [[2 * NF * 256, NQ], [1, 1024]]),
                                gt[32 * c:32 * c + 32, n % 2, :, :, :].rearrange("p f x c -> p (f x c)")).then_inc(g_stored[n % 2], 16)
            s.wait_ge(exp_in, 1)
            s.activation(t4[:, :], z4[:, :], ACT.Exp).then_inc(exp_done, 1)
            for n in range(2):
                s.wait_ge(var_ready, n + 2)
                s.activation(sr[:, :], s_t[:, :], ACT.Sqrt).then_inc(root_ready, 1)
            s.sem_inc(copied, 2)
            for part in range(2):
                with s.Fori(0, 4) as i:
                    for u in range(2):
                        n = 2 * i + (8 * part + u)
                        s.wait_ge(done, n + 3)
                        for h in range(2):
                            dst = xt[:, :, h, :, bass.ds(n * 4, 4)].rearrange("d q f t -> d t f q")
                            s.activation(dst, ps[:, u, h, :, :].rearrange("d t (f q) -> d t f q", q=NQ), ACT.Copy)\
                             .then_inc(copied, 1)
                s.wait_ge(m_ready, part + 1)
                for (high, low), raw in parts(part):
                    ins = s.activation(high, raw, ACT.Copy)
                ins.then_inc(m_high, 1)
            s.wait_ge(last, 1)
            s.activation(stu.xl[:, :], psl[:, :], ACT.Copy)
            for u in range(2):
                s.wait_ge(g_stored[u], 32 * ((NCH + 1 - u) // 2))

        @block.tensor
        def _(pe):
            pe.wait_ge(loaded, 112)
            for n in range(NCH):
                pe.wait_ge(phi_loaded[n % 2], 16 * (n // 2) + 16)
                if n >= 2:
                    pe.wait_ge(g_copied, n - 1)
                pe.matmul(ps_f[:, n % 2, :], fb[:, :], phi[:, n % 2, :, :], start=True, stop=True).then_inc(g_done, 1)
            pe.sem_inc(done, 2)
            with pe.Fori(0, 8) as i:
                for u in range(2):
                    pe.wait_ge(u_loaded[u], 16 * i + 16)
                    pe.wait_ge(copied, 4 * i + 2)
                    for j in range(GROUP):
                        mm = pe.matmul(ps[:, u, j % 2, j // 2, :], ug[:, u, j, :], fwd[:, 0, :], start=True, stop=True)
                    mm.then_inc(done, 1)
            pe.matmul(psl[:, :], ug[:, 1, GROUP - 1, :], fwd[:, 1, :], start=True, stop=True).then_inc(last, 1)


def stage_stu_filter(k, stu):
    nc, a = k.nc, k.a
    CH = [4, 4, 4, 4, 2]
    NC = len(CH)
    UN = 8 * NC
    BANKS = 5
    with ExitStack() as ctx:
        sb = lambda name, shape, dt=F32: k.sb(name, shape, dt, ctx=ctx)
        raw = sb("s9_raw", [128, 2, 8, 128])
        tc = [sb(f"s9_tc_{n}", [128, 2, 8, 128], F32R) for n in ("high", "low")]
        xq = sb("s9_xq", [128, 2, 2, 4, 64])
        xs = [sb(f"s9_xs_{n}", [128, 2, 3, 4, 64], F32R) for n in ("high", "low")]
        w = [sb(f"s9_w_{n}", [128, 2, 4, 2, 2, B, 128], F32R) for n in ("high", "low")]
        y = sb("s9_y", [128, 2, 512])
        psw = k.ps("s9_psw", [128, BANKS, 512], ctx)
        psy = k.ps("s9_psy", [128, 2, 512], ctx)
        raw_loaded, xq_loaded = [k.sem(f"s9_raw{u}_loaded") for u in range(2)], [k.sem(f"s9_xq{u}_loaded") for u in range(2)]
        y_stored = [k.sem(f"s9_y{u}_stored") for u in range(2)]
        xs_high, xs_ready = k.sem("s9_xs_high"), k.sem("s9_xs_ready")
        w_done, w_high, w_ready = k.sem("s9_w_done"), k.sem("s9_w_high"), k.sem("s9_w_ready")
        tc_high, tc_ready = k.sem("s9_tc_high"), k.sem("s9_tc_ready")
        filt_done, y_copied = k.sem("s9_filt_done"), k.sem("s9_y_copied")
        block = ctx.enter_context(nc.Block())

        def source(p, s):
            return s if p == 0 else 2 - 2 * s

        @block.sync
        def _(sp):
            for u in range(2):
                sp.sem_inc(y_stored[u], 1)
            with sp.Fori(0, NQ // 2) as i:
                for u in range(2):
                    q = 2 * i + u
                    sp.wait_ge(xs_ready, q + 1)
                    sp.dma_start(xq[:, u, :, :, :].rearrange("d s f t -> d (s f t)"),
                                 sub(a["xt_d"], q * 65536, [[512, 128], [1, 512]])).then_inc(xq_loaded[u], 16)
                    for c in range(NC):
                        n = u * NC + c
                        sp.wait_ge(tc_ready, i * (2 * NC) + (n + 1))
                        for h in range(2):
                            sp.dma_start(raw[64 * h:64 * h + 64, n % 2, 0:2 * CH[c], :],
                                         sub(a["tc_d"], (2 * q + h) * (NF * 256) + c * (8 * 256),
                                             [[2, 64], [256, 2 * CH[c]], [1, 128]])).then_inc(raw_loaded[n % 2], 16)
            for u in range(2):
                sp.wait_ge(y_stored[u], 16 * NQ + 1)

        @block.gpsimd
        def _(p):
            xl = stu.xl[:, :].rearrange("d (f q) -> d f q", f=4)

            def split(u, q, turn):
                p.wait_ge(xq_loaded[u], turn)
                p.tensor_copy(xs[0][:, u, 2, :, 0:1], xl[:, :, bass.ds(q, 1)])
                p.tensor_copy(xs[0][:, u, 0:2, :, :], xq[:, u, :, :, :])
                p.tensor_copy(xs[0][:, u, 2, :, 1:64], xq[:, u, 1, :, 0:63]).then_inc(xs_high, 1)
                p.wait_ge(xs_high, q + 1)
                high = xs[0][:, :, :, :, :].bitcast(F32)
                p.tensor_tensor(xs[1][:, u, 0:2, :, :], xq[:, u, :, :, :], high[:, u, 0:2, :, :], ALU.subtract)
                p.tensor_tensor(xs[1][:, u, 2, :, 1:64], xq[:, u, 1, :, 0:63], high[:, u, 2, :, 1:64], ALU.subtract)
                p.tensor_tensor(xs[1][:, u, 2, :, 0:1], xl[:, :, bass.ds(q, 1)], high[:, u, 2, :, 0:1], ALU.subtract)\
                 .then_inc(xs_ready, 1)

            p.sem_inc(xs_ready, 2)
            split(0, 0, 16)
            split(1, 1, 16)
            with p.Fori(0, NQ // 2 - 1) as i:
                for u in range(2):
                    p.wait_ge(w_done, (2 * i + u) * UN + UN)
                    split(u, 2 * i + (u + 2), 16 * i + 32)

        @block.tensor
        def _(pe):
            pe.sem_inc(filt_done, 2)
            with pe.Fori(0, NQ // 2) as i:
                for u in range(2):
                    q = 2 * i + u
                    pe.wait_ge(xs_ready, q + 3)
                    for c in range(NC + 1):
                        if c < NC:
                            for j in range(8):
                                pr, s, b = j // 4, j // 2 % 2, j % 2
                                n = 8 * c + j
                                pe.wait_ge(w_ready, q * UN + (n + 1))
                                m = stu.me if pr == 0 else stu.mo
                                kk = CH[c] - (c == NC - 1) * pr
                                passes(pe.matmul, psw[:, n % BANKS, 0:128 * kk],
                                       [x[:, u, source(pr, s), 2 * b:2 * b + 2, :] for x in xs],
                                       [x[:, 4 * c:4 * c + kk, :] for x in m], True, True).then_inc(w_done, 1)
                        if c == 1:
                            pe.wait_ge(y_copied, q + 1)
                        if c > 0:
                            g = c - 1
                            slot = (u * NC + g) % 2
                            pe.wait_ge(tc_ready, q * NC + (g + 3))
                            pe.wait_ge(w_ready, q * UN + (8 * c + BANKS))
                            for kk in range(CH[g]):
                                for pr in range(2):
                                    f = 2 * (4 * g + kk) + pr
                                    if f == NF - 1:
                                        continue
                                    mm = passes(pe.matmul, psy[:, u, :], [x[:, slot, 2 * kk + pr, :] for x in tc],
                                                [x[:, slot, kk, pr, :, :, :] for x in w], f == 0, f == NF - 2)
                            mm.then_inc(filt_done, 1)

        def products(c):
            for j in range(8):
                pr, s, b = j // 4, j // 2 % 2, j % 2
                yield 8 * c + j, CH[c] - (c == NC - 1) * pr, (pr, s, b)

        @block.scalar
        def _(s):
            s.sem_inc(y_copied, 2)
            with s.Fori(0, NQ // 2) as i:
                for u in range(2):
                    q = 2 * i + u
                    for c in range(NC):
                        n = u * NC + c
                        s.wait_ge(filt_done, i * (2 * NC) + (n + 1))
                        s.wait_ge(raw_loaded[n % 2], 32 * NC * i + 32 * (n // 2 + 1))
                        s.activation(tc[0][:, n % 2, 0:2 * CH[c], :], raw[:, n % 2, 0:2 * CH[c], :], ACT.Copy)\
                         .then_inc(tc_high, 1)
                        for m, kk, at in products(c):
                            s.wait_ge(w_done, q * UN + (m + 1))
                            s.activation(w[0][:, n % 2, 0:kk, at[0], at[1], at[2], :],
                                         psw[:, m % BANKS, 0:128 * kk].rearrange("p (k e) -> p k e", e=128),
                                         ACT.Copy).then_inc(w_high, 1)
                    s.wait_ge(filt_done, q * NC + (NC + 2))
                    s.wait_ge(y_stored[u], 32 * i + 1)
                    s.activation(y[:, u, :], psy[:, u, :], ACT.Copy).then_inc(y_copied, 1)
                    s.wait_ge(y_copied, q + 3)
                    for c in range(2):
                        s.dma_start(sub(a["yh_d"], (2 * q + c) * (64 * 512), [[512, 64], [1, 512]]), y[c::2, u, :])\
                         .then_inc(y_stored[u], 16)

        @block.vector
        def _(v):
            v.sem_inc(w_ready, BANKS)
            v.sem_inc(tc_ready, 2)
            with v.Fori(0, NQ // 2) as i:
                for u in range(2):
                    q = 2 * i + u
                    for c in range(NC):
                        n = u * NC + c
                        v.wait_ge(tc_high, i * (2 * NC) + (n + 1))
                        raw_c, high = raw[:, n % 2, 0:2 * CH[c], :], tc[0][:, n % 2, 0:2 * CH[c], :]
                        v.tensor_tensor(tc[1][:, n % 2, 0:2 * CH[c], :], raw_c, high.bitcast(F32), ALU.subtract)\
                         .then_inc(tc_ready, 1)
                        for m, kk, at in products(c):
                            v.wait_ge(w_high, q * UN + (m + 1))
                            v.tensor_tensor(w[1][:, n % 2, 0:kk, at[0], at[1], at[2], :],
                                            psw[:, m % BANKS, 0:128 * kk].rearrange("p (k e) -> p k e", e=128),
                                            w[0][:, n % 2, 0:kk, at[0], at[1], at[2], :].bitcast(F32),
                                            ALU.subtract).then_inc(w_ready, 1)


def stage_stu_output(k, stu):
    nc, a = k.nc, k.a
    with ExitStack() as ctx:
        sb = lambda name, shape: k.sb(name, shape, ctx=ctx)
        zq = sb("s10_zq", [128, 2, 16, HW])
        yn = sb("s10_yn", [64, 2, 16, HW])
        inv = sb("s10_inv", [128, 64])
        yg = sb("s10_yg", [128, 2, GROUP, HW])
        ps = k.ps("s10_ps", [64, 2, 16, HW], ctx)
        loaded, z_loaded = k.sem("s10_loaded"), [k.sem(f"s10_z{u}_loaded") for u in range(2)]
        done, copied, stored = k.sem("s10_done"), k.sem("s10_copied"), [k.sem(f"s10_y{u}_stored") for u in range(2)]
        y_loaded, added = [k.sem(f"s10_y{u}_loaded") for u in range(2)], k.sem("s10_added")
        block = ctx.enter_context(nc.Block())

        @block.sync
        def _(sp):
            sp.dma_start(inv[:, :], a["block_idft"]).then_inc(loaded, 16)
            with sp.Fori(0, 4) as i:
                for u in range(2):
                    sp.wait_ge(done, 2 * i + (u + 1))
                    for b in range(B):
                        for c in range(2):
                            sp.dma_start(zq[64 * b + 32 * c:64 * b + 32 * c + 32, u, :, :],
                                         sub(a["yh_d"], c * 32768 + b * 128 + (2 * i + u) * (8 * 512),
                                             [[65536, NQ], [256, 16], [1, 128]])).then_inc(z_loaded[u], 16)
            for u in range(2):
                sp.wait_ge(stored[u], 16 * 4 + 1)
            with sp.Fori(0, 4) as i:
                for u in range(2):
                    sp.wait_ge(added, 2 * i + (u + 1))
                    sp.dma_start(yg[:, u, :, :],
                                 a["y_d"][bass.ds((2 * i + u) * GROUP, GROUP)].rearrange("i h w -> h i w"))\
                      .then_inc(y_loaded[u], 16)
            sp.wait_ge(added, 10)

        @block.tensor
        def _(pe):
            pe.sem_inc(done, 2)
            pe.wait_ge(loaded, 16)
            with pe.Fori(0, 4) as i:
                for u in range(2):
                    pe.wait_ge(z_loaded[u], 64 * i + 64)
                    pe.wait_ge(copied, 2 * i + (u + 1))
                    for j in range(0, 16, 4):
                        mm = pe.matmul(ps[:, u, j:j + 4, :], inv[:, :], zq[:, u, j:j + 4, :], start=True, stop=True)
                    mm.then_inc(done, 1)

        @block.scalar
        def _(s):
            s.sem_inc(copied, 2)
            for u in range(2):
                s.sem_inc(stored[u], 1)
            with s.Fori(0, 4) as i:
                for u in range(2):
                    s.wait_ge(done, 2 * i + (u + 3))
                    s.wait_ge(stored[u], 16 * i + 1)
                    for j in range(8):
                        ins = s.activation(yn[:, u, 14 - 2 * j:16 - 2 * j, :], ps[:, u, 2 * j:2 * j + 2, :], ACT.Copy)
                    ins.then_inc(copied, 1)
                    s.wait_ge(copied, 2 * i + (u + 3))
                    s.dma_start(sub(a["y_d"], (112 - 16 * (2 * i + u)) * HW, [[PIX, NI], [HW, 16], [1, HW]]), yn[:, u, :, :])\
                     .then_inc(stored[u], 16)

        @block.vector
        def _(v):
            v.sem_inc(added, 2)
            with v.Fori(0, 4) as i:
                for u in range(2):
                    v.wait_ge(y_loaded[u], 16 * i + 16)
                    for j in range(GROUP):
                        o = bass.ds((2 * i + u) * GROUP + j, 1)
                        ins = v.scalar_tensor_tensor(out=k.x[:, o, :], in0=yg[:, u, j, :], scalar=stu.mask[:, o],
                                                     in1=k.x[:, o, :], op0=ALU.mult, op1=ALU.add)
                    ins.then_inc(added, 1)
                    v.wait_ge(added, 2 * i + (u + 3))
                    for j in range(GROUP):
                        o = bass.ds((2 * i + u) * GROUP + j, 1)
                        v.bn_stats(k.st[:, o, :], k.x[:, o, :])


class Stu:

    def __init__(self, k, ctx):
        pair = lambda name, n: tuple(k.sb(f"stu_{name}_{part}", [128, n, 128], F32R, ctx=ctx) for part in ("high", "low"))
        self.mask = k.sb("stu_mask", [128, NI], ctx=ctx)
        self.xl = k.sb("stu_xl", [128, 128], ctx=ctx)
        self.me = pair("me", NK)
        self.mo = pair("mo", NK - 1)


def v_row_norm(v, link, st, mean, var, rstd, root, tmp, eps, var_ready, root_ready):
    link(v.memset(tmp, 0.0))
    row_stats(v, link, st, mean, var, tmp)
    link(v.tensor_scalar(tmp, var, eps, None, ALU.add))
    v.tensor_copy(var, tmp).then_inc(var_ready, 1)
    v.wait_ge(var_ready, 1)
    newton_rsqrt(v, link, var, root, rstd, tmp, root_ready, 1)


PADW = HW + 6
GAIN = float(np.sqrt(2.0))


def stage_resample_conv(k):
    nc, a = k.nc, k.a
    ROUNDS = NI // 8
    with ExitStack() as ctx:
        sb = lambda name, shape, dt=F32: k.sb(name, shape, dt, ctx=ctx)
        pair = lambda name, shape: [sb(f"{name}_{part}", shape, F32R) for part in ("high", "low")]
        mean, var, rstd, root, tmp, bias = (sb(f"s11_{n}", [128, NI]) for n in ("mean", "var", "rstd", "root", "tmp", "bias"))
        v_raw = sb("s11_v_raw", [128, 2, 4, HW])
        v_in = pair("s11_v", [128, 2, 4, PADW])
        m_raw = sb("s11_m_raw", [128, 4, 4, HW])
        mid = pair("s11_mid", [128, 2, 4, 4, PADW])
        bands = sb("s11_bands", [128, 2 * WU + 2 * TAPS, 128])
        band = pair("s11_band", [128, 2 * WU + 2 * TAPS, 128])
        cut = (slice(0, 2 * WU), slice(2 * WU, 2 * WU + 2 * TAPS))
        bu, bd = [t[:, 0:2 * WU, :] for t in band], [t[:, 2 * WU:, :] for t in band]
        ps_m = k.ps("s11_psm", [128, 4, 512], ctx)
        ps_z = k.ps("s11_psz", [128, 2, 512], ctx)
        loaded, bands_loaded = k.sem("s11_loaded"), [k.sem(f"s11_bands{n}_loaded") for n in range(2)]
        bands_high, bands_ready = k.sem("s11_bands_high"), k.sem("s11_bands_ready")
        chain, var_ready, root_ready = k.sem("s11_chain"), k.sem("s11_var_ready"), k.sem("s11_root_ready")
        v_normed, v_high, v_ready, padded = k.sem("s11_v_normed"), k.sem("s11_v_high"), k.sem("s11_v_ready"), k.sem("s11_padded")
        mid_done, mid_copied, mid_leaky = k.sem("s11_mid_done"), k.sem("s11_mid_copied"), k.sem("s11_mid_leaky")
        mid_high, mid_ready = k.sem("s11_mid_high"), k.sem("s11_mid_ready")
        z_done, z_added = k.sem("s11_z_done"), k.sem("s11_z_added")
        block = ctx.enter_context(nc.Block())

        @block.sync
        def _(sp):
            sp.dma_start(bands[:, 0:2 * WU, :], sub(a["gu_d"], 0, [[1, 128], [256, 2 * WU], [1, 128]]))\
              .then_inc(bands_loaded[0], 16)
            sp.dma_start(bias[:, :], sub(a["bias"], 0, [[0, 128], [1, NI]])).then_inc(loaded, 16)
            sp.dma_start(bands[:, 2 * WU:, :], sub(a["gd_d"], 0, [[1, 128], [256, 2 * TAPS], [1, 128]]))\
              .then_inc(bands_loaded[1], 16)
            for n in range(2):
                sp.wait_ge(bands_loaded[n], 16)

        @block.gpsimd
        def _(p):
            for t in v_in:
                p.memset(t[:, :, :, :].bitcast(F32), 0.0).then_inc(padded, 1)
            for t in mid:
                p.memset(t[:, :, :, :, :].bitcast(F32), 0.0).then_inc(padded, 1)

        @block.vector
        def _(v):
            link = Chain(v, chain)

            def norm_rows(u, first, n):
                for j in range(4):
                    o = bass.ds(first + j, 1)
                    ins = v.tensor_scalar(v_raw[:, u, j, :], k.x[:, o, :], rstd[:, o], bias[:, o], ALU.mult, ALU.add)
                ins.then_inc(v_normed, 1)
                v.wait_ge(v_high, n)
                v.tensor_tensor(v_in[1][:, u, :, 3:3 + HW], v_raw[:, u, :, :],
                                v_in[0][:, u, :, 3:3 + HW].bitcast(F32), ALU.subtract).then_inc(v_ready, 1)

            def band_low(n):
                v.wait_ge(bands_high, n + 1)
                v.tensor_tensor(band[1][:, cut[n], :], bands[:, cut[n], :], band[0][:, cut[n], :].bitcast(F32), ALU.subtract)\
                 .then_inc(bands_ready, 1)

            def low(i, m):
                v.wait_ge(mid_high, 8 * i + (m + 1))
                v.tensor_tensor(mid[1][:, m // 4, m % 4, :, 3:3 + HW], m_raw[:, m % 4, :, :],
                                mid[0][:, m // 4, m % 4, :, 3:3 + HW].bitcast(F32), ALU.subtract).then_inc(mid_ready, 1)

            def round_(i, last):
                for m in range(8):
                    v.wait_ge(mid_copied, 8 * i + (m + 5))
                    y = m_raw[:, m % 4, :, :]
                    v.scalar_tensor_tensor(out=y, in0=y, scalar=0.2, in1=y, op0=ALU.mult, op1=ALU.max)\
                     .then_inc(mid_leaky, 1)
                    if m:
                        low(i, m - 1)
                low(i, 7)
                if not last:
                    for u in range(2):
                        norm_rows(u, 8 * i + (8 + 4 * u), 2 * i + (u + 3))
                for u in range(2):
                    v.wait_ge(z_done, 2 * i + (u + 2))
                    xg = k.x[:, bass.ds((2 * i + u) * 4, 4), :]
                    v.tensor_tensor(xg, ps_z[:, u, :].rearrange("p (i w) -> p i w", w=HW), xg, ALU.add).then_inc(z_added, 1)
                    v.wait_ge(z_added, 2 * i + (u + 3))
                    for j in range(4):
                        o = bass.ds(8 * i + (4 * u + j), 1)
                        v.bn_stats(k.st[:, o, :], k.x[:, o, :])

            v_row_norm(v, link, k.st, mean[:, :], var[:, :], rstd[:, :], root[:, :], tmp[:, :], 1e-6, var_ready, root_ready)
            v.wait_ge(loaded, 16)
            link(v.tensor_tensor(tmp[:, :], mean[:, :], rstd[:, :], ALU.mult))
            link(v.tensor_tensor(bias[:, :], bias[:, :], tmp[:, :], ALU.subtract))
            band_low(0)
            v.wait_ge(padded, 4)
            v.sem_inc(mid_ready, 4)
            v.sem_inc(z_added, 2)
            for u in range(2):
                norm_rows(u, 4 * u, u + 1)
            band_low(1)
            with v.Fori(0, ROUNDS - 1) as i:
                round_(i, False)
            round_(ROUNDS - 1, True)

        @block.scalar
        def _(s):
            def high_rows(u, n):
                s.wait_ge(v_normed, n)
                s.activation(v_in[0][:, u, :, 3:3 + HW], v_raw[:, u, :, :], ACT.Copy).then_inc(v_high, 1)

            def high(i, m):
                s.wait_ge(mid_leaky, 8 * i + (m + 1))
                s.activation(mid[0][:, m // 4, m % 4, :, 3:3 + HW], m_raw[:, m % 4, :, :], ACT.Copy).then_inc(mid_high, 1)

            def round_(i, last):
                s.wait_ge(z_done, 2 * i + 1)
                for m in range(8):
                    s.wait_ge(mid_done, 8 * i + (m + 1))
                    s.wait_ge(mid_ready, 8 * i + (m + 1))
                    s.activation(m_raw[:, m % 4, :, :], ps_m[:, m % 4, :].rearrange("p (i w) -> p i w", w=HW), ACT.Copy,
                                 scale=GAIN).then_inc(mid_copied, 1)
                    if m:
                        high(i, m - 1)
                high(i, 7)
                if not last:
                    for u in range(2):
                        high_rows(u, 2 * i + (u + 3))

            s.wait_ge(var_ready, 1)
            s.activation(root[:, :], var[:, :], ACT.Sqrt).then_inc(root_ready, 1)
            for n in range(2):
                s.wait_ge(bands_loaded[n], 16)
                s.activation(band[0][:, cut[n], :], bands[:, cut[n], :], ACT.Copy).then_inc(bands_high, 1)
            s.wait_ge(padded, 4)
            s.sem_inc(mid_copied, 4)
            for u in range(2):
                high_rows(u, u + 1)
            with s.Fori(0, ROUNDS - 1) as i:
                round_(i, False)
            round_(ROUNDS - 1, True)

        @block.tensor
        def _(pe):
            pe.wait_ge(bands_ready, 1)
            pe.sem_inc(z_done, 1)
            with pe.Fori(0, ROUNDS) as i:
                for u in range(2):
                    pe.wait_ge(v_ready, 2 * i + (u + 1))
                    for pq in range(4):
                        p, q = pq // 2, pq % 2
                        pe.wait_ge(mid_copied, 8 * i + (4 * u + pq + 1))
                        shifts = list(range(-3, 4)) if q == 0 else list(range(-2, 4))
                        for n, dc in enumerate(shifts):
                            mm = passes(pe.matmul, ps_m[:, pq, :], [t[:, 2 * (7 * q + n) + p, :] for t in bu],
                                        [t[:, u, :, 3 + dc:3 + dc + HW] for t in v_in], n == 0, n == len(shifts) - 1)
                        mm.then_inc(mid_done, 1)
                pe.wait_ge(bands_ready, 2)
                for u in range(2):
                    pe.wait_ge(mid_ready, 8 * i + (4 * u + 8))
                    pe.wait_ge(z_added, 2 * i + (u + 1))
                    for n in range(2 * TAPS):
                        j, p = n // 2, n % 2
                        q = 0 if j % 2 else 1
                        dc = (j - 5 - q) // 2
                        mm = passes(pe.matmul, ps_z[:, u, :], [t[:, n, :] for t in bd],
                                    [t[:, u, 2 * p + q, :, 3 + dc:3 + dc + HW] for t in mid], n == 0, n == 2 * TAPS - 1)
                    mm.then_inc(z_done, 1)


def stage_experts(k):
    nc, a = k.nc, k.a
    STEPS = NI // 8
    EG = 128 // EXP
    with ExitStack() as ctx:
        sb = lambda name, shape, dt=F32: k.sb(name, shape, dt, ctx=ctx)
        pair = lambda name, shape: [sb(f"{name}_{part}", shape, F32R) for part in ("high", "low")]
        mean, var, rstd, root, tmp = (sb(f"s12_{n}", [128, NI]) for n in ("mean", "var", "rstd", "root", "tmp"))
        tn = sb("s12_tn", [128, 2, 4, HW])
        tt_ = pair("s12_tt", [128, 4, 4, HW])
        tt_all = [sb(f"s12_tt_all_{part}", [128, NI, HW]) for part in ("high", "low")]
        w_raw = sb("s12_w_raw", [128, EXP * 128 + EXP])
        w = pair("s12_w", [128, EXP * 128 + EXP])
        rb, order = sb("s12_rb", [128, EXP]), sb("s12_order", [128, EXP])
        eb = sb("s12_eb", [128, EG * 128])
        lg, ex, eq, oh, g1 = (sb(f"s12_{n}", [128, NI, EXP]) for n in ("lg", "ex", "eq", "oh", "g1"))
        m0, m1, m2, r0 = (sb(f"s12_{n}", [128, NI]) for n in ("m0", "m1", "m2", "r0"))
        gt = sb("s12_gt", [128, NI // EG, 128])
        part_a, part_b = sb("s12_part_a", [128, 4, 4, HW]), sb("s12_part_b", [128, 4, 4, HW])
        half, quarter = sb("s12_half", [128, 4, 2, HW]), sb("s12_quarter", [128, 2, 4, HW])
        ps_t = k.ps("s12_pst", [128, 2, 4, 128], ctx)
        ps_l = k.ps("s12_psl", [128, NI, EXP], ctx)
        ps_e = k.ps("s12_pse", [128, 2, 2, 4, 128], ctx)
        loaded, chain = k.sem("s12_loaded"), k.sem("s12_chain")
        w_high, w_ready = k.sem("s12_w_high"), k.sem("s12_w_ready")
        var_ready, root_ready = k.sem("s12_var_ready"), k.sem("s12_root_ready")
        tn_ready, turned = k.sem("s12_tn_ready"), k.sem("s12_turned")
        tt_high, tt_ready, logits = k.sem("s12_tt_high"), k.sem("s12_tt_ready"), k.sem("s12_logits")
        kept = [k.sem(f"s12_kept{u}") for u in range(4)]
        exp_in, exp_done, gates, gt_done = k.sem("s12_exp_in"), k.sem("s12_exp_done"), k.sem("s12_gates"), k.sem("s12_gt_done")
        gt_copied, base, based = k.sem("s12_gt_copied"), k.sem("s12_base"), k.sem("s12_based")
        fetched = [k.sem(f"s12_fetched{u}") for u in range(2)]
        exp_ready, a_scaled, b_scaled = k.sem("s12_exp_ready"), k.sem("s12_a_scaled"), k.sem("s12_b_scaled")
        joined, halved, quartered = k.sem("s12_joined"), k.sem("s12_halved"), k.sem("s12_quartered")
        used, out_stored = k.sem("s12_used"), k.sem("s12_out_stored")
        block = ctx.enter_context(nc.Block())
        NE = EXP * 128

        @block.sync
        def _(sp):
            sp.dma_start(w_raw[:, 0:NE].rearrange("d (e c) -> d e c", c=128), a["expert_w"].rearrange("e d c -> d e c"))\
              .then_inc(loaded, 16)
            sp.dma_start(w_raw[:, NE:], a["router_w"]).then_inc(loaded, 16)
            sp.dma_start(rb[:, :], sub(a["router_b"], 0, [[0, 128], [1, EXP]])).then_inc(loaded, 16)
            sp.dma_start(order[:, :], sub(a["order"], 0, [[0, 128], [1, EXP]])).then_inc(loaded, 16)
            sp.dma_start(eb[:, :], a["expert_b"]).then_inc(loaded, 16)
            with sp.Fori(0, STEPS // 2) as i:
                for u in range(4):
                    sp.wait_ge(tt_ready, 4 * i + (u + 3))
                    for h in range(2):
                        sp.dma_start(tt_all[h][:, bass.ds((4 * i + u) * 4, 4), :], tt_[h][:, u, :, :].bitcast(F32)).then_inc(kept[u], 16)
            for u in range(4):
                sp.wait_ge(kept[u], 1 + 16 * STEPS)
            sp.wait_ge(logits, 4 + 2 * STEPS)

            def fetch(i, first):
                for u in range(2):
                    sp.wait_ge(exp_ready, first + 8 * u)
                    for h in range(2):
                        sp.dma_start(tt_[h][:, u, :, :].bitcast(F32), tt_all[h][:, bass.ds((2 * i + u) * 4, 4), :])\
                          .then_inc(fetched[u], 16)

            def store(i):
                sp.wait_ge(used, 2 * i + 4)
                sp.dma_start(a["out"][bass.ds(8 * i, 8)].rearrange("i h w -> h i w"), k.x[:, bass.ds(8 * i, 8), :])\
                  .then_inc(out_stored, 16)

            fetch(0, 1)
            with sp.Fori(0, STEPS - 1) as i:
                fetch(i + 1, 16 * i + 17)
                store(i)
            store(STEPS - 1)
            sp.wait_ge(out_stored, 16 * STEPS)

        @block.vector
        def _(v):
            link = Chain(v, chain)
            tt = lambda o, x, y, op: link(v.tensor_tensor(o, x, y, op))
            wide = lambda t: t.unsqueeze(2).broadcast_to([128, NI, EXP])
            each = lambda t: t.unsqueeze(1).broadcast_to([128, NI, EXP])
            v_row_norm(v, link, k.st, mean[:, :], var[:, :], rstd[:, :], root[:, :], tmp[:, :], 1e-5, var_ready, root_ready)
            v.wait_ge(w_high, 1)
            v.tensor_tensor(w[1][:, :], w_raw[:, :], w[0][:, :].bitcast(F32), ALU.subtract).then_inc(w_ready, 1)

            def norm_rows(u, first):
                for j in range(4):
                    o = bass.ds(first + j, 1)
                    ins = v.tensor_scalar(tn[:, u, j, :], k.x[:, o, :], mean[:, o], rstd[:, o], ALU.subtract, ALU.mult)
                ins.then_inc(tn_ready, 1)

            def turn_low(i, last):
                for u in range(4):
                    if not last or u < 2:
                        v.wait_ge(turned, 4 * i + (u + 1))
                        norm_rows(u % 2, 16 * i + (8 + 4 * u))
                    v.wait_ge(tt_high, 4 * i + (u + 1))
                    v.tensor_tensor(tt_[1][:, u, :, :], ps_t[:, u % 2, :, :], tt_[0][:, u, :, :].bitcast(F32), ALU.subtract)\
                     .then_inc(tt_ready, 1)

            v.sem_inc(tt_ready, 2)
            for u in range(2):
                norm_rows(u, 4 * u)
            with v.Fori(0, STEPS // 2 - 1) as i:
                turn_low(i, False)
            turn_low(STEPS // 2 - 1, True)

            v.wait_ge(logits, 4 + 2 * STEPS)
            tt(lg[:, :, :], ps_l[:, :, :], each(rb[:, :]), ALU.add)
            link(v.tensor_reduce(m0[:, :], lg[:, :, :], AX.X, ALU.max))
            v.tensor_tensor(lg[:, :, :], lg[:, :, :], wide(m0[:, :]), ALU.subtract).then_inc(exp_in, 1)
            v.wait_ge(exp_done, 1)
            link(v.tensor_reduce(m0[:, :], ex[:, :, :], AX.X, ALU.add))
            link(v.reciprocal(r0[:, :], m0[:, :]))
            tt(ex[:, :, :], ex[:, :, :], wide(r0[:, :]), ALU.mult)
            for n, m in enumerate((m1, m2)):
                link(v.tensor_reduce(m[:, :], ex[:, :, :], AX.X, ALU.max))
                tt(eq[:, :, :], ex[:, :, :], wide(m[:, :]), ALU.is_equal)
                tt(eq[:, :, :], eq[:, :, :], each(order[:, :]), ALU.mult)
                link(v.tensor_reduce(r0[:, :], eq[:, :, :], AX.X, ALU.max))
                tt(oh[:, :, :], eq[:, :, :], wide(r0[:, :]), ALU.is_equal)
                if n == 0:
                    tt(g1[:, :, :], oh[:, :, :], wide(m[:, :]), ALU.mult)
                    link(v.scalar_tensor_tensor(out=ex[:, :, :], in0=oh[:, :, :], scalar=-2.0, in1=ex[:, :, :],
                                                op0=ALU.mult, op1=ALU.add))
                else:
                    tt(oh[:, :, :], oh[:, :, :], wide(m[:, :]), ALU.mult)
            tt(m1[:, :], m1[:, :], m2[:, :], ALU.add)
            link(v.reciprocal(r0[:, :], m1[:, :]))
            tt(g1[:, :, :], g1[:, :, :], oh[:, :, :], ALU.add)
            v.tensor_tensor(g1[:, :, :], g1[:, :, :], wide(r0[:, :]), ALU.mult).then_inc(gates, 1)
            v.wait_ge(gates, 1)
            for n in range(NI // 4):
                v.wait_ge(base, n + 1)
                v.tensor_tensor(k.x[:, 4 * n:4 * n + 4, :], ps_t[:, n % 2, :, :], k.x[:, 4 * n:4 * n + 4, :], ALU.add)\
                 .then_inc(based, 1)
            v.sem_inc(a_scaled, 2)
            v.sem_inc(used, 2)

            def join(i, j):
                v.wait_ge(a_scaled, 8 * i + (j + 3))
                v.wait_ge(b_scaled, 8 * i + (j + 3))
                v.tensor_tensor(part_a[:, j % 4, :, :], part_a[:, j % 4, :, :], part_b[:, j % 4, :, :], ALU.add)\
                 .then_inc(joined, 1)

            def add_rows(u, step):
                v.wait_ge(quartered, 4 * step + 4)
                xg = k.x[:, bass.ds(4 * step, 4), :]
                v.tensor_tensor(xg, quarter[:, u, :, :], xg, ALU.add).then_inc(used, 1)

            def round_(i, first):
                for j in range(8):
                    v.wait_ge(exp_ready, 16 * i + (2 * j + 10))
                    v.wait_ge(halved, 8 * i + (j + 1))
                    v.tensor_tensor(part_a[:, j % 4, :, :], ps_e[:, j % 2, 0, :, :],
                                    g1[:, bass.ds(8 * i + j, 1), 0:4].rearrange("p i e -> p (i e)").unsqueeze(2)
                                    .broadcast_to([128, 4, HW]), ALU.mult).then_inc(a_scaled, 1)
                    if j:
                        join(i, j - 1)
                    if j == 2 and not first:
                        add_rows(1, i * 2 - 1)
                    if j == 6:
                        add_rows(0, i * 2)
                join(i, 7)

            round_(0, True)
            with v.Fori(0, STEPS - 1) as i:
                round_(i + 1, False)
            add_rows(1, NI // 4 - 1)

        @block.scalar
        def _(s):
            s.wait_ge(var_ready, 1)
            s.activation(root[:, :], var[:, :], ACT.Sqrt).then_inc(root_ready, 1)
            s.wait_ge(loaded, 80)
            s.activation(w[0][:, :], w_raw[:, :], ACT.Copy).then_inc(w_high, 1)
            for u in range(4):
                s.sem_inc(kept[u], 1)
            s.sem_inc(logits, 4)
            with s.Fori(0, STEPS // 2) as i:
                for u in range(4):
                    s.wait_ge(turned, 4 * i + (u + 1))
                    s.wait_ge(logits, 4 * i + (u + 1))
                    s.wait_ge(kept[u], 32 * i + 1)
                    s.activation(tt_[0][:, u, :, :], ps_t[:, u % 2, :, :], ACT.Copy).then_inc(tt_high, 1)
            s.wait_ge(exp_in, 1)
            s.activation(ex[:, :, :], lg[:, :, :], ACT.Exp).then_inc(exp_done, 1)
            s.wait_ge(gt_done, NI // EG)
            s.activation(gt[:, :, :], ps_l[:, :, :].rearrange("p (n i) e -> p n (i e)", i=EG), ACT.Copy).then_inc(gt_copied, 1)
            s.sem_inc(b_scaled, 2)
            with s.Fori(0, STEPS) as i:
                for j in range(8):
                    s.wait_ge(exp_ready, 16 * i + (2 * j + 11))
                    s.wait_ge(halved, 8 * i + (j + 1))
                    for e in range(4):
                        ins = s.activation(part_b[:, j % 4, e, :], ps_e[:, j % 2, 1, e, :], ACT.Copy,
                                           scale=g1[:, bass.ds(8 * i + j, 1), 4 + e:5 + e].rearrange("p i e -> p (i e)"))
                    ins.then_inc(b_scaled, 1)

        @block.gpsimd
        def _(p):
            p.sem_inc(halved, 4)
            with p.Fori(0, STEPS) as i:
                for j in range(8):
                    p.wait_ge(joined, 8 * i + (j + 1))
                    p.tensor_tensor(half[:, j % 4, :, :], part_a[:, j % 4, 0:2, :], part_a[:, j % 4, 2:4, :], ALU.add)\
                     .then_inc(halved, 1)
                    p.wait_ge(halved, 8 * i + (j + 5))
                    if j % 4 == 0:
                        p.wait_ge(used, 2 * i + (j // 4 + 1))
                    p.tensor_tensor(quarter[:, j // 4, j % 4, :], half[:, j % 4, 0, :], half[:, j % 4, 1, :], ALU.add)\
                     .then_inc(quartered, 1)

        @block.tensor
        def _(pe):
            def turn(u, n):
                pe.wait_ge(tn_ready, n + 1)
                pe.wait_ge(tt_ready, n + 1)
                for j in range(4):
                    mm = pe.transpose(ps_t[:, u, j, :], tn[:, u, j, :], k.ident[:, :])
                mm.then_inc(turned, 1)

            def route(i, last):
                for u in range(4):
                    pe.wait_ge(tt_ready, 4 * i + (u + 3))
                    if not last or u < 2:
                        turn(u % 2, 4 * i + (u + 2))
                    for j in range(4):
                        mm = passes(pe.matmul, ps_l[:, bass.ds(16 * i + (4 * u + j), 1), :], [t[:, u, j, :] for t in tt_],
                                    [t[:, NE:NE + EXP] for t in w])
                    mm.then_inc(logits, 1)

            turn(0, 0)
            turn(1, 1)
            pe.wait_ge(w_ready, 1)
            with pe.Fori(0, STEPS // 2 - 1) as i:
                route(i, False)
            route(STEPS // 2 - 1, True)
            pe.sem_inc(exp_ready, 9)
            pe.wait_ge(gates, 1)
            for n in range(NI // EG):
                pe.transpose(ps_l[:, 16 * n:16 * n + 16, :].rearrange("p i e -> p (i e)"),
                             g1[:, 16 * n:16 * n + 16, :].rearrange("p i e -> p (i e)"), k.ident[:, :]).then_inc(gt_done, 1)
            pe.wait_ge(gt_copied, 1)
            for n in range(NI // 4):
                if n >= 2:
                    pe.wait_ge(based, n - 1)
                pe.matmul(ps_t[:, n % 2, :, :], gt[:, n // 4, :], eb[:, 512 * (n % 4):512 * (n % 4) + 512],
                          start=True, stop=True).then_inc(base, 1)
            with pe.Fori(0, STEPS) as i:
                for u in range(2):
                    pe.wait_ge(fetched[u], 32 * i + 32)
                    for j in range(4):
                        n = 4 * u + j
                        for h, scaled in enumerate((a_scaled, b_scaled)):
                            pe.wait_ge(scaled, 8 * i + (n + 1))
                            passes(pe.matmul, ps_e[:, n % 2, h, :, :], [t[:, u, j, :] for t in tt_],
                                   [t[:, 512 * h:512 * h + 512] for t in w]).then_inc(exp_ready, 1)




def low_modes(w):
    w = np.concatenate([w[0, 0], w[1, 0]], 1)
    rev = np.zeros_like(w)
    rev[:, 1:LM // 2, 0] = w[:, :LM // 2:-1, 0]
    rev[:, LM // 2 + 1:, 0] = w[:, LM // 2 - 1:0:-1, 0]
    rev[:, 0, 0] = w[:, 0, 0]
    parts = [x[..., c].transpose(2, 1, 0).reshape(64, 256) for x in (w, rev) for c in range(2)]
    one = np.stack(parts, 1)
    return np.concatenate([one, one], 0)


def full_modes(w):
    full = np.zeros((HEADS, NM, NN, 2), w.dtype)
    full[:, :LM // 2, :LN] = w[0, 0]
    full[:, NM - LM // 2:, :LN] = w[1, 0]
    rev = np.zeros_like(full)
    idx = (-np.arange(NM)) % NM
    keep = np.arange(NM) != NM // 2
    rev[:, keep, 0] = full[:, idx[keep], 0]
    parts = [x[..., c].transpose(0, 2, 1).reshape(128, 512) for x in (full, rev) for c in range(2)]
    return np.stack(parts, 1)


def layout(inputs):
    r = {}
    g = {n: np.asarray(v) for n, v in inputs.items()}
    r["x"] = g["x"].reshape(NI, HW, HW)
    c = "L0_conv_"
    r["norm_g"], r["norm_b"] = g[c + "norm_g"], g[c + "norm_b"]
    for n in "KQ":
        r["w" + n] = low_modes(g[c + "w" + n])
    for n in "KQV":
        r[f"w{n}s"] = g[f"{c}w{n}s"].reshape(HEADS)
        r[f"b{n}s"] = g[f"{c}b{n}s"]
    r["wV"] = full_modes(g[c + "wV"])
    wp = np.concatenate([g[c + "wP"][0, :, 0], g[c + "wP"][1, :, 0]], 1)
    r["wP"] = np.stack([wp[..., j].transpose(0, 2, 1).reshape(128, 512) for j in range(2)], 1)
    r["wP00"] = wp[:, 0, 0, 0]
    r["wPs"] = g[c + "wPs"].reshape(HEADS)
    r["bPs"] = g[c + "bPs"]
    for n in ("M0", "M1"):
        w = np.concatenate([g[f"{c}w{n}"][0, 0, 0], g[f"{c}w{n}"][1, 0, 0]], 0).transpose(1, 0, 2)
        r["w" + n] = np.stack([np.concatenate([w[..., j]] * 2, 0) for j in range(2)], 1)
        r[f"w{n}s"] = g[f"{c}w{n}s"].reshape(1)
        r[f"b{n}s"] = g[f"{c}b{n}s"]
    f = "L0_ffn_"
    for n in ("sigma", "log_weights", "gumbel", "M_u", "M_phi_plus", "M_phi_minus"):
        r[n] = g[f + n]
    at = HB * np.arange(NQ + 1)[:, None] + (HB - 1) - np.arange(128)[None]
    inside = (at >= 0) & (at < PIX // 8)
    phi = np.zeros((NQ + 1, NF, 128), np.float32)
    for p in range(2):
        phi[:, p:2 * FT:2] = np.where(inside[..., None], g[f + "phi"][p::2][np.where(inside, at, 0)], 0).transpose(0, 2, 1)
    phi[:, 2 * FT] = phi[:, 2 * FT + 1] = at == 0
    phi[:, 2 * FT + 2] = at == 1
    r["phi"] = phi
    r["bias"] = np.tile(g["L1_conv_bias"].reshape(T), B)
    r["up_t"], r["dn"] = g["L1_conv_up_filter"][0, 0].T, g["L1_conv_dn_filter"][0, 0]
    for n in ("router_w", "router_b", "expert_w"):
        r[n] = g["L1_ffn_" + n]
    eg = 128 // EXP
    eb = np.zeros((eg, EXP, eg, 128), np.float32)
    eb[np.arange(eg), :, np.arange(eg)] = g["L1_ffn_expert_b"]
    r["expert_b"] = eb.reshape(128, eg * 128)
    r.update(tables())
    return {n: np.ascontiguousarray(v) for n, v in r.items()}


SCRATCH = {
    "u_d": (NI, HW, HW), "xt_d": (NQ, 128, 2, 256), "tc_d": (NQ, 2, NF, 128, 2), "yh_d": (NQ, 2, 64, 512), "y_d": (NI, HW, HW),
    "gu_d": (13, 512), "gd_d": (TAPS, 512),
    "xn_d": (NI, HW, HW), "xf_d": (NI, 2, NN, NM), "xl_d": (2 * LN, LM, NI),
    "d_d": (HEADS, 2, NN, NM), "z_d": (NI, 2, NN, NM), "sk_d": (NI, HW, HW),
}


def program(nc, a):
    with ExitStack() as ctx:
        k = Core(nc, ctx, a)
        with ExitStack() as conv:
            k.image_buffer(conv)
            with ExitStack() as attn:
                att = Attention(k, attn)
                stage_spectrum(k, att)
                stage_attention(k, att)
                stage_mix(k, att)
                stage_project(k, att)
            stage_mixer(k)
        k.recycle_sems()
        with ExitStack() as ffn:
            stu = Stu(k, ffn)
            stage_stu_setup(k, stu)
            stage_stu_filter(k, stu)
            stage_stu_output(k, stu)
        stage_resample_conv(k)
        stage_experts(k)


def kernel(**inputs):
    import concourse.bacc as bacc
    from concourse.bass_utils import run_bass_kernel_spmd

    nc = bacc.Bacc("TRN2", target_bir_lowering=False, num_devices=1)
    arrays, a = {}, {}
    for name, v in layout(inputs).items():
        arrays[f"in_{name}"] = v
        a[name] = nc.dram_tensor(f"in_{name}", v.shape, mybir.dt.from_np(v.dtype), kind="ExternalInput").ap()
    for name, shape in SCRATCH.items():
        a[name] = nc.dram_tensor(name, shape, F32, kind="Internal").ap()
    a["out"] = nc.dram_tensor("out_x", (NI, HW, HW), F32, kind="ExternalOutput").ap()
    program(nc, a)
    r = run_bass_kernel_spmd(nc, [arrays], core_ids=[0])
    return r.results[0]["out_x"].reshape(B, T, HW, HW)
```
